# Optimizing a Trainium2 kernel written in Bass

```python
import numpy as np
import jax
import jax.numpy as jnp

def _softmax(x, axis=-1):
    return jax.nn.softmax(x, axis=axis)

def _gelu(x):
    return jax.nn.gelu(x, approximate=True)

def _silu(x):
    return jax.nn.silu(x)

def _sigmoid(x):
    return jax.nn.sigmoid(x)

def _layernorm(x, axis=-1, eps=1e-05):
    m = jnp.mean(x, axis=axis, keepdims=True)
    v = jnp.var(x, axis=axis, keepdims=True)
    return (x - m) / jnp.sqrt(v + eps)

def _scatter_add(tgt, idx, src, axis=0):
    return tgt.at[idx].add(src)

def _segment_sum(src, seg, n):
    return jax.ops.segment_sum(src, seg, n)
kernel_name = 'mk_conv_attn_hybrid_d2_conv_nhwc256_r4_9e0107'

def setup_inputs(seed: int=0):
    np.random.seed(seed)
    _w = jnp.asarray

    def _rec_inputs():
        import jax
        import jax.numpy as jnp
        _gk = jax.random.key(seed)
        x = -0.0002023 + 1 * jax.random.normal(jax.random.fold_in(_gk, 1), (8, 56, 56, 64), jnp.float32)
        return x
    x = _rec_inputs()

    def _L0_conv_setup():
        import jax, jax.numpy as jnp
        import numpy as np
        P = 32
        C = 64
        D = 4
        EPS = 0.001

        def _bn(x, g, b, m, v):
            return g * (x - m) * jax.lax.rsqrt(v + EPS) + b

        def _path(x, w1, b1, g1, be1, m1, v1, w2, b2, g2, be2, m2, v2, w3, b3, g3, be3, m3, v3):
            h = jnp.einsum('nhwc,cd->nhwd', x, w1) + b1
            h = jax.nn.relu(_bn(h, g1, be1, m1, v1))
            h = jax.lax.conv_general_dilated(h, w2, window_strides=(1, 1), padding='SAME', dimension_numbers=('NHWC', 'HWIO', 'NHWC')) + b2
            h = jax.nn.relu(_bn(h, g2, be2, m2, v2))
            h = jnp.einsum('nhwd,dc->nhwc', h, w3) + b3
            h = jax.nn.relu(_bn(h, g3, be3, m3, v3))
            return h
        key = jax.random.key(seed)
        ks = jax.random.split(key, 24)

        def nrm(k, shape, s=0.05):
            return jax.random.normal(k, shape, dtype=jnp.float32) * s
        inp = {}
        inp['x'] = jax.random.normal(ks[0], (8, 56, 56, C), dtype=jnp.float32)
        inp['W1'] = nrm(ks[1], (P, C, D))
        inp['B1'] = nrm(ks[2], (P, D))
        inp['W2'] = nrm(ks[3], (P, 3, 3, D, D))
        inp['B2'] = nrm(ks[4], (P, D))
        inp['W3'] = nrm(ks[5], (P, D, C))
        inp['B3'] = nrm(ks[6], (P, C))
        inp['G1'] = 1.0 + nrm(ks[7], (P, D))
        inp['Be1'] = nrm(ks[8], (P, D))
        inp['M1'] = nrm(ks[9], (P, D))
        inp['V1'] = 1.0 + 0.1 * jax.random.uniform(ks[10], (P, D), dtype=jnp.float32)
        inp['G2'] = 1.0 + nrm(ks[11], (P, D))
        inp['Be2'] = nrm(ks[12], (P, D))
        inp['M2'] = nrm(ks[13], (P, D))
        inp['V2'] = 1.0 + 0.1 * jax.random.uniform(ks[14], (P, D), dtype=jnp.float32)
        inp['G3'] = 1.0 + nrm(ks[15], (P, C))
        inp['Be3'] = nrm(ks[16], (P, C))
        inp['M3'] = nrm(ks[17], (P, C))
        inp['V3'] = 1.0 + 0.1 * jax.random.uniform(ks[18], (P, C), dtype=jnp.float32)
        return inp
    _L0_conv_all = _L0_conv_setup()
    _L0_conv_in = {k: v for k, v in _L0_conv_all.items() if k in ('W1', 'B1', 'G1', 'Be1', 'M1', 'V1', 'W2', 'B2', 'G2', 'Be2', 'M2', 'V2', 'W3', 'B3', 'G3', 'Be3', 'M3', 'V3')}
    del _L0_conv_all

    def _L1_attn_setup():
        import jax, jax.numpy as jnp
        import numpy as np
        D_MODEL = 64
        D_STATE = 16
        D_CONV = 4
        D_INNER = 128
        DT_RANK = 16
        BN = 32
        M = 16
        PARAM_NAMES = ['in_proj_w', 'conv_w', 'conv_b', 'x_proj_w', 'dt_proj_w', 'dt_proj_b', 'A_log', 'D', 'out_proj_w']

        def _mamba(x, in_proj_w, conv_w, conv_b, x_proj_w, dt_proj_w, dt_proj_b, A_log, Dvec, out_proj_w):
            xz = x @ in_proj_w.T
            xs, z = jnp.split(xz, 2, axis=-1)
            xs_pad = jnp.pad(xs, ((0, 0), (D_CONV - 1, 0), (0, 0)))
            kern = jnp.transpose(conv_w, (2, 1, 0))
            xs = jax.lax.conv_general_dilated(xs_pad, kern, (1,), 'VALID', dimension_numbers=('NWC', 'WIO', 'NWC'), feature_group_count=D_INNER) + conv_b
            xs = jax.nn.silu(xs)
            dbc = xs @ x_proj_w.T
            dt = jax.nn.softplus(dbc[..., :DT_RANK] @ dt_proj_w.T + dt_proj_b)
            Bm = dbc[..., DT_RANK:DT_RANK + D_STATE]
            Cm = dbc[..., DT_RANK + D_STATE:]
            A = -jnp.exp(A_log)
            dA = jnp.exp(dt[..., None] * A)
            dBu = dt[..., None] * Bm[:, :, None, :] * xs[..., None]

            def combine(c1, c2):
                a1, b1 = c1
                a2, b2 = c2
                return (a1 * a2, a2 * b1 + b2)
            _, hs = jax.lax.associative_scan(combine, (dA, dBu), axis=1)
            y = jnp.einsum('blds,bls->bld', hs, Cm) + xs * Dvec
            y = y * jax.nn.silu(z)
            return y @ out_proj_w.T

        def _core(x, ln_gamma, ln_beta, fp, bp):
            mu = x.mean(-1, keepdims=True)
            var = x.var(-1, keepdims=True)
            xn = (x - mu) / jnp.sqrt(var + 1e-05) * ln_gamma + ln_beta
            y_fwd = _mamba(xn, *fp)
            y_bwd = jnp.flip(_mamba(jnp.flip(xn, 1), *bp), 1)
            return y_fwd + y_bwd + x

        def _mamba_params(key):
            ks = jax.random.split(key, 5)
            s = 0.02
            return {'in_proj_w': jax.random.normal(ks[0], (2 * D_INNER, D_MODEL)) * s, 'conv_w': jax.random.normal(ks[1], (D_INNER, 1, D_CONV)) * s, 'conv_b': jnp.zeros((D_INNER,)), 'x_proj_w': jax.random.normal(ks[2], (DT_RANK + 2 * D_STATE, D_INNER)) * s, 'dt_proj_w': jax.random.normal(ks[3], (D_INNER, DT_RANK)) * s, 'dt_proj_b': jnp.full((D_INNER,), -4.6), 'A_log': jnp.log(jnp.tile(jnp.arange(1, D_STATE + 1, dtype=jnp.float32), (D_INNER, 1))), 'D': jnp.ones((D_INNER,)), 'out_proj_w': jax.random.normal(ks[4], (D_MODEL, D_INNER)) * s}
        key = jax.random.key(seed)
        kx, kf, kb = jax.random.split(key, 3)
        inp = {'x': jax.random.normal(kx, (BN, M, D_MODEL), dtype=jnp.float32), 'ln_gamma': jnp.ones((D_MODEL,), jnp.float32), 'ln_beta': jnp.zeros((D_MODEL,), jnp.float32)}
        fp = _mamba_params(kf)
        bp = _mamba_params(kb)
        for n in PARAM_NAMES:
            inp['f_' + n] = fp[n]
            inp['b_' + n] = bp[n]
        return inp
    _L1_attn_all = _L1_attn_setup()
    _L1_attn_in = {k: v for k, v in _L1_attn_all.items() if k in ('ln_gamma', 'ln_beta', 'f_in_proj_w', 'f_conv_w', 'f_conv_b', 'f_x_proj_w', 'f_dt_proj_w', 'f_dt_proj_b', 'f_A_log', 'f_D', 'f_out_proj_w', 'b_in_proj_w', 'b_conv_w', 'b_conv_b', 'b_x_proj_w', 'b_dt_proj_w', 'b_dt_proj_b', 'b_A_log', 'b_D', 'b_out_proj_w')}
    del _L1_attn_all

    def _L1_ffn_setup():
        import jax, jax.numpy as jnp
        import numpy as np
        TOP_K = 2
        LN_EPS = 1e-05
        key = jax.random.key(seed)
        ks = jax.random.split(key, 8)
        B, S, D, E, H = (16, 256, 64, 8, 256)
        x = jax.random.normal(ks[0], (B, S, D), dtype=jnp.float32)
        Wr = jax.random.normal(ks[1], (D, E), dtype=jnp.float32) * 0.1
        br = jnp.zeros((E,), dtype=jnp.float32)
        ln_g = jnp.ones((E, D), dtype=jnp.float32)
        ln_b = jnp.zeros((E, D), dtype=jnp.float32)
        W1 = jax.random.normal(ks[2], (E, D, H), dtype=jnp.float32) * (1.0 / np.sqrt(D))
        b1 = jnp.zeros((E, H), dtype=jnp.float32)
        W2 = jax.random.normal(ks[3], (E, H, D), dtype=jnp.float32) * (1.0 / np.sqrt(H))
        b2 = jnp.zeros((E, D), dtype=jnp.float32)
        return {'x': x, 'Wr': Wr, 'br': br, 'ln_g': ln_g, 'ln_b': ln_b, 'W1': W1, 'b1': b1, 'W2': W2, 'b2': b2}
    _L1_ffn_all = _L1_ffn_setup()
    _L1_ffn_in = {k: v for k, v in _L1_ffn_all.items() if k in ('Wr', 'br', 'ln_g', 'ln_b', 'W1', 'b1', 'W2', 'b2')}
    del _L1_ffn_all
    return {'x': x, 'L0_conv_W1': _L0_conv_in['W1'], 'L0_conv_B1': _L0_conv_in['B1'], 'L0_conv_G1': _L0_conv_in['G1'], 'L0_conv_Be1': _L0_conv_in['Be1'], 'L0_conv_M1': _L0_conv_in['M1'], 'L0_conv_V1': _L0_conv_in['V1'], 'L0_conv_W2': _L0_conv_in['W2'], 'L0_conv_B2': _L0_conv_in['B2'], 'L0_conv_G2': _L0_conv_in['G2'], 'L0_conv_Be2': _L0_conv_in['Be2'], 'L0_conv_M2': _L0_conv_in['M2'], 'L0_conv_V2': _L0_conv_in['V2'], 'L0_conv_W3': _L0_conv_in['W3'], 'L0_conv_B3': _L0_conv_in['B3'], 'L0_conv_G3': _L0_conv_in['G3'], 'L0_conv_Be3': _L0_conv_in['Be3'], 'L0_conv_M3': _L0_conv_in['M3'], 'L0_conv_V3': _L0_conv_in['V3'], 'L1_attn_ln_gamma': _L1_attn_in['ln_gamma'], 'L1_attn_ln_beta': _L1_attn_in['ln_beta'], 'L1_attn_f_in_proj_w': _L1_attn_in['f_in_proj_w'], 'L1_attn_f_conv_w': _L1_attn_in['f_conv_w'], 'L1_attn_f_conv_b': _L1_attn_in['f_conv_b'], 'L1_attn_f_x_proj_w': _L1_attn_in['f_x_proj_w'], 'L1_attn_f_dt_proj_w': _L1_attn_in['f_dt_proj_w'], 'L1_attn_f_dt_proj_b': _L1_attn_in['f_dt_proj_b'], 'L1_attn_f_A_log': _L1_attn_in['f_A_log'], 'L1_attn_f_D': _L1_attn_in['f_D'], 'L1_attn_f_out_proj_w': _L1_attn_in['f_out_proj_w'], 'L1_attn_b_in_proj_w': _L1_attn_in['b_in_proj_w'], 'L1_attn_b_conv_w': _L1_attn_in['b_conv_w'], 'L1_attn_b_conv_b': _L1_attn_in['b_conv_b'], 'L1_attn_b_x_proj_w': _L1_attn_in['b_x_proj_w'], 'L1_attn_b_dt_proj_w': _L1_attn_in['b_dt_proj_w'], 'L1_attn_b_dt_proj_b': _L1_attn_in['b_dt_proj_b'], 'L1_attn_b_A_log': _L1_attn_in['b_A_log'], 'L1_attn_b_D': _L1_attn_in['b_D'], 'L1_attn_b_out_proj_w': _L1_attn_in['b_out_proj_w'], 'L1_ffn_Wr': _L1_ffn_in['Wr'], 'L1_ffn_br': _L1_ffn_in['br'], 'L1_ffn_ln_g': _L1_ffn_in['ln_g'], 'L1_ffn_ln_b': _L1_ffn_in['ln_b'], 'L1_ffn_W1': _L1_ffn_in['W1'], 'L1_ffn_b1': _L1_ffn_in['b1'], 'L1_ffn_W2': _L1_ffn_in['W2'], 'L1_ffn_b2': _L1_ffn_in['b2']}

def reference(x, L0_conv_W1, L0_conv_B1, L0_conv_G1, L0_conv_Be1, L0_conv_M1, L0_conv_V1, L0_conv_W2, L0_conv_B2, L0_conv_G2, L0_conv_Be2, L0_conv_M2, L0_conv_V2, L0_conv_W3, L0_conv_B3, L0_conv_G3, L0_conv_Be3, L0_conv_M3, L0_conv_V3, L1_attn_ln_gamma, L1_attn_ln_beta, L1_attn_f_in_proj_w, L1_attn_f_conv_w, L1_attn_f_conv_b, L1_attn_f_x_proj_w, L1_attn_f_dt_proj_w, L1_attn_f_dt_proj_b, L1_attn_f_A_log, L1_attn_f_D, L1_attn_f_out_proj_w, L1_attn_b_in_proj_w, L1_attn_b_conv_w, L1_attn_b_conv_b, L1_attn_b_x_proj_w, L1_attn_b_dt_proj_w, L1_attn_b_dt_proj_b, L1_attn_b_A_log, L1_attn_b_D, L1_attn_b_out_proj_w, L1_ffn_Wr, L1_ffn_br, L1_ffn_ln_g, L1_ffn_ln_b, L1_ffn_W1, L1_ffn_b1, L1_ffn_W2, L1_ffn_b2):
    import jax
    import jax.numpy as jnp

    def _L0_conv_ref(x, W1, B1, G1, Be1, M1, V1, W2, B2, G2, Be2, M2, V2, W3, B3, G3, Be3, M3, V3):
        import jax, jax.numpy as jnp
        import numpy as np
        P = 32
        C = 64
        D = 4
        EPS = 0.001

        def _bn(x, g, b, m, v):
            return g * (x - m) * jax.lax.rsqrt(v + EPS) + b

        def _path(x, w1, b1, g1, be1, m1, v1, w2, b2, g2, be2, m2, v2, w3, b3, g3, be3, m3, v3):
            h = jnp.einsum('nhwc,cd->nhwd', x, w1) + b1
            h = jax.nn.relu(_bn(h, g1, be1, m1, v1))
            h = jax.lax.conv_general_dilated(h, w2, window_strides=(1, 1), padding='SAME', dimension_numbers=('NHWC', 'HWIO', 'NHWC')) + b2
            h = jax.nn.relu(_bn(h, g2, be2, m2, v2))
            h = jnp.einsum('nhwd,dc->nhwc', h, w3) + b3
            h = jax.nn.relu(_bn(h, g3, be3, m3, v3))
            return h
        paths = jax.vmap(_path, in_axes=(None,) + (0,) * 18)(x, W1, B1, G1, Be1, M1, V1, W2, B2, G2, Be2, M2, V2, W3, B3, G3, Be3, M3, V3)
        return jax.nn.relu(paths.sum(axis=0) + x)

    def _L1_attn_ref(x, ln_gamma, ln_beta, f_in_proj_w, f_conv_w, f_conv_b, f_x_proj_w, f_dt_proj_w, f_dt_proj_b, f_A_log, f_D, f_out_proj_w, b_in_proj_w, b_conv_w, b_conv_b, b_x_proj_w, b_dt_proj_w, b_dt_proj_b, b_A_log, b_D, b_out_proj_w):
        import jax, jax.numpy as jnp
        import numpy as np
        D_MODEL = 64
        D_STATE = 16
        D_CONV = 4
        D_INNER = 128
        DT_RANK = 16
        BN = 32
        M = 16
        PARAM_NAMES = ['in_proj_w', 'conv_w', 'conv_b', 'x_proj_w', 'dt_proj_w', 'dt_proj_b', 'A_log', 'D', 'out_proj_w']

        def _mamba(x, in_proj_w, conv_w, conv_b, x_proj_w, dt_proj_w, dt_proj_b, A_log, Dvec, out_proj_w):
            xz = x @ in_proj_w.T
            xs, z = jnp.split(xz, 2, axis=-1)
            xs_pad = jnp.pad(xs, ((0, 0), (D_CONV - 1, 0), (0, 0)))
            kern = jnp.transpose(conv_w, (2, 1, 0))
            xs = jax.lax.conv_general_dilated(xs_pad, kern, (1,), 'VALID', dimension_numbers=('NWC', 'WIO', 'NWC'), feature_group_count=D_INNER) + conv_b
            xs = jax.nn.silu(xs)
            dbc = xs @ x_proj_w.T
            dt = jax.nn.softplus(dbc[..., :DT_RANK] @ dt_proj_w.T + dt_proj_b)
            Bm = dbc[..., DT_RANK:DT_RANK + D_STATE]
            Cm = dbc[..., DT_RANK + D_STATE:]
            A = -jnp.exp(A_log)
            dA = jnp.exp(dt[..., None] * A)
            dBu = dt[..., None] * Bm[:, :, None, :] * xs[..., None]

            def combine(c1, c2):
                a1, b1 = c1
                a2, b2 = c2
                return (a1 * a2, a2 * b1 + b2)
            _, hs = jax.lax.associative_scan(combine, (dA, dBu), axis=1)
            y = jnp.einsum('blds,bls->bld', hs, Cm) + xs * Dvec
            y = y * jax.nn.silu(z)
            return y @ out_proj_w.T

        def _core(x, ln_gamma, ln_beta, fp, bp):
            mu = x.mean(-1, keepdims=True)
            var = x.var(-1, keepdims=True)
            xn = (x - mu) / jnp.sqrt(var + 1e-05) * ln_gamma + ln_beta
            y_fwd = _mamba(xn, *fp)
            y_bwd = jnp.flip(_mamba(jnp.flip(xn, 1), *bp), 1)
            return y_fwd + y_bwd + x

        def _mamba_params(key):
            ks = jax.random.split(key, 5)
            s = 0.02
            return {'in_proj_w': jax.random.normal(ks[0], (2 * D_INNER, D_MODEL)) * s, 'conv_w': jax.random.normal(ks[1], (D_INNER, 1, D_CONV)) * s, 'conv_b': jnp.zeros((D_INNER,)), 'x_proj_w': jax.random.normal(ks[2], (DT_RANK + 2 * D_STATE, D_INNER)) * s, 'dt_proj_w': jax.random.normal(ks[3], (D_INNER, DT_RANK)) * s, 'dt_proj_b': jnp.full((D_INNER,), -4.6), 'A_log': jnp.log(jnp.tile(jnp.arange(1, D_STATE + 1, dtype=jnp.float32), (D_INNER, 1))), 'D': jnp.ones((D_INNER,)), 'out_proj_w': jax.random.normal(ks[4], (D_MODEL, D_INNER)) * s}
        fp = (f_in_proj_w, f_conv_w, f_conv_b, f_x_proj_w, f_dt_proj_w, f_dt_proj_b, f_A_log, f_D, f_out_proj_w)
        bp = (b_in_proj_w, b_conv_w, b_conv_b, b_x_proj_w, b_dt_proj_w, b_dt_proj_b, b_A_log, b_D, b_out_proj_w)
        return _core(x, ln_gamma, ln_beta, fp, bp)

    def _L1_ffn_ref(x, Wr, br, ln_g, ln_b, W1, b1, W2, b2):
        import jax, jax.numpy as jnp
        import numpy as np
        TOP_K = 2
        LN_EPS = 1e-05
        B, S, D = x.shape
        N = B * S
        xt = x.reshape(N, D)
        logits = xt @ Wr + br
        probs = jax.nn.softmax(logits, axis=-1)
        top_p, top_idx = jax.lax.top_k(probs, TOP_K)
        weights = top_p / top_p.sum(axis=-1, keepdims=True)
        mu = xt.mean(axis=-1, keepdims=True)
        var = ((xt - mu) ** 2).mean(axis=-1, keepdims=True)
        xn = (xt - mu) * jax.lax.rsqrt(var + LN_EPS)
        xe = xn[None, :, :] * ln_g[:, None, :] + ln_b[:, None, :]
        h = jax.nn.gelu(jnp.einsum('end,edh->enh', xe, W1) + b1[:, None, :], approximate=False)
        y = jnp.einsum('enh,ehd->end', h, W2) + b2[:, None, :]
        y_tok = jnp.transpose(y, (1, 0, 2))
        sel = jnp.take_along_axis(y_tok, top_idx[:, :, None], axis=1)
        out = (weights[:, :, None] * sel).sum(axis=1)
        return out.reshape(B, S, D)

    def _gn(v, G=32, eps=1e-05):
        B_, H_, W_, C_ = v.shape
        g = v.reshape(B_, H_, W_, G, C_ // G)
        m = jnp.mean(g, axis=(1, 2, 4), keepdims=True)
        s = jnp.var(g, axis=(1, 2, 4), keepdims=True)
        return ((g - m) / jnp.sqrt(s + eps)).reshape(v.shape)

    def _ln_c(v, eps=1e-06):
        m = jnp.mean(v, axis=-1, keepdims=True)
        s = jnp.var(v, axis=-1, keepdims=True)
        return (v - m) / jnp.sqrt(s + eps)

    def _ln_t(v, eps=1e-05):
        m = jnp.mean(v, axis=-1, keepdims=True)
        s = jnp.var(v, axis=-1, keepdims=True)
        return (v - m) / jnp.sqrt(s + eps)

    def _to_tokens(v):
        B_, H_, W_, C_ = v.shape
        return v.reshape(B_, H_ * W_, C_)

    def _from_tokens(t, like):
        return t.reshape(like.shape)
    x = _L0_conv_ref(x, L0_conv_W1, L0_conv_B1, L0_conv_G1, L0_conv_Be1, L0_conv_M1, L0_conv_V1, L0_conv_W2, L0_conv_B2, L0_conv_G2, L0_conv_Be2, L0_conv_M2, L0_conv_V2, L0_conv_W3, L0_conv_B3, L0_conv_G3, L0_conv_Be3, L0_conv_M3, L0_conv_V3)
    t = _to_tokens(x)
    t = t + _L1_attn_ref(_ln_t(t), L1_attn_ln_gamma, L1_attn_ln_beta, L1_attn_f_in_proj_w, L1_attn_f_conv_w, L1_attn_f_conv_b, L1_attn_f_x_proj_w, L1_attn_f_dt_proj_w, L1_attn_f_dt_proj_b, L1_attn_f_A_log, L1_attn_f_D, L1_attn_f_out_proj_w, L1_attn_b_in_proj_w, L1_attn_b_conv_w, L1_attn_b_conv_b, L1_attn_b_x_proj_w, L1_attn_b_dt_proj_w, L1_attn_b_dt_proj_b, L1_attn_b_A_log, L1_attn_b_D, L1_attn_b_out_proj_w)
    t = t + _L1_ffn_ref(_ln_t(t), L1_ffn_Wr, L1_ffn_br, L1_ffn_ln_g, L1_ffn_ln_b, L1_ffn_W1, L1_ffn_b1, L1_ffn_W2, L1_ffn_b2)
    x = _from_tokens(t, x)
    return x

_drawn_inputs = setup_inputs


def setup_inputs(seed=0):
    import zlib

    import numpy as np

    out = dict(_drawn_inputs(seed))
    spreads = {'L1_attn_ln_gamma': (1.0, 0.6),
     'L1_attn_ln_beta': (0.0, 0.8),
     'L1_attn_f_conv_b': (0.0, 0.8),
     'L1_attn_f_dt_proj_b': (-4.599999904632568, 0.6),
     'L1_attn_f_D': (1.0, 0.6),
     'L1_attn_b_conv_b': (0.0, 0.8),
     'L1_attn_b_dt_proj_b': (-4.599999904632568, 0.6),
     'L1_attn_b_D': (1.0, 0.6),
     'L1_ffn_br': (0.0, 0.1),
     'L1_ffn_ln_g': (1.0, 0.6),
     'L1_ffn_ln_b': (0.0, 0.366),
     'L1_ffn_b1': (0.0, 0.351),
     'L1_ffn_b2': (0.0, 0.431)}
    factors = {'L0_conv_B1': 6.526,
     'L0_conv_G1': 188.047,
     'L0_conv_Be1': 19.185,
     'L0_conv_M1': 6.091,
     'L0_conv_V1': 200.0,
     'L0_conv_B2': 7.42,
     'L0_conv_G2': 40.704,
     'L0_conv_Be2': 2.879,
     'L0_conv_M2': 2.862,
     'L0_conv_V2': 200.0,
     'L0_conv_G3': 9.276,
     'L0_conv_V3': 200.0,
     'L1_attn_f_in_proj_w': 8.0,
     'L1_attn_f_conv_w': 8.0,
     'L1_attn_f_x_proj_w': 8.0,
     'L1_attn_f_dt_proj_w': 8.0,
     'L1_attn_f_A_log': 8.0,
     'L1_attn_f_out_proj_w': 8.0,
     'L1_attn_b_in_proj_w': 8.0,
     'L1_attn_b_conv_w': 8.0,
     'L1_attn_b_x_proj_w': 8.0,
     'L1_attn_b_dt_proj_w': 8.0,
     'L1_attn_b_A_log': 8.0,
     'L1_attn_b_out_proj_w': 8.0}
    for name, (base, spread) in spreads.items():
        noise = np.random.default_rng([zlib.crc32(name.encode()), seed]).standard_normal(out[name].shape)
        drawn = base * np.exp(spread * noise) if base else spread * noise
        out[name] = jnp.asarray(drawn.astype(out[name].dtype))
    for name, factor in factors.items():
        out[name] = (out[name] * factor).astype(out[name].dtype)
    return out
```

```python
import concourse.bass as bass
from concourse import mybir
from contextlib import ExitStack

F32 = mybir.dt.float32
BF16 = mybir.dt.bfloat16
ALU = mybir.AluOpType
ACT = mybir.ActivationFunctionType
AX = mybir.AxisListType

NB, HH, WW, C = 8, 56, 56, 64
TOK = HH * WW
ROWS = 8
CH = ROWS * WW
NCH = TOK // CH
TT = 112
KT = CH // TT
NT = TOK // TT
PATHS, PD = 32, 4
PW = WW + 2
ZP = PATHS * C // 128
DI, DS, DR, TAPS = 128, 16, 16, 4
EX, HID = 8, 256
MT = EX * HID // 128
LN_EPS, BN_EPS = 1e-5, 1e-3
DT_CLAMP = 40.0
FAR = 1.0e30
STEPS = 2 * NCH


def build(nc, T):
    ctx = ExitStack()
    with ctx:
        def sb(name, shape, dt=F32):
            return ctx.enter_context(nc.sbuf_tensor(name, shape, dt))

        sems = []

        def sem(name):
            s = ctx.enter_context(nc.semaphore(name))
            sems.append(s)
            return s

        ident = sb("ident", [128, 128])
        identb = sb("identb", [128, 128], BF16)
        path_mask = sb("path_mask", [128, PATHS])
        pair_mask = sb("pair_mask", [128, 8])
        rank8 = sb("rank8", [TT, EX])
        pick_small = sb("pick_small", [96, 2 * DS])
        pick = sb("pick", [96, 2 * DS, 128], BF16)
        half_pow = sb("half_pow", [128, 82])
        w1 = sb("w1", [C, 128])
        w2c = sb("w2c", [128, 9, PD])
        w2 = sb("w2", [128, 9, 128])
        w3c = sb("w3c", [128, C])
        w3 = sb("w3", [128, 8, C])
        bnv = sb("bnv", [128, 82])
        bng = sb("bng", [128, 82])
        bnm = sb("bnm", [128, 18])
        bnb = sb("bnb", [128, 18])
        bnbe = sb("bnbe", [128, 18])
        nb3 = sb("nb3", [128, ZP])
        sum_b3 = sb("sum_b3", [128, 1])
        gb = sb("gb", [C, 2])
        wx = [sb(f"wx{d}", [128, 2, DI]) for d in range(2)]
        tapw = [sb(f"tapw{d}", [128, 2, DI]) for d in range(2)]
        wz = [sb(f"wz{d}", [C, DI]) for d in range(2)]
        wdt_a = [sb(f"wdt_a{d}", [DR, DI]) for d in range(2)]
        wdt_b = [sb(f"wdt_b{d}", [DR, DI]) for d in range(2)]
        wdt = [sb(f"wdt{d}", [DI, DI]) for d in range(2)]
        wbc = [sb(f"wbc{d}", [DI, 2 * DS]) for d in range(2)]
        wo = [sb(f"wo{d}", [DI, C]) for d in range(2)]
        dvec = [sb(f"dvec{d}", [DI, 3 + DS]) for d in range(2)]
        we1 = sb("we1", [C, MT, 128])
        we2 = sb("we2", [128, MT, C])
        be1 = sb("be1", [128, MT])
        be2 = sb("be2", [EX, C])
        lng = sb("lng", [C, EX])
        lnb = sb("lnb", [C, EX])
        wr = sb("wr", [C, EX])
        br = sb("br", [TT, EX])

        x_tok = sb("x_tok", [TT, NT, C])
        res = sb("res", [TT, NT, C])
        xn = sb("xn", [128, TOK + 6])
        u = [sb(f"u{d}", [DI, TOK]) for d in range(2)]
        zs = [sb(f"zs{d}", [DI, TOK]) for d in range(2)]

        xT = sb("xT", [C, 2, CH])
        h1 = sb("h1", [128, (HH + 2) * PW])
        h1v = h1[:, :].rearrange("p (r w) -> p r w", w=PW)
        h2 = sb("h2", [128, 2, CH])
        rz = sb("rz", [128, 4, CH])
        acc = sb("acc", [128, 2, CH])
        tmp = sb("tmp", [TT, 3, KT, C])
        xnt = sb("xnt", [TT, 2, KT, C])
        stat = sb("stat", [TT, 2, 8, KT])
        sq2 = sb("sq2", [TT, NT])
        dtv = sb("dtv", [DI, 2, CH])
        dtu = sb("dtu", [DI, 2, CH])
        sp = sb("sp", [DI, 4, CH])
        bct = sb("bct", [TT, KT, 3, 2 * DS], BF16)
        bcr = sb("bcr", [TT, KT, 2 * DS])
        bc3 = sb("bc3", [96, 2, CH], BF16)
        dA = sb("dA", [DI, 3, CH])
        dBu = sb("dBu", [DI, 2, CH])
        hs = sb("hs", [DI, 3, CH])
        cb = sb("cb", [DI, 3, CH])
        hc = sb("hc", [DI, 3, CH])
        state = sb("state", [DI, 2, DS])
        ytok = sb("ytok", [TT, KT * 128])
        hg = rz
        lg = sp[0:TT, :, :].rearrange("p a b -> p (a b)").rearrange("p (i n e) -> p i n e", n=NT, e=EX)
        l1 = sb("l1", [TT, 8, NT])
        wgt = sb("wgt", [TT, NT, EX])
        wT = sb("wT", [EX, 2, CH])
        yw = dA[0:TT, :, :].rearrange("p a b -> p (a b)")[:, 0:2 * EX * C].rearrange("p (i e c) -> p i e c", e=EX, c=C)
        red = sb("red", [TT, 2, C])
        outb = dBu[0:TT, :, :].rearrange("p a b -> p (a b)")[:, 0:2 * KT * C].rearrange("p (i k c) -> p i k c", k=KT, c=C)

        ps = [ctx.enter_context(nc.psum_tensor(f"ps{i}", [128, 512], F32)) for i in range(8)]

        x_dram = T["x"].rearrange("b h w c -> b (h w) c").rearrange("b (n p) c -> b p n c", p=TT)
        o_dram = T["out"].rearrange("b h w c -> b (h w) c").rearrange("b (n p) c -> b p n c", p=TT)

        s_load = sem("s_load")
        s_prep = sem("s_prep")
        s_pool = sem("s_pool")
        s_pe = sem("s_pe")
        s_act = sem("s_act")

        LOADS = [(ident, "ident"), (path_mask, "path_mask"), (pair_mask, "pair_mask"), (rank8, "rank8"),
                 (pick_small, "pick"), (w1, "w1"), (w2c, "w2"), (w3c, "w3"), (bnv, "bnv"), (bng, "bng"),
                 (bnm, "bnm"), (bnb, "bnb"), (bnbe, "bnbe"), (gb, "gb"), (we1, "we1"), (we2, "we2"),
                 (be1, "be1"), (be2, "be2"), (lng, "lng"), (lnb, "lnb"), (wr, "wr"), (br, "br")]
        for d in range(2):
            LOADS += [(wx[d], f"wx{d}"), (tapw[d], f"tapw{d}"), (wz[d], f"wz{d}"), (wdt_a[d], f"wdt_a{d}"),
                      (wdt_b[d], f"wdt_b{d}"), (wbc[d], f"wbc{d}"), (wo[d], f"wo{d}"), (dvec[d], f"dvec{d}")]

        with nc.Block() as block:
            @block.sync
            def _(sp_):
                for tile, name in LOADS:
                    src, dst = T[name], tile
                    idx = tuple(slice(None) for _ in tile.shape)
                    sp_.dma_start(dst[idx], src).then_inc(s_load, 16)

            @block.gpsimd
            def _(pool):
                pool.memset(half_pow[:, :], -0.5).then_inc(s_pool, 1)
                pool.memset(h1[:, :], 0.0).then_inc(s_pool, 1)
                pool.memset(xn[:, :], 0.0).then_inc(s_pool, 1)
                pool.wait_ge(s_pool, 1)
                pool.wait_ge(s_prep, 1)
                nc.gpsimd.tensor_tensor(bnv[:, :], bnv[:, :], half_pow[:, :], ALU.pow).then_inc(s_pool, 1)

            @block.scalar
            def _(act):
                act.wait_ge(s_load, 16 * len(LOADS))
                for d in range(2):
                    nc.scalar.activation(dvec[d][:, 3:3 + DS], dvec[d][:, 3:3 + DS], ACT.Exp).then_inc(s_act, 1)

            @block.vector
            def _(dve):
                step = [0]

                def then(ins):
                    step[0] += 1
                    ins.then_inc(s_prep, 1)
                    dve.wait_ge(s_prep, step[0])

                V = nc.vector
                dve.wait_ge(s_load, 16 * len(LOADS))
                then(V.tensor_scalar(bnv[:, :], bnv[:, :], BN_EPS, None, ALU.add))
                then(V.tensor_copy(identb[:, :], ident[:, :]))
                then(V.tensor_copy(pick[:, :, :], pick_small[:, :].unsqueeze(2).to_broadcast([96, 2 * DS, 128])))
                for t in range(9):
                    then(V.tensor_tensor(w2[:, t, :].rearrange("p (a b) -> p a b", b=PD),
                                         w2c[:, t, :].unsqueeze(1).to_broadcast([128, PATHS, PD]),
                                         path_mask[:, :].unsqueeze(2).to_broadcast([128, PATHS, PD]), ALU.mult))
                dve.wait_ge(s_pool, 4)
                then(V.tensor_tensor(bng[:, :], bng[:, :], bnv[:, :], ALU.mult))
                then(V.tensor_tensor(w3c[:, :], w3c[:, :], bng[:, 18:82], ALU.mult))
                then(V.tensor_tensor(w3[:, :, :], w3c[:, :].unsqueeze(1).to_broadcast([128, 8, C]),
                                     pair_mask[:, :].unsqueeze(2).to_broadcast([128, 8, C]), ALU.mult))
                then(V.tensor_tensor(bnb[:, :], bnb[:, :], bnm[:, :], ALU.subtract))
                then(V.tensor_tensor(bnb[:, :], bnb[:, :], bng[:, 0:18], ALU.mult))
                then(V.tensor_tensor(bnb[:, :], bnb[:, :], bnbe[:, :], ALU.add))
                then(V.tensor_scalar(nb3[:, :], bnb[:, 2:18], -1.0, None, ALU.mult))
                then(V.reduce_sum(sum_b3[:, :], bnb[:, 2:18].rearrange("p (a b) -> p b a", b=2)[:, 0, :], axis=AX.X))
                for d in range(2):
                    then(V.tensor_tensor(wx[d][:, :, :], wx[d][:, :, :], tapw[d][:, :, :], ALU.mult))
                dve.wait_ge(s_act, 2)
                for d in range(2):
                    then(V.tensor_scalar(dvec[d][:, 3:3 + DS], dvec[d][:, 3:3 + DS], -1.0, None, ALU.mult))
                dve.wait_ge(s_pe, 1)
                for d in range(2):
                    then(V.tensor_copy(wdt[d][:, :], ps[d][:, 0:DI]))
                then(V.tensor_tensor(be1[:, :], be1[:, :], ps[2][:, 0:MT], ALU.add))
                for e in range(EX):
                    then(V.tensor_scalar(we1[:, 2 * e:2 * e + 2, :], we1[:, 2 * e:2 * e + 2, :],
                                         lng[:, e:e + 1], None, ALU.mult))

            @block.tensor
            def _(pe):
                pe.wait_ge(s_load, 16 * len(LOADS))
                for d in range(2):
                    nc.tensor.matmul(ps[d][:, 0:DI], wdt_a[d][:, :], wdt_b[d][:, :], start=True, stop=True)
                for m in range(MT):
                    last = nc.tensor.matmul(ps[2][:, m:m + 1], we1[:, m, :], lnb[:, m // 2:m // 2 + 1],
                                            start=True, stop=True)
                last.then_inc(s_pe, 1)

        nc.gpsimd.sem_clear(s_load)
        nc.gpsimd.sem_clear(s_prep)
        nc.gpsimd.sem_clear(s_pool)
        nc.gpsimd.sem_clear(s_pe)
        nc.gpsimd.sem_clear(s_act)
        nc.all_engine_barrier()

        x_in = sem("x_in")
        xT_ps, xT_sb = sem("xT_ps"), sem("xT_sb")
        h1_ps, h1_sb = sem("h1_ps"), sem("h1_sb")
        h2_ps, h2_sb = sem("h2_ps"), sem("h2_sb")
        z_ps, z_dve, z_act, z_T = sem("z_ps"), sem("z_dve"), sem("z_act"), sem("z_T")
        x1_ps, x1_out = sem("x1_ps"), sem("x1_out")
        a_ch, pw_req, pw_done = sem("a_ch"), sem("pw_req"), sem("pw_done")
        xn_tok, xn_ps, xn_sb = sem("xn_tok"), sem("xn_ps"), sem("xn_sb")
        b_ps, b_sb = sem("b_ps"), sem("b_sb")
        dt_ps, bc_ps, bc_tok, bcT_ps, bcT_sb = (sem(n) for n in ("dt_ps", "bc_ps", "bc_tok", "bcT_ps", "bcT_sb"))
        c_ch, dt_x, dt_e, dt_y, dt_l, dt_ok = (sem(n) for n in ("c_ch", "dt_x", "dt_e", "dt_y", "dt_l", "dt_ok"))
        bb_ps, cb_ps, a_ok, cb_ok = sem("bb_ps"), sem("cb_ps"), sem("a_ok"), sem("cb_ok")
        bu_ok, h_ok, hc_ok, st_ok, y_acc = (sem(n) for n in ("bu_ok", "h_ok", "hc_ok", "st_ok", "y_acc"))
        y_tok, yT_ps, yz_ok, st0 = sem("y_tok"), sem("yT_ps"), sem("yz_ok"), sem("st0")
        o_ps, d_ch, d_tok, dT_ps, dT_sb, lg_ps, lg_ok = (sem(n) for n in
            ("o_ps", "d_ch", "d_tok", "dT_ps", "dT_sb", "lg_ps", "lg_ok"))
        e_req, e_ok, w_ok = sem("e_req"), sem("e_ok"), sem("w_ok")
        wT_ps, wT_sb, up_ps, g_ok, dn, ye_ps, ye_dve, out_ok = (sem(n) for n in
            ("wT_ps", "wT_sb", "up_ps", "g_ok", "dn", "ye_ps", "ye_dve", "out_ok"))
        stored = [sem("stored0"), sem("stored1")]
        loop_sems = sems[5:]

        def tile4(bank, n):
            return bank[0:TT, 0:KT * n].rearrange("p (k n) -> p k n", n=n)

        def bc_last(ap, n):
            return ap.unsqueeze(2).to_broadcast([ap.shape[0], ap.shape[1], n])

        def norm_steps(dve, link, src, xc, i, pw_n):
            V = nc.vector
            st = stat[:, i]
            link(V.reduce_sum(st[:, 0, :], src, axis=AX.X))
            link(V.tensor_scalar(st[:, 0, :], st[:, 0, :], 1.0 / C, None, ALU.mult))
            link(V.tensor_tensor(xc, src, bc_last(st[:, 0, :], C), ALU.subtract))
            link(V.tensor_tensor(tmp[:, 2], xc, xc, ALU.mult))
            link(V.reduce_sum(st[:, 5, :], tmp[:, 2], axis=AX.X))
            link(V.tensor_scalar(st[:, 5, :], st[:, 5, :], 1.0 / C, None, ALU.mult))
            V.tensor_scalar(st[:, 1, :], st[:, 5, :], LN_EPS, None, ALU.add).then_inc(pw_req, 1)
            dve.wait_ge(pw_done, pw_n + 1)
            link(V.tensor_tensor(st[:, 3, :], st[:, 5, :], st[:, 2, :], ALU.mult))
            link(V.tensor_tensor(st[:, 3, :], st[:, 3, :], st[:, 2, :], ALU.mult))
            V.tensor_scalar(st[:, 3, :], st[:, 3, :], LN_EPS, None, ALU.add).then_inc(pw_req, 1)
            dve.wait_ge(pw_done, pw_n + 2)

        def linker(dve, s):
            count = [0]

            def link(ins):
                count[0] += 1
                ins.then_inc(s, 1)
                dve.wait_ge(s, count[0])
            return link

        def rev(ap, d):
            return ap[:, ::-1] if d else ap

        def chunk_of(k):
            return k // 2 if k % 2 == 0 else NCH - 1 - k // 2

        with nc.Fori(0, NB) as img:
            with nc.Block() as block:
                @block.sync
                def _(sp_):
                    sp_.dma_start(x_tok[:, :, :], x_dram[img]).then_inc(x_in, 16)

                @block.gpsimd
                def _(pool):
                    for c in range(NCH):
                        i = c % 2
                        pool.wait_ge(pw_req, 2 * c + 1)
                        nc.gpsimd.tensor_tensor(stat[:, i, 2, :], stat[:, i, 1, :], half_pow[0:TT, 0:KT], ALU.pow)\
                            .then_inc(pw_done, 1)
                        pool.wait_ge(pw_req, 2 * c + 2)
                        nc.gpsimd.tensor_tensor(stat[:, i, 4, :], stat[:, i, 3, :], half_pow[0:TT, 0:KT], ALU.pow)\
                            .then_inc(pw_done, 1)

                @block.tensor
                def _(pe):
                    def first(c):
                        pe.wait_ge(x_in, 16)
                        if c:
                            pe.wait_ge(xT_sb, c)
                        for k in range(KT):
                            last = nc.tensor.transpose(ps[0][0:C, k * TT:(k + 1) * TT], x_tok[:, c * KT + k, :],
                                                       ident[0:TT, 0:TT])
                        last.then_inc(xT_ps, 1)
                        pe.wait_ge(xT_sb, c + 1)
                        if c:
                            pe.wait_ge(h1_sb, c)
                        nc.tensor.matmul(ps[1][:, 0:CH], w1[:, :], xT[:, c % 2, :], start=True, stop=True)\
                            .then_inc(h1_ps, 1)

                    def second(c):
                        pe.wait_ge(h1_sb, min(c + 2, NCH))
                        if c:
                            pe.wait_ge(h2_sb, c)
                        for t in range(9):
                            dy, dx = t // 3, t % 3
                            last = nc.tensor.matmul(ps[2][:, 0:CH], w2[:, t, :],
                                                    h1v[:, c * ROWS + dy:c * ROWS + dy + ROWS, dx:dx + WW],
                                                    start=(t == 0), stop=(t == 8))
                        last.then_inc(h2_ps, 1)

                    def third(c):
                        def fold(m):
                            src = rz[:, m % 4, :] if m < ZP // 2 else acc[:, c % 2, :]
                            if m < ZP // 2:
                                pe.wait_ge(z_act, c * ZP // 2 + m + 1)
                            else:
                                pe.wait_ge(z_dve, c * ZP // 2 + ZP // 2)
                            if m == 0 and c:
                                pe.wait_ge(x1_out, c)
                            for k in range(KT):
                                last = nc.tensor.matmul(ps[3][0:TT, k * 128:(k + 1) * 128],
                                                        src[:, k * TT:(k + 1) * TT], ident[:, :], is_transpose=True,
                                                        start=(m == 0 and k == 0), stop=(m == ZP // 2 and k == KT - 1),
                                                        skip_group_check=True)
                            last.then_inc(z_T, 1)

                        pe.wait_ge(h2_sb, c + 1)
                        for j in range(ZP):
                            g = c * ZP + j
                            if g >= 4:
                                pe.wait_ge(z_dve if j % 2 == 0 else z_act, (g - 4) // 2 + 1)
                            q, jj = j // 4, j % 4
                            nc.tensor.matmul(ps[4 + j % 4][:, 0:CH], w3[32 * q:32 * q + 32, 2 * jj:2 * jj + 2, :],
                                             h2[32 * q:32 * q + 32, c % 2, :], start=True, stop=True,
                                             tile_position=(32 * q, 0)).then_inc(z_ps, 1)
                            if j % 2 == 1 and j >= 5:
                                fold((j - 5) // 2)
                        for m in range((ZP - 4) // 2, ZP // 2 + 1):
                            fold(m)

                    def norm_T(c):
                        pe.wait_ge(xn_tok, c + 1)
                        pe.wait_ge(xT_sb, min(c + 3, NCH))
                        if c:
                            pe.wait_ge(xn_sb, c)
                        for k in range(KT):
                            last = nc.tensor.transpose(ps[0][64:64 + C, k * TT:(k + 1) * TT] if False else
                                                       ps[2][0:C, k * TT:(k + 1) * TT], xnt[:, c % 2, k, :],
                                                       ident[0:TT, 0:TT])
                        last.then_inc(xn_ps, 1)

                    first(0)
                    first(1)
                    second(0)
                    for c in range(NCH):
                        if c + 2 < NCH:
                            first(c + 2)
                        if c + 1 < NCH:
                            second(c + 1)
                        third(c)
                        if c >= 1:
                            pe.wait_ge(h2_sb, min(c + 2, NCH))
                            norm_T(c - 1)
                            pe.wait_ge(xn_sb, c)
                    norm_T(NCH - 1)

                @block.scalar
                def _(act):
                    A = nc.scalar

                    def evac_x(c):
                        act.wait_ge(xT_ps, c + 1)
                        if c >= 2:
                            act.wait_ge(h1_ps, c - 1)
                        A.activation(xT[:, c % 2, :], ps[0][0:C, 0:CH], ACT.Copy).then_inc(xT_sb, 1)
                        act.wait_ge(h1_ps, c + 1)
                        A.activation(h1v[:, 1 + c * ROWS:1 + (c + 1) * ROWS, 1:1 + WW],
                                     ps[1][:, 0:CH].rearrange("p (r w) -> p r w", w=WW), ACT.Relu,
                                     bias=bnb[:, 0:1], scale=bng[:, 0:1]).then_inc(h1_sb, 1)

                    def evac_h2(c):
                        act.wait_ge(h2_ps, c + 1)
                        if c >= 2:
                            act.wait_ge(z_ps, ZP * (c - 1))
                        A.activation(h2[:, c % 2, :], ps[2][:, 0:CH], ACT.Relu,
                                     bias=bnb[:, 1:2], scale=bng[:, 1:2]).then_inc(h2_sb, 1)

                    def evac_xn(c):
                        act.wait_ge(xn_ps, c + 1)
                        t0 = c * CH
                        A.activation(xn[0:C, 3 + t0:3 + t0 + CH], ps[2][0:C, 0:CH], ACT.Identity,
                                     bias=gb[:, 1:2], scale=gb[:, 0:1])
                        A.activation(xn[C:128, 2 + t0:2 + t0 + CH], ps[2][0:C, 0:CH], ACT.Identity,
                                     bias=gb[:, 1:2], scale=gb[:, 0:1]).then_inc(xn_sb, 1)

                    evac_x(0)
                    evac_x(1)
                    evac_h2(0)
                    for c in range(NCH):
                        if c + 2 < NCH:
                            evac_x(c + 2)
                        if c + 1 < NCH:
                            evac_h2(c + 1)
                        for m in range(ZP // 2):
                            g = c * (ZP // 2) + m
                            act.wait_ge(z_ps, c * ZP + 2 * m + 2)
                            if g >= 4:
                                gg = g - 4
                                act.wait_ge(z_T, (gg // 8) * 9 + gg % 8 + 1)
                            A.activation(rz[:, m % 4, :], ps[4 + (2 * m + 1) % 4][:, 0:CH], ACT.Relu,
                                         bias=bnb[:, 3 + 2 * m:4 + 2 * m]).then_inc(z_act, 1)
                        if c >= 1:
                            evac_xn(c - 1)
                    evac_xn(NCH - 1)

                @block.vector
                def _(dve):
                    V = nc.vector
                    link = linker(dve, a_ch)

                    def sums(c):
                        a = acc[:, c % 2, :]
                        if c >= 2:
                            dve.wait_ge(z_T, 9 * (c - 1))
                        for m in range(ZP // 2):
                            z = ps[4 + (2 * m) % 4][:, 0:CH]
                            dve.wait_ge(z_ps, c * ZP + 2 * m + 1)
                            if m:
                                dve.wait_ge(z_dve, c * (ZP // 2) + m)
                                V.scalar_tensor_tensor(a, z, nb3[:, 2 * m:2 * m + 1], a, ALU.max, ALU.add)\
                                    .then_inc(z_dve, 1)
                            else:
                                V.tensor_scalar(a, z, nb3[:, 0:1], sum_b3[:, 0:1], ALU.max, ALU.add)\
                                    .then_inc(z_dve, 1)

                    def norms(c):
                        n0 = c * KT
                        r = res[:, n0:n0 + KT, :]
                        b3 = tile4(ps[3], 128)
                        dve.wait_ge(z_T, 9 * (c + 1))
                        link(V.tensor_tensor(tmp[:, 0], b3[:, :, 0:C], x_tok[:, n0:n0 + KT, :], ALU.add))
                        ins = V.tensor_tensor(tmp[:, 1], b3[:, :, C:128], tmp[:, 0], ALU.add)
                        ins.then_inc(x1_out, 1)
                        dve.wait_ge(x1_out, c + 1)
                        link(V.tensor_scalar(r, tmp[:, 1], 0.0, None, ALU.max))
                        norm_steps(dve, link, r, tmp[:, 0], c % 2, 2 * c)
                        link(V.tensor_tensor(tmp[:, 1], tmp[:, 0], bc_last(stat[:, c % 2, 2, :], C), ALU.mult))
                        link(V.tensor_tensor(r, r, tmp[:, 1], ALU.add))
                        if c >= 2:
                            dve.wait_ge(xn_ps, c - 1)
                        V.tensor_tensor(xnt[:, c % 2], tmp[:, 1], bc_last(stat[:, c % 2, 4, :], C), ALU.mult)\
                            .then_inc(xn_tok, 1)

                    for c in range(NCH):
                        sums(c)
                        norms(c)

            with nc.Block() as block:
                @block.tensor
                def _(pe):
                    for i in range(2 * STEPS):
                        c, d, z = i // 4, (i // 2) % 2, i % 2
                        t0 = c * CH
                        if i >= 8:
                            pe.wait_ge(b_sb, i - 7)
                        bank = ps[i % 8][:, 0:CH]
                        if z:
                            nc.tensor.matmul(bank, wz[d][:, :], xn[0:C, t0 + 3:t0 + 3 + CH], start=True, stop=True)\
                                .then_inc(b_ps, 1)
                        else:
                            at = t0 + 3 * d
                            nc.tensor.matmul(bank, wx[d][:, 0, :], xn[:, at:at + CH], start=True, stop=False)
                            nc.tensor.matmul(bank, wx[d][:, 1, :], xn[:, at + 2:at + 2 + CH], start=False, stop=True)\
                                .then_inc(b_ps, 1)

                @block.scalar
                def _(act):
                    for i in range(2 * STEPS):
                        c, d, z = i // 4, (i // 2) % 2, i % 2
                        act.wait_ge(b_ps, i + 1)
                        if z:
                            nc.scalar.activation(zs[d][:, c * CH:(c + 1) * CH], ps[i % 8][:, 0:CH], ACT.Silu)\
                                .then_inc(b_sb, 1)
                        else:
                            nc.scalar.activation(u[d][:, c * CH:(c + 1) * CH], ps[i % 8][:, 0:CH], ACT.Silu,
                                                 bias=dvec[d][:, 0:1]).then_inc(b_sb, 1)

            def ucols(k):
                c = chunk_of(k)
                return u[k % 2][:, c * CH:(c + 1) * CH]

            PREP_AT, POST_AT = 5, 3

            with nc.Block() as block:
                @block.tensor
                def _(pe):
                    def prep(k):
                        d, c = k % 2, chunk_of(k)
                        if k >= 2:
                            pe.wait_ge(yz_ok, k - 1)
                        if k:
                            pe.wait_ge(bcT_sb, k)
                        nc.tensor.matmul(ps[0][:, 0:CH], wdt[d][:, :], ucols(k), start=True, stop=True)\
                            .then_inc(dt_ps, 1)
                        for j in range(KT):
                            last = nc.tensor.matmul(ps[1][0:TT, 32 * j:32 * j + 32],
                                                    u[d][:, c * CH + j * TT:c * CH + (j + 1) * TT], wbc[d][:, :],
                                                    start=True, stop=True)
                        last.then_inc(bc_ps, 1)

                    def prep_T(k):
                        pe.wait_ge(bc_tok, k + 1)
                        out = ps[1][0:96, 0:CH // 2].bitcast(BF16)
                        for j in range(KT):
                            last = nc.tensor.transpose(out[:, j * TT:(j + 1) * TT],
                                                       bct[:, j].rearrange("p a b -> p (a b)"), identb[0:TT, 0:TT])
                        last.then_inc(bcT_ps, 1)

                    def fold(g):
                        k, s = g // DS, g % DS
                        pe.wait_ge(hc_ok, g + 1)
                        if s == 0 and k >= 2:
                            pe.wait_ge(y_tok, k - 1)
                        bank = ps[2 if k % 2 == 0 else 7]
                        for j in range(KT):
                            last = nc.tensor.matmul(bank[0:TT, j * 128:(j + 1) * 128],
                                                    hc[:, g % 3, j * TT:(j + 1) * TT], ident[:, :], is_transpose=True,
                                                    start=(s == 0 and j == 0), stop=(s == DS - 1 and j == KT - 1),
                                                    skip_group_check=True)
                        last.then_inc(y_acc, 1)

                    def post(k):
                        pe.wait_ge(y_tok, k + 1)
                        if k + 1 < STEPS:
                            pe.wait_ge(dt_ok, k + 2)
                        for j in range(KT):
                            last = nc.tensor.transpose(ps[0][:, j * TT:(j + 1) * TT], ytok[:, j * 128:(j + 1) * 128],
                                                       ident[0:TT, 0:TT])
                        last.then_inc(yT_ps, 1)

                    prep(0)
                    prep_T(0)
                    G = STEPS * DS
                    for g in range(G):
                        k, s = g // DS, g % DS
                        if s == 0:
                            pe.wait_ge(bcT_sb, k + 1)
                        if g >= 2:
                            pe.wait_ge(bu_ok, g - 1)
                            pe.wait_ge(cb_ok, g - 1)
                        nc.tensor.matmul(ps[3 + g % 2][:, 0:CH], pick[:, s, :], bc3[:, k % 2, :], start=True, stop=True)\
                            .then_inc(bb_ps, 1)
                        nc.tensor.matmul(ps[5 + g % 2][:, 0:CH], pick[:, DS + s, :], bc3[:, k % 2, :],
                                         start=True, stop=True).then_inc(cb_ps, 1)
                        if g >= 3:
                            fold(g - 3)
                        if s == POST_AT + 1 and k:
                            post(k - 1)
                        if s == 8 and k + 1 < STEPS:
                            prep(k + 1)
                        if s == 12 and k + 1 < STEPS:
                            prep_T(k + 1)
                    for g in range(G - 3, G):
                        fold(g)
                    post(STEPS - 1)

                @block.scalar
                def _(act):
                    A = nc.scalar
                    A.preload_act_table_set("natural_log_exp_and_others")

                    def soft_exp(k):
                        act.wait_ge(dt_x, k + 1)
                        A.activation(sp[:, 1, :], sp[:, 0, :], ACT.Exp).then_inc(dt_e, 1)

                    def soft_ln(k):
                        act.wait_ge(dt_y, k + 1)
                        A.activation(sp[:, 3, :], sp[:, 2, :], ACT.Ln).then_inc(dt_l, 1)

                    def copy_bc(k):
                        act.wait_ge(bcT_ps, k + 1)
                        A.activation(bc3[:, k % 2, :], ps[1][0:96, 0:CH // 2].bitcast(BF16), ACT.Copy)\
                            .then_inc(bcT_sb, 1)

                    soft_exp(0)
                    soft_ln(0)
                    copy_bc(0)
                    G = STEPS * DS
                    for g in range(G):
                        k, s = g // DS, g % DS
                        if s == 0:
                            act.wait_ge(dt_ok, k + 1)
                        if g >= 3:
                            act.wait_ge(h_ok, g - 2)
                        A.activation(dA[:, g % 3, :], dtv[:, k % 2, :], ACT.Exp, scale=dvec[k % 2][:, 3 + s:4 + s])\
                            .then_inc(a_ok, 1)
                        act.wait_ge(cb_ps, g + 1)
                        if g >= 3:
                            act.wait_ge(hc_ok, g - 2)
                        A.activation(cb[:, g % 3, :], ps[5 + g % 2][:, 0:CH], ACT.Copy).then_inc(cb_ok, 1)
                        if s == POST_AT and k:
                            act.wait_ge(y_acc, DS * k)
                            A.activation(ytok[:, :], ps[2 if (k - 1) % 2 == 0 else 7][0:TT, :], ACT.Copy)\
                                .then_inc(y_tok, 1)
                        if k + 1 < STEPS:
                            if s == 10:
                                soft_exp(k + 1)
                            if s == 12:
                                soft_ln(k + 1)
                            if s == 13:
                                copy_bc(k + 1)
                    act.wait_ge(y_acc, G)
                    A.activation(ytok[:, :], ps[2 if (STEPS - 1) % 2 == 0 else 7][0:TT, :], ACT.Copy)\
                        .then_inc(y_tok, 1)

                @block.vector
                def _(dve):
                    V = nc.vector
                    link = linker(dve, c_ch)

                    def split_bc(k):
                        dve.wait_ge(bc_ps, k + 1)
                        src = tile4(ps[1], 2 * DS)
                        if k:
                            dve.wait_ge(bcT_ps, k)
                        link(V.tensor_copy(bct[:, :, 0, :], src))
                        link(V.tensor_tensor(bcr[:, :, :], src, bct[:, :, 0, :], ALU.subtract))
                        link(V.tensor_copy(bct[:, :, 1, :], bcr[:, :, :]))
                        link(V.tensor_tensor(bcr[:, :, :], bcr[:, :, :], bct[:, :, 1, :], ALU.subtract))
                        V.tensor_copy(bct[:, :, 2, :], bcr[:, :, :]).then_inc(bc_tok, 1)

                    def soft_x(k):
                        dve.wait_ge(dt_ps, k + 1)
                        V.tensor_scalar(sp[:, 0, :], ps[0][:, 0:CH], dvec[k % 2][:, 1:2], DT_CLAMP, ALU.add, ALU.min)\
                            .then_inc(dt_x, 1)

                    def soft_y(k):
                        dve.wait_ge(dt_e, k + 1)
                        V.tensor_scalar(sp[:, 2, :], sp[:, 1, :], 1.0, None, ALU.add).then_inc(dt_y, 1)
                        dve.wait_ge(dt_y, k + 1)
                        link(V.scalar_tensor_tensor(sp[:, 1, :], sp[:, 2, :], -1.0, sp[:, 1, :], ALU.add, ALU.subtract))

                    def soft_end(k):
                        dve.wait_ge(dt_l, k + 1)
                        link(V.tensor_tensor(sp[:, 3, :], sp[:, 3, :], sp[:, 1, :], ALU.subtract))
                        V.scalar_tensor_tensor(dtv[:, k % 2, :], ps[0][:, 0:CH], dvec[k % 2][:, 1:2], sp[:, 3, :],
                                               ALU.add, ALU.max).then_inc(dt_ok, 1)
                        dve.wait_ge(dt_ok, k + 1)
                        link(V.tensor_tensor(dtu[:, k % 2, :], dtv[:, k % 2, :], ucols(k), ALU.mult))

                    def finish(k):
                        c = chunk_of(k)
                        z = zs[k % 2][:, c * CH:(c + 1) * CH]
                        dve.wait_ge(yT_ps, k + 1)
                        V.scalar_tensor_tensor(sp[:, 0, :], ucols(k), dvec[k % 2][:, 2:3], ps[0][:, 0:CH],
                                               ALU.mult, ALU.add).then_inc(yz_ok, 1)
                        dve.wait_ge(yz_ok, k + 1)
                        link(V.tensor_tensor(z, z, sp[:, 0, :], ALU.mult))

                    link(V.memset(state[:, :, :], 0.0))
                    soft_x(0)
                    split_bc(0)
                    soft_y(0)
                    soft_end(0)
                    G = STEPS * DS

                    def bu(g):
                        k = g // DS
                        dve.wait_ge(bb_ps, g + 1)
                        V.tensor_tensor(dBu[:, g % 2, :], ps[3 + g % 2][:, 0:CH], dtu[:, k % 2, :], ALU.mult)\
                            .then_inc(bu_ok, 1)

                    bu(0)
                    for g in range(G):
                        k, s, d = g // DS, g % DS, (g // DS) % 2
                        if g + 1 < G:
                            if g >= 1:
                                dve.wait_ge(h_ok, g)
                            bu(g + 1)
                        dve.wait_ge(bu_ok, g + 1)
                        dve.wait_ge(a_ok, g + 1)
                        if g >= 3:
                            dve.wait_ge(hc_ok, g - 2)
                        if g >= 2 * DS:
                            dve.wait_ge(st_ok, g - 2 * DS + 1)
                        V.tensor_tensor_scan(rev(hs[:, g % 3, :], d), rev(dA[:, g % 3, :], d), rev(dBu[:, g % 2, :], d),
                                             state[:, d, s:s + 1], ALU.mult, ALU.add).then_inc(h_ok, 1)
                        if s == POST_AT + 2 and k:
                            finish(k - 1)
                        if k + 1 < STEPS:
                            if s == 9:
                                soft_x(k + 1)
                                split_bc(k + 1)
                            if s == 11:
                                soft_y(k + 1)
                            if s == 13:
                                soft_end(k + 1)
                    finish(STEPS - 1)

                @block.gpsimd
                def _(pool):
                    P = nc.gpsimd
                    G = STEPS * DS
                    for g in range(G):
                        s, d = g % DS, (g // DS) % 2
                        pool.wait_ge(h_ok, g + 1)
                        at = 0 if d else CH - 1
                        P.tensor_copy(state[:, d, s:s + 1], hs[:, g % 3, at:at + 1]).then_inc(st_ok, 1)
                        pool.wait_ge(cb_ok, g + 1)
                        if g >= 3:
                            pool.wait_ge(y_acc, g - 2)
                        P.tensor_tensor(hc[:, g % 3, :], hs[:, g % 3, :], cb[:, g % 3, :], ALU.mult).then_inc(hc_ok, 1)

            with nc.Block() as block:
                @block.tensor
                def _(pe):
                    def outp(c):
                        if c >= 2:
                            pe.wait_ge(d_tok, c - 1)
                        for j in range(KT):
                            t0 = c * CH + j * TT
                            for d in range(2):
                                last = nc.tensor.matmul(ps[c % 2][0:TT, j * C:(j + 1) * C], zs[d][:, t0:t0 + TT],
                                                        wo[d][:, :], start=(d == 0), stop=(d == 1))
                        last.then_inc(o_ps, 1)

                    def route(c):
                        pe.wait_ge(d_tok, c + 1)
                        if c:
                            pe.wait_ge(dT_sb, c)
                        for j in range(KT):
                            last = nc.tensor.transpose(ps[2][0:C, j * TT:(j + 1) * TT], xnt[:, c % 2, j, :],
                                                       ident[0:TT, 0:TT])
                        last.then_inc(dT_ps, 1)
                        pe.wait_ge(dT_sb, c + 1)
                        for j in range(KT):
                            t0 = c * CH + j * TT
                            last = nc.tensor.matmul(ps[3][0:TT, (c * KT + j) * EX:(c * KT + j + 1) * EX],
                                                    xn[0:C, 3 + t0:3 + t0 + TT], wr[:, :], start=True, stop=True)
                        last.then_inc(lg_ps, 1)

                    outp(0)
                    for c in range(NCH):
                        if c + 1 < NCH:
                            outp(c + 1)
                        route(c)

                @block.scalar
                def _(act):
                    for c in range(NCH):
                        act.wait_ge(dT_ps, c + 1)
                        nc.scalar.activation(xn[0:C, 3 + c * CH:3 + (c + 1) * CH], ps[2][0:C, 0:CH], ACT.Copy)\
                            .then_inc(dT_sb, 1)
                    act.wait_ge(e_req, 1)
                    nc.scalar.activation(l1[:, 4, :], l1[:, 3, :], ACT.Exp).then_inc(e_ok, 1)

                @block.gpsimd
                def _(pool):
                    for c in range(NCH):
                        i = c % 2
                        pool.wait_ge(pw_req, 2 * NCH + 2 * c + 1)
                        nc.gpsimd.tensor_tensor(stat[:, i, 2, :], stat[:, i, 1, :], half_pow[0:TT, 0:KT], ALU.pow)\
                            .then_inc(pw_done, 1)
                        pool.wait_ge(pw_req, 2 * NCH + 2 * c + 2)
                        nc.gpsimd.tensor_tensor(stat[:, i, 4, :], stat[:, i, 3, :], half_pow[0:TT, 0:KT], ALU.pow)\
                            .then_inc(pw_done, 1)

                @block.vector
                def _(dve):
                    V = nc.vector
                    link = linker(dve, d_ch)
                    for c in range(NCH):
                        n0 = c * KT
                        r = res[:, n0:n0 + KT, :]
                        dve.wait_ge(o_ps, c + 1)
                        link(V.tensor_tensor(r, tile4(ps[c % 2], C), r, ALU.add))
                        norm_steps(dve, link, r, tmp[:, 0], c % 2, 2 * NCH + 2 * c)
                        st = stat[:, c % 2]
                        link(V.tensor_tensor(sq2[:, n0:n0 + KT], st[:, 3, :], st[:, 4, :], ALU.mult))
                        link(V.tensor_tensor(tmp[:, 1], tmp[:, 0], bc_last(st[:, 2, :], C), ALU.mult))
                        if c >= 2:
                            dve.wait_ge(dT_ps, c - 1)
                        V.tensor_tensor(xnt[:, c % 2], tmp[:, 1], bc_last(st[:, 4, :], C), ALU.mult)\
                            .then_inc(d_tok, 1)
                    dve.wait_ge(lg_ps, NCH)
                    L, eq, cand, s1, s2, t8 = (lg[:, i] for i in range(6))
                    rk = rank8[:, :].unsqueeze(1).to_broadcast([TT, NT, EX])
                    link(V.tensor_tensor(L, ps[3][0:TT, 0:NT * EX].rearrange("p (n e) -> p n e", e=EX),
                                         bc_last(sq2[:, :], EX), ALU.mult))
                    link(V.tensor_tensor(L, L, br[:, :].unsqueeze(1).to_broadcast([TT, NT, EX]), ALU.add))

                    def top(src, sel, m):
                        link(V.reduce_max(m, src, axis=AX.X))
                        link(V.tensor_tensor(eq, src, bc_last(m, EX), ALU.is_equal))
                        link(V.tensor_tensor(cand, eq, rk, ALU.mult))
                        link(V.reduce_max(l1[:, 7, :], cand, axis=AX.X))
                        link(V.tensor_tensor(sel, rk, bc_last(l1[:, 7, :], EX), ALU.is_equal))

                    top(L, s1, l1[:, 0, :])
                    link(V.scalar_tensor_tensor(t8, s1, -FAR, L, ALU.mult, ALU.add))
                    top(t8, s2, l1[:, 1, :])
                    V.tensor_tensor(l1[:, 3, :], l1[:, 1, :], l1[:, 0, :], ALU.subtract).then_inc(e_req, 1)
                    dve.wait_ge(e_ok, 1)
                    link(V.tensor_scalar(l1[:, 5, :], l1[:, 4, :], 1.0, None, ALU.add))
                    link(V.reciprocal(l1[:, 5, :], l1[:, 5, :]))
                    link(V.tensor_tensor(l1[:, 6, :], l1[:, 4, :], l1[:, 5, :], ALU.mult))
                    link(V.tensor_tensor(s1, s1, bc_last(l1[:, 5, :], EX), ALU.mult))
                    link(V.tensor_tensor(s2, s2, bc_last(l1[:, 6, :], EX), ALU.mult))
                    link(V.tensor_tensor(wgt[:, :, :], s1, s2, ALU.add))

            with nc.Block() as block:
                G = NCH * MT

                @block.tensor
                def _(pe):
                    def up(g):
                        c, m = g // MT, g % MT
                        if g >= 3:
                            pe.wait_ge(g_ok, g - 2)
                        nc.tensor.matmul(ps[g % 3][:, 0:CH], we1[:, m, :], xn[0:C, 3 + c * CH:3 + (c + 1) * CH],
                                         start=True, stop=True).then_inc(up_ps, 1)

                    def down(g):
                        c, m = g // MT, g % MT
                        pe.wait_ge(g_ok, g + 1)
                        for j in range(KT):
                            if m == 0 and c:
                                pe.wait_ge(ye_dve, (c - 1) * KT + j + 1)
                            e = m // 2
                            last = nc.tensor.matmul(ps[3 + j][0:TT, e * C:(e + 1) * C],
                                                    hg[:, g % 4, j * TT:(j + 1) * TT], we2[:, m, :],
                                                    start=(m % 2 == 0), stop=(m % 2 == 1))
                            if m == MT - 1:
                                last.then_inc(ye_ps, 1)
                        last.then_inc(dn, 1) if m < MT - 1 else None

                    def bias(c):
                        if c:
                            pe.wait_ge(out_ok, c)
                        for j in range(KT):
                            last = nc.tensor.transpose(ps[7][0:EX, j * TT:(j + 1) * TT], wgt[:, c * KT + j, :],
                                                       ident[0:TT, 0:TT])
                        last.then_inc(wT_ps, 1)
                        pe.wait_ge(wT_sb, c + 1)
                        for j in range(KT):
                            last = nc.tensor.matmul(ps[7][0:TT, j * C:(j + 1) * C], wT[:, c % 2, j * TT:(j + 1) * TT],
                                                    be2[:, :], start=True, stop=True)
                        last.then_inc(lg_ok, 1)

                    up(0)
                    up(1)
                    for g in range(G):
                        if g + 2 < G:
                            up(g + 2)
                        down(g)
                        if g % MT == 2:
                            bias(g // MT)

                @block.scalar
                def _(act):
                    for g in range(G):
                        c, m = g // MT, g % MT
                        act.wait_ge(up_ps, g + 1)
                        if g >= 4:
                            o = g - 4
                            if o % MT == MT - 1:
                                act.wait_ge(ye_ps, KT * (o // MT + 1))
                            else:
                                act.wait_ge(dn, (o // MT) * (MT - 1) + o % MT + 1)
                        nc.scalar.activation(hg[:, g % 4, :], ps[g % 3][:, 0:CH], ACT.Gelu, bias=be1[:, m:m + 1])\
                            .then_inc(g_ok, 1)
                        if m == 4:
                            act.wait_ge(wT_ps, c + 1)
                            nc.scalar.activation(wT[:, c % 2, :], ps[7][0:EX, 0:CH], ACT.Copy).then_inc(wT_sb, 1)

                @block.vector
                def _(dve):
                    V = nc.vector
                    link = linker(dve, w_ok)
                    for c in range(NCH):
                        dve.wait_ge(lg_ok, c + 1)
                        if c >= 2:
                            dve.wait_ge(stored[c % 2], 16 * (c // 2))
                        ob = outb[:, c % 2]
                        V.tensor_tensor(ob, tile4(ps[7], C), res[:, c * KT:(c + 1) * KT, :], ALU.add)\
                            .then_inc(w_ok, 1)
                        for j in range(KT):
                            dve.wait_ge(ye_ps, c * KT + j + 1)
                            i = j % 2
                            V.tensor_tensor(yw[:, i], ps[3 + j][0:TT, :].rearrange("p (e c) -> p e c", c=C),
                                            bc_last(wgt[:, c * KT + j, :], C), ALU.mult).then_inc(ye_dve, 1)
                            dve.wait_ge(ye_dve, c * KT + j + 1)
                            V.reduce_sum(red[:, i, :], yw[:, i].rearrange("p e c -> p c e"), axis=AX.X)\
                                .then_inc(w_ok, 1)
                            dve.wait_ge(w_ok, c * 5 + j + 2)
                            last = V.tensor_tensor(ob[:, j, :], ob[:, j, :], red[:, i, :], ALU.add)
                        last.then_inc(out_ok, 1)

                @block.sync
                def _(sp_):
                    for c in range(NCH):
                        sp_.wait_ge(out_ok, c + 1)
                        if c >= 2:
                            sp_.wait_ge(stored[c % 2], 16 * (c // 2))
                        sp_.dma_start(o_dram[img][:, c * KT:(c + 1) * KT, :], outb[:, c % 2]).then_inc(stored[c % 2], 16)
                    for i in range(2):
                        sp_.wait_ge(stored[i], 16 * ((NCH + 1 - i) // 2))

            for s in loop_sems:
                nc.gpsimd.sem_clear(s)
            nc.all_engine_barrier()


def _layouts(np, I):
    a = {k: np.asarray(v) for k, v in I.items()}
    L = {"x": a["x"]}
    cv = lambda n: a["L0_conv_" + n]
    L["ident"] = np.eye(128, dtype=np.float32)
    L["path_mask"] = np.repeat(np.eye(PATHS, dtype=np.float32), PD, axis=0)
    L["pair_mask"] = np.tile(np.repeat(np.eye(8, dtype=np.float32), PD, axis=0), (4, 1))
    L["rank8"] = np.tile(np.arange(EX, 0, -1, dtype=np.float32), (TT, 1))
    L["pick"] = np.tile(np.eye(2 * DS, dtype=np.float32), (3, 1))
    L["w1"] = cv("W1").transpose(1, 0, 2).reshape(C, 128)
    L["w2"] = cv("W2").transpose(0, 3, 1, 2, 4).reshape(128, 9, PD)
    L["w3"] = cv("W3").reshape(128, C)

    def wide(n):
        third = cv(n + "3").reshape(ZP, 2, C).transpose(1, 2, 0).reshape(128, ZP)
        return np.concatenate([cv(n + "1").reshape(128, 1), cv(n + "2").reshape(128, 1), third], axis=1)

    rows = lambda n: np.repeat(cv(n + "3"), PD, axis=0)
    L["bnv"] = np.concatenate([wide("V"), rows("V")], axis=1)
    L["bng"] = np.concatenate([wide("G"), rows("G")], axis=1)
    L["bnm"], L["bnb"], L["bnbe"] = wide("M"), wide("B"), wide("Be")
    L["gb"] = np.stack([a["L1_attn_ln_gamma"], a["L1_attn_ln_beta"]], axis=1)
    for d, p in enumerate("fb"):
        m = lambda n: a[f"L1_attn_{p}_{n}"]
        inp = m("in_proj_w").transpose(1, 0)
        L[f"wx{d}"] = np.tile(inp[:, 0:DI].reshape(1, C, 1, DI), (2, 1, 2, 1)).reshape(128, 2, DI)
        taps = m("conv_w").reshape(DI, TAPS).transpose(1, 0)
        if d:
            taps = taps[::-1]
        taps = taps.reshape(2, 2, DI).transpose(1, 0, 2)
        L[f"tapw{d}"] = np.repeat(taps, C, axis=0)
        L[f"wz{d}"] = inp[:, DI:2 * DI]
        L[f"wdt_a{d}"] = m("x_proj_w")[0:DR]
        L[f"wdt_b{d}"] = m("dt_proj_w").transpose(1, 0)
        L[f"wbc{d}"] = m("x_proj_w")[DR:DR + 2 * DS].transpose(1, 0)
        L[f"wo{d}"] = m("out_proj_w").transpose(1, 0)
        L[f"dvec{d}"] = np.concatenate([m("conv_b").reshape(DI, 1), m("dt_proj_b").reshape(DI, 1),
                                        m("D").reshape(DI, 1), m("A_log")], axis=1)
    f = lambda n: a["L1_ffn_" + n]
    L["we1"] = f("W1").transpose(1, 0, 2).reshape(C, MT, 128)
    L["we2"] = f("W2").reshape(MT, 128, C).transpose(1, 0, 2)
    L["be1"] = f("b1").reshape(MT, 128).transpose(1, 0)
    L["be2"] = f("b2")
    L["lng"], L["lnb"] = f("ln_g").transpose(1, 0), f("ln_b").transpose(1, 0)
    L["wr"] = f("Wr")
    L["br"] = np.tile(f("br").reshape(1, EX), (TT, 1))
    return {k: np.ascontiguousarray(v) for k, v in L.items()}


def kernel(**inputs):
    import numpy as _np
    import concourse.bacc as _bacc
    from concourse import mybir as _mybir
    from concourse.bass_utils import run_bass_kernel_spmd as _run

    nc = _bacc.Bacc("TRN2", target_bir_lowering=False, num_devices=1)
    arrays, T = {}, {}
    for name, a in _layouts(_np, inputs).items():
        arrays[f"in_{name}_dram"] = a
        T[name] = nc.dram_tensor(f"in_{name}_dram", a.shape, _mybir.dt.from_np(a.dtype), kind="ExternalInput").ap()
    T["out"] = nc.dram_tensor("out_0_dram", (NB, HH, WW, C), _mybir.dt.float32, kind="ExternalOutput").ap()
    build(nc, T)
    r = _run(nc, [arrays], core_ids=[0])
    return r.results[0]["out_0_dram"]
```

```python
import concourse.bass as bass
from concourse import mybir
from contextlib import ExitStack

F32 = mybir.dt.float32
BF16 = mybir.dt.bfloat16
ALU = mybir.AluOpType
ACT = mybir.ActivationFunctionType
AX = mybir.AxisListType

NB, HH, WW, C = 8, 56, 56, 64
TOK = HH * WW
ROWS = 8
CH = ROWS * WW
NCH = TOK // CH
TT = 112
KT = CH // TT
NT = TOK // TT
PATHS, PD = 32, 4
PW = WW + 2
ZP = PATHS * C // 128
DI, DS, DR, TAPS = 128, 16, 16, 4
EX, HID = 8, 256
MT = EX * HID // 128
LN_EPS, BN_EPS = 1e-5, 1e-3
DT_CLAMP = 40.0
FAR = 1.0e30
QUADS = 4
SLAB = (ROWS + 2) * PW
COMBOS = (0, 1, 2, 0, 1, 0)
W_COMBOS = (0, 0, 0, 1, 1, 2)
ZT = 8
ACT_J = (1, 4, 7, 9, 12, 15)
DVE_J = tuple(j for j in range(ZP) if j not in ACT_J)
STEPS = 2 * NCH


def build(nc, T):
    ctx = ExitStack()
    with ctx:
        def sb(name, shape, dt=F32):
            return ctx.enter_context(nc.sbuf_tensor(name, shape, dt))

        sems = []

        def sem(name):
            s = ctx.enter_context(nc.semaphore(name))
            sems.append(s)
            return s

        ident = sb("ident", [128, 128])
        identb = sb("identb", [128, 128], BF16)
        quad_mask = sb("quad_mask", [96, 8])
        four_mask = sb("four_mask", [96, 4])
        rank8 = sb("rank8", [TT, EX])
        pick_small = sb("pick_small", [128, 2 * DS])
        pick = sb("pick", [128, 2 * DS, 128], BF16)
        half_pow = sb("half_pow", [128, 82])
        w1 = sb("w1", [C, 128])
        w2c = sb("w2c", [96, 3 * QUADS, PD])
        w2 = sb("w2", [96, 3 * QUADS, 8 * PD])
        w3c = sb("w3c", [128, C])
        w3p = sb("w3p", [128, 3, C], BF16)
        w3x = sb("w3x", [96, ZT, C], BF16)
        w3 = sb("w3", [96, ZT, 4, C], BF16)
        bnv = sb("bnv", [128, 82])
        bng = sb("bng", [128, 82])
        bnm = sb("bnm", [128, 18])
        bnb = sb("bnb", [128, 18])
        bnbe = sb("bnbe", [128, 18])
        nb3 = sb("nb3", [128, ZP])
        sum_b3 = sb("sum_b3", [128, 1])
        gb = sb("gb", [C, 2])
        wx = [sb(f"wx{d}", [128, 2, DI]) for d in range(2)]
        tapw = [sb(f"tapw{d}", [128, 2, DI]) for d in range(2)]
        wz = [sb(f"wz{d}", [C, DI]) for d in range(2)]
        wdt_a = [sb(f"wdt_a{d}", [DR, DI]) for d in range(2)]
        wdt_b = [sb(f"wdt_b{d}", [DR, DI]) for d in range(2)]
        wdt = [sb(f"wdt{d}", [DI, DI]) for d in range(2)]
        wbc = [sb(f"wbc{d}", [DI, 2 * DS]) for d in range(2)]
        wo = [sb(f"wo{d}", [DI, C]) for d in range(2)]
        dvec = [sb(f"dvec{d}", [DI, 3 + DS]) for d in range(2)]
        we1s = [sb(f"we1s{i}", [128, MT, 128], BF16) for i in range(3)]
        we2 = sb("we2", [128, MT, C])
        pick_w_small = sb("pick_w_small", [3 * EX, EX])
        pick_w = sb("pick_w", [3 * EX, EX, C], BF16)
        be1 = sb("be1", [128, MT])
        be2 = sb("be2", [128, EX // 2])
        lng = sb("lng", [128, EX])
        lnb = sb("lnb", [128, EX])
        wr = sb("wr", [C, EX])
        br = sb("br", [TT, EX])

        x_tok = sb("x_tok", [TT, NT, C])
        res = sb("res", [TT, NT, C])
        xn = sb("xn", [128, TOK + 6])
        u = [sb(f"u{d}", [DI, TOK]) for d in range(2)]
        zs = [sb(f"zs{d}", [DI, TOK]) for d in range(2)]

        xT = sb("xT", [C, 2, CH])
        h1 = sb("h1", [128, (HH + 2) * PW + 2])
        h1v = h1[:, 0:(HH + 2) * PW].rearrange("p (r w) -> p r w", w=PW)
        h2 = sb("h2", [128, 2, CH])
        rz = sb("rz", [128, 4, CH])
        tmp = sb("tmp", [TT, 3, KT, C])
        xnt = sb("xnt", [TT, 2, KT, 2, C])
        stat = sb("stat", [TT, 2, 8, KT])
        sq2 = sb("sq2", [TT, NT])
        dtv = sb("dtv", [DI, 2, CH])
        dtu = sb("dtu", [DI, 2, CH])
        sp = sb("sp", [DI, 4, CH])
        bct = sb("bct", [TT, KT, 3, 2 * DS], BF16)
        bcr = sb("bcr", [TT, KT, 2 * DS])
        bc3 = sb("bc3", [128, 2, CH], BF16)
        dA = sb("dA", [DI, 3, CH])
        dBu = sb("dBu", [DI, 3, CH])
        acc = dBu
        hs = sb("hs", [DI, 3, CH])
        cb = sb("cb", [DI, 3, CH])
        hc = sb("hc", [DI, 3, CH])
        slab = [u[i][0:96, 0:QUADS * SLAB].rearrange("p (q n) -> p q n", q=QUADS) for i in range(2)]
        h2p = dA[:, :, :].rearrange("p a b -> p (a b)").bitcast(BF16).rearrange("p (i a n) -> p i a n", i=2, a=3)
        h3 = [zs[i][0:96, :].bitcast(BF16)[:, 0:ZT * CH].rearrange("p (t n) -> p t n", t=ZT) for i in range(2)]
        state = sb("state", [DI, 2, DS])
        ytok = sb("ytok", [TT, KT * 128])
        hg = rz
        lg = sp[0:TT, :, :].rearrange("p a b -> p (a b)").rearrange("p (i n e) -> p i n e", n=NT, e=EX)
        l1 = sb("l1", [TT, 8, NT])
        wgt = sb("wgt", [TT, NT, EX])
        wgt3 = sb("wgt3", [TT, NT, 3, EX], BF16)
        wT = sb("wT", [3 * EX, 2, CH], BF16)
        yw = dA
        wb = hs
        xn32 = cb[0:C, :, :]
        tok_parts = u[0][:, :].bitcast(BF16).rearrange("p (i t) -> p i t", i=2)
        we1 = u[1][:, 0:MT * 128].rearrange("p (m h) -> p m h", m=MT)
        we1r = zs[0][:, 0:MT * 128].rearrange("p (m h) -> p m h", m=MT)
        outb = dBu[0:TT, :, :].rearrange("p a b -> p (a b)")[:, 0:2 * KT * C].rearrange("p (i k c) -> p i k c", k=KT, c=C)

        ps = [ctx.enter_context(nc.psum_tensor(f"ps{i}", [128, 512], F32)) for i in range(8)]

        x_dram = T["x"].rearrange("b h w c -> b (h w) c").rearrange("b (n p) c -> b p n c", p=TT)
        o_dram = T["out"].rearrange("b h w c -> b (h w) c").rearrange("b (n p) c -> b p n c", p=TT)

        s_load = sem("s_load")
        s_prep = sem("s_prep")
        s_pool = sem("s_pool")
        s_pe = sem("s_pe")
        s_act = sem("s_act")
        s_w3, s_w3d, s_w3x = sem("s_w3"), sem("s_w3d"), sem("s_w3x")

        LOADS = [(ident, "ident"), (quad_mask, "quad_mask"), (four_mask, "four_mask"), (rank8, "rank8"),
                 (pick_small, "pick"), (w1, "w1"), (w2c, "w2"), (w3c, "w3"), (bnv, "bnv"), (bng, "bng"),
                 (bnm, "bnm"), (bnb, "bnb"), (bnbe, "bnbe"), (gb, "gb"), (we1, "we1"), (we2, "we2"),
                 (be1, "be1"), (be2, "be2"), (lng, "lng"), (lnb, "lnb"), (wr, "wr"), (br, "br"),
                 (pick_w_small, "pick_w")]
        for d in range(2):
            LOADS += [(wx[d], f"wx{d}"), (tapw[d], f"tapw{d}"), (wz[d], f"wz{d}"), (wdt_a[d], f"wdt_a{d}"),
                      (wdt_b[d], f"wdt_b{d}"), (wbc[d], f"wbc{d}"), (wo[d], f"wo{d}"), (dvec[d], f"dvec{d}")]

        with nc.Block() as block:
            @block.sync
            def _(sp_):
                for tile, name in LOADS:
                    src, dst = T[name], tile
                    idx = tuple(slice(None) for _ in tile.shape)
                    sp_.dma_start(dst[idx], src).then_inc(s_load, 16)
                sp_.wait_ge(s_w3, 1)
                sp_.dma_start(T["w3_scratch"], w3p[:, :, :]).then_inc(s_w3d, 16)
                sp_.wait_ge(s_w3d, 16)
                for k in range(6):
                    sp_.dma_start(w3x[16 * k:16 * k + 16, :, :],
                                  T["w3_scratch"][:, W_COMBOS[k], :].rearrange("(t c) n -> c t n", c=16))\
                       .then_inc(s_w3x, 16)

            @block.gpsimd
            def _(pool):
                pool.memset(half_pow[:, :], -0.5).then_inc(s_pool, 1)
                pool.memset(h1[:, :], 0.0).then_inc(s_pool, 1)
                pool.memset(xn[:, :], 0.0).then_inc(s_pool, 1)
                pool.memset(bc3[:, :, :], 0.0).then_inc(s_pool, 1)
                pool.wait_ge(s_pool, 1)
                pool.wait_ge(s_prep, 1)
                nc.gpsimd.tensor_tensor(bnv[:, :], bnv[:, :], half_pow[:, :], ALU.pow).then_inc(s_pool, 1)

            @block.scalar
            def _(act):
                act.wait_ge(s_load, 16 * len(LOADS))
                for d in range(2):
                    nc.scalar.activation(dvec[d][:, 3:3 + DS], dvec[d][:, 3:3 + DS], ACT.Exp).then_inc(s_act, 1)

            @block.vector
            def _(dve):
                step = [0]

                def then(ins):
                    step[0] += 1
                    ins.then_inc(s_prep, 1)
                    dve.wait_ge(s_prep, step[0])

                V = nc.vector
                dve.wait_ge(s_load, 16 * len(LOADS))
                then(V.tensor_scalar(bnv[:, :], bnv[:, :], BN_EPS, None, ALU.add))
                then(V.tensor_copy(identb[:, :], ident[:, :]))
                then(V.tensor_copy(pick[:, :, :], pick_small[:, :].unsqueeze(2).to_broadcast([128, 2 * DS, 128])))
                wide = [96, 3 * QUADS, 8, PD]
                then(V.tensor_tensor(w2[:, :, :].rearrange("p t (a b) -> p t a b", b=PD),
                                     w2c[:, :, :].unsqueeze(2).to_broadcast(wide),
                                     quad_mask[:, :].unsqueeze(1).unsqueeze(3).to_broadcast(wide), ALU.mult))
                dve.wait_ge(s_pool, 5)
                then(V.tensor_tensor(bng[:, :], bng[:, :], bnv[:, :], ALU.mult))
                then(V.tensor_tensor(w3c[:, :], w3c[:, :], bng[:, 18:82], ALU.mult))
                then(V.tensor_copy(w3p[:, 0, :], w3c[:, :]))
                then(V.tensor_tensor(w3c[:, :], w3c[:, :], w3p[:, 0, :], ALU.subtract))
                then(V.tensor_copy(w3p[:, 1, :], w3c[:, :]))
                then(V.tensor_tensor(w3c[:, :], w3c[:, :], w3p[:, 1, :], ALU.subtract))
                V.tensor_copy(w3p[:, 2, :], w3c[:, :]).then_inc(s_w3, 1)
                then(V.tensor_tensor(bnb[:, :], bnb[:, :], bnm[:, :], ALU.subtract))
                then(V.tensor_tensor(bnb[:, :], bnb[:, :], bng[:, 0:18], ALU.mult))
                then(V.tensor_tensor(bnb[:, :], bnb[:, :], bnbe[:, :], ALU.add))
                then(V.tensor_scalar(nb3[:, :], bnb[:, 2:18], -1.0, None, ALU.mult))
                then(V.reduce_sum(sum_b3[:, :], bnb[:, 2:18], axis=AX.X))
                for j in ACT_J:
                    then(V.tensor_tensor(sum_b3[:, :], sum_b3[:, :], bnb[:, 2 + j:3 + j], ALU.subtract))
                for d in range(2):
                    then(V.tensor_tensor(wx[d][:, :, :], wx[d][:, :, :], tapw[d][:, :, :], ALU.mult))
                dve.wait_ge(s_w3x, 16 * 6)
                wide = [96, ZT, 4, C]
                then(V.tensor_tensor(w3[:, :, :, :], w3x[:, :, :].unsqueeze(2).to_broadcast(wide),
                                     four_mask[:, :].unsqueeze(1).unsqueeze(3).to_broadcast(wide), ALU.mult))
                dve.wait_ge(s_act, 2)
                for d in range(2):
                    then(V.tensor_scalar(dvec[d][:, 3:3 + DS], dvec[d][:, 3:3 + DS], -1.0, None, ALU.mult))
                dve.wait_ge(s_pe, 1)
                for d in range(2):
                    then(V.tensor_copy(wdt[d][:, :], ps[d][:, 0:DI]))
                then(V.tensor_tensor(be1[:, :], be1[:, :], ps[2][:, 0:MT], ALU.add))
                for e in range(EX):
                    then(V.tensor_scalar(we1[:, 2 * e:2 * e + 2, :], we1[:, 2 * e:2 * e + 2, :],
                                         lng[:, e:e + 1], None, ALU.mult))
                then(V.tensor_copy(we1s[0][:, :, :], we1))
                then(V.tensor_tensor(we1r, we1, we1s[0][:, :, :], ALU.subtract))
                then(V.tensor_copy(we1s[1][:, :, :], we1r))
                then(V.tensor_tensor(we1r, we1r, we1s[1][:, :, :], ALU.subtract))
                then(V.tensor_copy(we1s[2][0:C, :, :], we1r[0:C]))
                then(V.tensor_copy(we1s[2][C:128, :, :], we1s[0][C:128, :, :]))
                then(V.tensor_copy(pick_w[:, :, :], pick_w_small[:, :].unsqueeze(2).to_broadcast([3 * EX, EX, C])))

            @block.tensor
            def _(pe):
                pe.wait_ge(s_load, 16 * len(LOADS))
                for d in range(2):
                    nc.tensor.matmul(ps[d][:, 0:DI], wdt_a[d][:, :], wdt_b[d][:, :], start=True, stop=True)
                for m in range(MT):
                    last = nc.tensor.matmul(ps[2][:, m:m + 1], we1[0:C, m, :], lnb[0:C, m // 2:m // 2 + 1],
                                            start=True, stop=True)
                last.then_inc(s_pe, 1)

        for s in sems:
            nc.gpsimd.sem_clear(s)
        nc.all_engine_barrier()

        x_in = sem("x_in")
        xT_ps, xT_sb = sem("xT_ps"), sem("xT_sb")
        h1_ps, h1_sb = sem("h1_ps"), sem("h1_sb")
        h2_ps, h2_p, h2_r = sem("h2_ps"), sem("h2_p"), sem("h2_r")
        slabbed = [sem("slabbed0"), sem("slabbed1")]
        bounced = [sem("bounced0"), sem("bounced1")]
        arranged = [sem("arranged0"), sem("arranged1")]
        z_ps, z_dve, z_act, z_T = sem("z_ps"), sem("z_dve"), sem("z_act"), sem("z_T")
        x1_ps, x1_out = sem("x1_ps"), sem("x1_out")
        a_ch, pw_req, pw_done = sem("a_ch"), sem("pw_req"), sem("pw_done")
        xn_tok, xn_ps, xn_sb = sem("xn_tok"), sem("xn_ps"), sem("xn_sb")
        b_ps, b_sb = sem("b_ps"), sem("b_sb")
        dt_ps, bc_ps, bc_tok, bcT_ps, bcT_sb = (sem(n) for n in ("dt_ps", "bc_ps", "bc_tok", "bcT_ps", "bcT_sb"))
        dt_x, dt_e, dt_y, dt_r, dt_l, dt_s, dt_ok, dtu_ok = (sem(n) for n in
            ("dt_x", "dt_e", "dt_y", "dt_r", "dt_l", "dt_s", "dt_ok", "dtu_ok"))
        bc_part, gated = sem("bc_part"), sem("gated")
        bb_ps, cb_ps, a_ok, cb_ok = sem("bb_ps"), sem("cb_ps"), sem("a_ok"), sem("cb_ok")
        bu_ok, h_ok, hc_ok, st_ok, y_acc = (sem(n) for n in ("bu_ok", "h_ok", "hc_ok", "st_ok", "y_acc"))
        y_tok, yT_ps, yz_ok, st0 = sem("y_tok"), sem("yT_ps"), sem("yz_ok"), sem("st0")
        o_ps, d_ch, d_tok, dT_ps, dT_sb, lg_ps, lg_ok = (sem(n) for n in
            ("o_ps", "d_ch", "d_tok", "dT_ps", "dT_sb", "lg_ps", "lg_ok"))
        dp_a, dp_r, o_rd = sem("dp_a"), sem("dp_r"), sem("o_rd")
        e_req, e_ok, w_ok = sem("e_req"), sem("e_ok"), sem("w_ok")
        wb_ps, wb_sb, up_ps, g_ok, dn, ye_dve, ye_T, o_sum, out_ok = (sem(n) for n in
            ("wb_ps", "wb_sb", "up_ps", "g_ok", "dn", "ye_dve", "ye_T", "o_sum", "out_ok"))
        stored = [sem("stored0"), sem("stored1")]
        loop_sems = sems[8:]

        def tile4(bank, n):
            return bank[0:TT, 0:KT * n].rearrange("p (k n) -> p k n", n=n)

        def bc_last(ap, n):
            return ap.unsqueeze(2).to_broadcast([ap.shape[0], ap.shape[1], n])

        def norm_sums(link, src, xc, i):
            norm_mean(link, src, i)
            norm_var(link, src, xc, i)

        def norm_mean(link, src, i):
            V, st = nc.vector, stat[:, i]
            link(V.reduce_sum(st[:, 0, :], src, axis=AX.X))
            link(V.tensor_scalar(st[:, 0, :], st[:, 0, :], 1.0 / C, None, ALU.mult))

        def norm_var(link, src, xc, i):
            V, st = nc.vector, stat[:, i]
            link(V.tensor_tensor(xc, src, bc_last(st[:, 0, :], C), ALU.subtract))
            link(V.tensor_tensor(tmp[:, 2], xc, xc, ALU.mult))
            link(V.reduce_sum(st[:, 5, :], tmp[:, 2], axis=AX.X))
            link(V.tensor_scalar(st[:, 5, :], st[:, 5, :], 1.0 / C, None, ALU.mult))
            V.tensor_scalar(st[:, 1, :], st[:, 5, :], LN_EPS, None, ALU.add).then_inc(pw_req, 1)

        def norm_again(dve, link, i, pw_n):
            V, st = nc.vector, stat[:, i]
            dve.wait_ge(pw_done, pw_n + 1)
            link(V.tensor_tensor(st[:, 3, :], st[:, 5, :], st[:, 2, :], ALU.mult))
            link(V.tensor_tensor(st[:, 3, :], st[:, 3, :], st[:, 2, :], ALU.mult))
            V.tensor_scalar(st[:, 3, :], st[:, 3, :], LN_EPS, None, ALU.add).then_inc(pw_req, 1)

        def linker(dve, s):
            count = [0]

            def link(ins):
                count[0] += 1
                ins.then_inc(s, 1)
                dve.wait_ge(s, count[0])
            return link

        def rev(ap, d):
            return ap[:, ::-1] if d else ap

        def chunk_of(k):
            return k // 2 if k % 2 == 0 else NCH - 1 - k // 2

        with nc.Fori(0, NB) as img:
            with nc.Block() as block:
                @block.sync
                def _(sp_):
                    def shift(c):
                        sp_.wait_ge(h1_sb, min(c + 2, NCH))
                        if c >= 2:
                            sp_.wait_ge(h2_ps, c - 1)
                        for dx in range(3):
                            at = c * ROWS * PW + dx
                            for q in range(QUADS):
                                sp_.dma_start(slab[c % 2][32 * dx:32 * dx + 32, q, :],
                                              h1[32 * q:32 * q + 32, at:at + SLAB]).then_inc(slabbed[c % 2], 16)

                    def put(c):
                        if c >= 2:
                            sp_.wait_ge(arranged[c % 2], 48 * (c // 2))
                        for a in range(3):
                            sp_.wait_ge(h2_p, 3 * c + a + 1)
                            sp_.dma_start(T["h2_scratch"][c % 2, a].rearrange("c t n -> t c n"), h2p[:, c % 2, a, :])\
                               .then_inc(bounced[c % 2], 16)

                    def arrange(c):
                        sp_.wait_ge(bounced[c % 2], 48 * (c // 2 + 1))
                        if c >= 2:
                            sp_.wait_ge(z_ps, ZP * (c - 1))
                        src = T["h2_scratch"][c % 2].rearrange("a c t n -> (a c) t n")
                        row = 0
                        for parts in (3, 2, 1):
                            sp_.dma_start(h3[c % 2][row:row + 16 * parts, :, :], src[0:16 * parts])\
                               .then_inc(arranged[c % 2], 16)
                            row += 16 * parts

                    sp_.dma_start(x_tok[:, :, :], x_dram[img]).then_inc(x_in, 16)
                    shift(0)
                    shift(1)
                    put(0)
                    arrange(0)
                    shift(2)
                    for c in range(NCH):
                        if c + 1 < NCH:
                            put(c + 1)
                            arrange(c + 1)
                        if c + 3 < NCH:
                            shift(c + 3)

                @block.gpsimd
                def _(pool):
                    for c in range(NCH):
                        i = c % 2
                        pool.wait_ge(pw_req, 2 * c + 1)
                        nc.gpsimd.tensor_tensor(stat[:, i, 2, :], stat[:, i, 1, :], half_pow[0:TT, 0:KT], ALU.pow)\
                            .then_inc(pw_done, 1)
                        pool.wait_ge(pw_req, 2 * c + 2)
                        nc.gpsimd.tensor_tensor(stat[:, i, 4, :], stat[:, i, 3, :], half_pow[0:TT, 0:KT], ALU.pow)\
                            .then_inc(pw_done, 1)

                @block.tensor
                def _(pe):
                    def first(c):
                        pe.wait_ge(x_in, 16)
                        if c:
                            pe.wait_ge(xT_sb, c)
                        if c >= 6:
                            pe.wait_ge(xn_sb, c - 5)
                        for k in range(KT):
                            last = nc.tensor.transpose(ps[0][0:C, k * TT:(k + 1) * TT], x_tok[:, c * KT + k, :],
                                                       ident[0:TT, 0:TT])
                        last.then_inc(xT_ps, 1)

                    def first_paths(c):
                        pe.wait_ge(xT_sb, c + 1)
                        if c:
                            pe.wait_ge(h1_sb, c)
                        nc.tensor.matmul(ps[1][:, 0:CH], w1[:, :], xT[:, c % 2, :], start=True, stop=True)\
                            .then_inc(h1_ps, 1)

                    def second(c):
                        pe.wait_ge(slabbed[c % 2], 16 * 3 * QUADS * (c // 2 + 1))
                        if c:
                            pe.wait_ge(h2_p, 3 * c - 2)
                        for dy in range(3):
                            for q in range(QUADS):
                                rows = slab[c % 2][:, q, dy * PW:(dy + ROWS) * PW]
                                last = nc.tensor.matmul(ps[2][32 * q:32 * q + 32, 0:CH], w2[:, dy * QUADS + q, :],
                                                        rows.rearrange("p (r w) -> p r w", w=PW)[:, :, 0:WW],
                                                        start=(dy == 0), stop=(dy == 2))
                        last.then_inc(h2_ps, 1)

                    def fold(c, m):
                        n = len(ACT_J)
                        if m < n:
                            src = rz[:, (c * n + m) % 4, :]
                            pe.wait_ge(z_act, c * n + m + 1)
                        else:
                            src = acc[:, c % 2, :]
                            pe.wait_ge(z_dve, (c + 1) * len(DVE_J))
                        if m == 0 and c:
                            pe.wait_ge(x1_out, c)
                        for k in range(KT):
                            last = nc.tensor.matmul(ps[3][0:TT, k * 128:(k + 1) * 128], src[:, k * TT:(k + 1) * TT],
                                                    ident[:, :], is_transpose=True, start=(m == 0 and k == 0),
                                                    stop=(m == n and k == KT - 1), skip_group_check=True)
                        last.then_inc(z_T, 1)

                    def third(c):
                        pe.wait_ge(arranged[c % 2], 48 * (c // 2 + 1))
                        m = 0
                        for j in range(ZP):
                            g = c * ZP + j - 4
                            if g >= 0:
                                cc, jj = g // ZP, g % ZP
                                if jj in ACT_J:
                                    pe.wait_ge(z_act, cc * len(ACT_J) + ACT_J.index(jj) + 1)
                                else:
                                    pe.wait_ge(z_dve, cc * len(DVE_J) + DVE_J.index(jj) + 1)
                            nc.tensor.matmul(ps[4 + j % 4][:, 0:CH],
                                             w3[:, j // 2, 2 * (j % 2):2 * (j % 2) + 2, :].rearrange("p a b -> p (a b)"),
                                             h3[c % 2][:, j // 2, :], start=True, stop=True).then_inc(z_ps, 1)
                            if j == 3 and c + 4 < NCH:
                                first_paths(c + 4)
                            if m < len(ACT_J) and j >= ACT_J[m] + 4:
                                fold(c, m)
                                m += 1
                        return m

                    def norm_T(c):
                        pe.wait_ge(xn_tok, c + 1)
                        pe.wait_ge(xT_sb, min(c + 6, NCH))
                        if c:
                            pe.wait_ge(xn_sb, c)
                        for k in range(KT):
                            last = nc.tensor.transpose(ps[0][0:C, k * TT:(k + 1) * TT], xnt[:, c % 2, k, 0, :],
                                                       ident[0:TT, 0:TT])
                        last.then_inc(xn_ps, 1)

                    for c in range(4):
                        first(c)
                        first_paths(c)
                    second(0)
                    second(1)
                    for c in range(NCH):
                        if c + 4 < NCH:
                            first(c + 4)
                        m = third(c)
                        if c + 2 < NCH:
                            second(c + 2)
                        for i in range(m, len(ACT_J) + 1):
                            fold(c, i)
                        if c:
                            norm_T(c - 1)
                    norm_T(NCH - 1)

                @block.scalar
                def _(act):
                    A = nc.scalar

                    def evac_x(c):
                        act.wait_ge(xT_ps, c + 1)
                        if c >= 2:
                            act.wait_ge(h1_ps, c - 1)
                        A.activation(xT[:, c % 2, :], ps[0][0:C, 0:CH], ACT.Copy).then_inc(xT_sb, 1)

                    def evac_h1(c):
                        act.wait_ge(h1_ps, c + 1)
                        A.activation(h1v[:, 1 + c * ROWS:1 + (c + 1) * ROWS, 1:1 + WW],
                                     ps[1][:, 0:CH].rearrange("p (r w) -> p r w", w=WW), ACT.Relu,
                                     bias=bnb[:, 0:1], scale=bng[:, 0:1]).then_inc(h1_sb, 1)

                    def evac_h2(c):
                        act.wait_ge(h2_ps, c + 1)
                        if c >= 2:
                            act.wait_ge(bounced[c % 2], 48 * (c // 2))
                        A.activation(h2[:, c % 2, :], ps[2][:, 0:CH], ACT.Relu,
                                     bias=bnb[:, 1:2], scale=bng[:, 1:2])
                        A.activation(h2p[:, c % 2, 0, :], ps[2][:, 0:CH], ACT.Relu,
                                     bias=bnb[:, 1:2], scale=bng[:, 1:2]).then_inc(h2_p, 1)

                    def part(c, i):
                        act.wait_ge(h2_r, 2 * c + i)
                        A.activation(h2p[:, c % 2, i, :], sp[:, i, :], ACT.Copy).then_inc(h2_p, 1)

                    def evac_xn(c):
                        act.wait_ge(xn_ps, c + 1)
                        t0 = c * CH
                        A.activation(xn[0:C, 3 + t0:3 + t0 + CH], ps[0][0:C, 0:CH], ACT.Identity,
                                     bias=gb[:, 1:2], scale=gb[:, 0:1])
                        A.activation(xn[C:128, 2 + t0:2 + t0 + CH], ps[0][0:C, 0:CH], ACT.Identity,
                                     bias=gb[:, 1:2], scale=gb[:, 0:1]).then_inc(xn_sb, 1)

                    def rectify(c, m):
                        n, j = len(ACT_J), ACT_J[m]
                        act.wait_ge(z_ps, c * ZP + j + 1)
                        gg = c * n + m - 4
                        if gg >= 0:
                            act.wait_ge(z_T, (gg // n) * (n + 1) + gg % n + 1)
                        A.activation(rz[:, (c * n + m) % 4, :], ps[4 + j % 4][:, 0:CH], ACT.Relu,
                                     bias=bnb[:, 2 + j:3 + j]).then_inc(z_act, 1)

                    for c in range(4):
                        evac_x(c)
                        evac_h1(c)
                    evac_h2(0)
                    part(0, 1)
                    part(0, 2)
                    evac_h2(1)
                    for c in range(NCH):
                        more = c + 1 < NCH
                        if c + 4 < NCH:
                            evac_x(c + 4)
                        rectify(c, 0)
                        if more:
                            part(c + 1, 1)
                        if c + 4 < NCH:
                            evac_h1(c + 4)
                        rectify(c, 1)
                        rectify(c, 2)
                        if more:
                            part(c + 1, 2)
                        rectify(c, 3)
                        rectify(c, 4)
                        rectify(c, 5)
                        if c + 2 < NCH:
                            evac_h2(c + 2)
                        if c:
                            evac_xn(c - 1)
                    evac_xn(NCH - 1)

                @block.vector
                def _(dve):
                    V = nc.vector
                    link = linker(dve, a_ch)

                    def rectify(c, m):
                        j, a = DVE_J[m], acc[:, c % 2, :]
                        z = ps[4 + j % 4][:, 0:CH]
                        if m == 0 and c >= 2:
                            dve.wait_ge(z_T, (len(ACT_J) + 1) * (c - 1))
                        dve.wait_ge(z_ps, c * ZP + j + 1)
                        if m:
                            dve.wait_ge(z_dve, c * len(DVE_J) + m)
                            V.scalar_tensor_tensor(a, z, nb3[:, j:j + 1], a, ALU.max, ALU.add).then_inc(z_dve, 1)
                        else:
                            V.tensor_scalar(a, z, nb3[:, j:j + 1], sum_b3[:, 0:1], ALU.max, ALU.add)\
                                .then_inc(z_dve, 1)

                    def remainder(c, i):
                        dve.wait_ge(h2_p, 3 * c + i)
                        if i == 1 and c:
                            dve.wait_ge(h2_p, 3 * c)
                        src = h2[:, c % 2, :] if i == 1 else sp[:, 1, :]
                        V.tensor_tensor(sp[:, i, :], src, h2p[:, c % 2, i - 1, :], ALU.subtract).then_inc(h2_r, 1)

                    def paths_out(c):
                        n0 = c * KT
                        b3 = tile4(ps[3], 128)
                        dve.wait_ge(z_T, (len(ACT_J) + 1) * (c + 1))
                        link(V.tensor_tensor(tmp[:, 0], b3[:, :, 0:C], x_tok[:, n0:n0 + KT, :], ALU.add))
                        V.tensor_tensor(tmp[:, 1], b3[:, :, C:128], tmp[:, 0], ALU.add).then_inc(x1_out, 1)
                        dve.wait_ge(x1_out, c + 1)
                        link(V.tensor_scalar(res[:, n0:n0 + KT, :], tmp[:, 1], 0.0, None, ALU.max))

                    def tokens_out(c):
                        r, st = res[:, c * KT:(c + 1) * KT, :], stat[:, c % 2]
                        link(V.tensor_tensor(tmp[:, 1], tmp[:, 0], bc_last(st[:, 2, :], C), ALU.mult))
                        V.tensor_tensor(r, r, tmp[:, 1], ALU.add)
                        dve.wait_ge(pw_done, 2 * c + 2)
                        if c >= 2:
                            dve.wait_ge(xn_ps, c - 1)
                        V.tensor_tensor(xnt[:, c % 2, :, 0, :], tmp[:, 1], bc_last(st[:, 4, :], C), ALU.mult)\
                            .then_inc(xn_tok, 1)

                    remainder(0, 1)
                    remainder(0, 2)
                    for c in range(NCH + 1):
                        here, more, behind = c < NCH, c + 1 < NCH, c > 0
                        if more:
                            remainder(c + 1, 1)
                        if here:
                            rectify(c, 0)
                            rectify(c, 1)
                        if behind:
                            paths_out(c - 1)
                        if here:
                            rectify(c, 2)
                            rectify(c, 3)
                        if more:
                            remainder(c + 1, 2)
                        if here:
                            rectify(c, 4)
                        if behind:
                            norm_sums(link, res[:, (c - 1) * KT:c * KT, :], tmp[:, 0], (c - 1) % 2)
                        if here:
                            rectify(c, 5)
                            rectify(c, 6)
                        if behind:
                            norm_again(dve, link, (c - 1) % 2, 2 * (c - 1))
                        if here:
                            rectify(c, 7)
                            rectify(c, 8)
                        if behind:
                            tokens_out(c - 1)
                        if here:
                            rectify(c, 9)

            with nc.Block() as block:
                @block.tensor
                def _(pe):
                    for i in range(2 * STEPS):
                        c, d, z = i // 4, (i // 2) % 2, i % 2
                        t0 = c * CH
                        if i >= 8:
                            pe.wait_ge(b_sb, i - 7)
                        bank = ps[i % 8][:, 0:CH]
                        if z:
                            nc.tensor.matmul(bank, wz[d][:, :], xn[0:C, t0 + 3:t0 + 3 + CH], start=True, stop=True)\
                                .then_inc(b_ps, 1)
                        else:
                            at = t0 + 3 * d
                            nc.tensor.matmul(bank, wx[d][:, 0, :], xn[:, at:at + CH], start=True, stop=False)
                            nc.tensor.matmul(bank, wx[d][:, 1, :], xn[:, at + 2:at + 2 + CH], start=False, stop=True)\
                                .then_inc(b_ps, 1)

                @block.scalar
                def _(act):
                    for i in range(2 * STEPS):
                        c, d, z = i // 4, (i // 2) % 2, i % 2
                        act.wait_ge(b_ps, i + 1)
                        if z:
                            nc.scalar.activation(zs[d][:, c * CH:(c + 1) * CH], ps[i % 8][:, 0:CH], ACT.Silu)\
                                .then_inc(b_sb, 1)
                        else:
                            nc.scalar.activation(u[d][:, c * CH:(c + 1) * CH], ps[i % 8][:, 0:CH], ACT.Silu,
                                                 bias=dvec[d][:, 0:1]).then_inc(b_sb, 1)

            def ucols(k):
                c = chunk_of(k)
                return u[k % 2][:, c * CH:(c + 1) * CH]

            PREP_AT, POST_AT = 5, 3

            with nc.Block() as block:
                @block.tensor
                def _(pe):
                    def prep_dt(k):
                        d = k % 2
                        if k >= 2:
                            pe.wait_ge(yz_ok, k - 1)
                        nc.tensor.matmul(ps[0][:, 0:CH], wdt[d][:, :], ucols(k), start=True, stop=True)\
                            .then_inc(dt_ps, 1)

                    def prep_bc(k):
                        d, c = k % 2, chunk_of(k)
                        if k:
                            pe.wait_ge(bcT_sb, k)
                        for j in range(KT):
                            last = nc.tensor.matmul(ps[1][0:TT, 32 * j:32 * j + 32],
                                                    u[d][:, c * CH + j * TT:c * CH + (j + 1) * TT], wbc[d][:, :],
                                                    start=True, stop=True)
                        last.then_inc(bc_ps, 1)

                    def prep_T(k):
                        pe.wait_ge(bc_tok, k + 1)
                        out = ps[1][0:96, 0:CH // 2].bitcast(BF16)
                        for j in range(KT):
                            last = nc.tensor.transpose(out[:, j * TT:(j + 1) * TT],
                                                       bct[:, j].rearrange("p a b -> p (a b)"), identb[0:TT, 0:TT])
                        last.then_inc(bcT_ps, 1)

                    def fold(g):
                        k, s = g // DS, g % DS
                        pe.wait_ge(hc_ok, g + 1)
                        if s == 0 and k >= 2:
                            pe.wait_ge(y_tok, k - 1)
                        bank = ps[2 if k % 2 == 0 else 7]
                        for j in range(KT):
                            last = nc.tensor.matmul(bank[0:TT, j * 128:(j + 1) * 128],
                                                    hc[:, g % 3, j * TT:(j + 1) * TT], ident[:, :], is_transpose=True,
                                                    start=(s == 0 and j == 0), stop=(s == DS - 1 and j == KT - 1),
                                                    skip_group_check=True)
                        last.then_inc(y_acc, 1)

                    def post(k):
                        pe.wait_ge(y_tok, k + 1)
                        if k + 1 < STEPS:
                            pe.wait_ge(dt_ok, k + 2)
                        for j in range(KT):
                            last = nc.tensor.transpose(ps[0][:, j * TT:(j + 1) * TT], ytok[:, j * 128:(j + 1) * 128],
                                                       ident[0:TT, 0:TT])
                        last.then_inc(yT_ps, 1)

                    prep_dt(0)
                    prep_bc(0)
                    prep_T(0)
                    G = STEPS * DS
                    for g in range(G):
                        k, s = g // DS, g % DS
                        if s == 0:
                            pe.wait_ge(bcT_sb, k + 1)
                        if g >= 2:
                            pe.wait_ge(bu_ok, g - 1)
                            pe.wait_ge(cb_ok, g - 1)
                        nc.tensor.matmul(ps[3 + g % 2][:, 0:CH], pick[:, s, :], bc3[:, k % 2, :], start=True, stop=True)\
                            .then_inc(bb_ps, 1)
                        nc.tensor.matmul(ps[5 + g % 2][:, 0:CH], pick[:, DS + s, :], bc3[:, k % 2, :],
                                         start=True, stop=True).then_inc(cb_ps, 1)
                        if g >= 3:
                            fold(g - 3)
                        if s == POST_AT + 1 and k:
                            post(k - 1)
                        if s == 7 and k + 1 < STEPS:
                            prep_dt(k + 1)
                        if s == 8 and k + 1 < STEPS:
                            prep_bc(k + 1)
                        if s == 12 and k + 1 < STEPS:
                            prep_T(k + 1)
                    for g in range(G - 3, G):
                        fold(g)
                    post(STEPS - 1)

                @block.scalar
                def _(act):
                    A = nc.scalar
                    A.preload_act_table_set("natural_log_exp_and_others")

                    def soft_exp(k):
                        act.wait_ge(dt_x, k + 1)
                        A.activation(sp[:, 1, :], sp[:, 0, :], ACT.Exp).then_inc(dt_e, 1)

                    def soft_ln(k):
                        act.wait_ge(dt_y, k + 1)
                        A.activation(sp[:, 3, :], sp[:, 2, :], ACT.Ln).then_inc(dt_l, 1)

                    def copy_bc(k):
                        act.wait_ge(bcT_ps, k + 1)
                        A.activation(bc3[0:96, k % 2, :], ps[1][0:96, 0:CH // 2].bitcast(BF16), ACT.Copy)\
                            .then_inc(bcT_sb, 1)

                    soft_exp(0)
                    soft_ln(0)
                    copy_bc(0)
                    G = STEPS * DS
                    for g in range(G):
                        k, s = g // DS, g % DS
                        if s == 0:
                            act.wait_ge(dt_ok, k + 1)
                        if g >= 3:
                            act.wait_ge(h_ok, g - 2)
                        A.activation(dA[:, g % 3, :], dtv[:, k % 2, :], ACT.Exp, scale=dvec[k % 2][:, 3 + s:4 + s])\
                            .then_inc(a_ok, 1)
                        act.wait_ge(cb_ps, g + 1)
                        if g >= 3:
                            act.wait_ge(hc_ok, g - 2)
                        A.activation(cb[:, g % 3, :], ps[5 + g % 2][:, 0:CH], ACT.Copy).then_inc(cb_ok, 1)
                        if s == POST_AT and k:
                            act.wait_ge(y_acc, DS * k)
                            A.activation(ytok[:, :], ps[2 if (k - 1) % 2 == 0 else 7][0:TT, :], ACT.Copy)\
                                .then_inc(y_tok, 1)
                        if k + 1 < STEPS:
                            if s == 10:
                                soft_exp(k + 1)
                            if s == 12:
                                soft_ln(k + 1)
                            if s == 13:
                                copy_bc(k + 1)
                    act.wait_ge(y_acc, G)
                    A.activation(ytok[:, :], ps[2 if (STEPS - 1) % 2 == 0 else 7][0:TT, :], ACT.Copy)\
                        .then_inc(y_tok, 1)

                @block.vector
                def _(dve):
                    V = nc.vector

                    def soft_x(k):
                        dve.wait_ge(dt_ps, k + 1)
                        if k >= 2:
                            dve.wait_ge(gated, k - 1)
                        V.tensor_scalar(sp[:, 0, :], ps[0][:, 0:CH], dvec[k % 2][:, 1:2], DT_CLAMP, ALU.add, ALU.min)\
                            .then_inc(dt_x, 1)

                    def soft_y(k):
                        dve.wait_ge(dt_e, k + 1)
                        V.tensor_scalar(sp[:, 2, :], sp[:, 1, :], 1.0, None, ALU.add).then_inc(dt_y, 1)

                    def soft_rest(k):
                        dve.wait_ge(dt_y, k + 1)
                        V.scalar_tensor_tensor(sp[:, 1, :], sp[:, 2, :], -1.0, sp[:, 1, :], ALU.add, ALU.subtract)\
                            .then_inc(dt_r, 1)

                    def soft_sub(k):
                        dve.wait_ge(dt_l, k + 1)
                        dve.wait_ge(dt_r, k + 1)
                        V.tensor_tensor(sp[:, 3, :], sp[:, 3, :], sp[:, 1, :], ALU.subtract).then_inc(dt_s, 1)

                    def soft_max(k):
                        dve.wait_ge(dt_s, k + 1)
                        V.scalar_tensor_tensor(dtv[:, k % 2, :], ps[0][:, 0:CH], dvec[k % 2][:, 1:2], sp[:, 3, :],
                                               ALU.add, ALU.max).then_inc(dt_ok, 1)

                    def soft_u(k):
                        dve.wait_ge(dt_ok, k + 1)
                        V.tensor_tensor(dtu[:, k % 2, :], dtv[:, k % 2, :], ucols(k), ALU.mult).then_inc(dtu_ok, 1)

                    def split_bc(k, i):
                        if i == 0:
                            dve.wait_ge(bc_ps, k + 1)
                            if k:
                                dve.wait_ge(bcT_ps, k)
                        else:
                            dve.wait_ge(bc_part, 4 * k + i)
                        src = tile4(ps[1], 2 * DS)
                        if i == 0:
                            V.tensor_copy(bct[:, :, 0, :], src).then_inc(bc_part, 1)
                        elif i == 1:
                            V.tensor_tensor(bcr[:, :, :], src, bct[:, :, 0, :], ALU.subtract).then_inc(bc_part, 1)
                        elif i == 2:
                            V.tensor_copy(bct[:, :, 1, :], bcr[:, :, :]).then_inc(bc_part, 1)
                        elif i == 3:
                            V.tensor_tensor(bcr[:, :, :], bcr[:, :, :], bct[:, :, 1, :], ALU.subtract)\
                                .then_inc(bc_part, 1)
                        else:
                            V.tensor_copy(bct[:, :, 2, :], bcr[:, :, :]).then_inc(bc_tok, 1)

                    def y_plus_ud(k):
                        dve.wait_ge(yT_ps, k + 1)
                        V.scalar_tensor_tensor(sp[:, 0, :], ucols(k), dvec[k % 2][:, 2:3], ps[0][:, 0:CH],
                                               ALU.mult, ALU.add).then_inc(yz_ok, 1)

                    def bu(g):
                        k = g // DS
                        dve.wait_ge(bb_ps, g + 1)
                        if g % DS == 0:
                            dve.wait_ge(dtu_ok, k + 1)
                        if g >= 3:
                            dve.wait_ge(h_ok, g - 2)
                        V.tensor_tensor(dBu[:, g % 3, :], ps[3 + g % 2][:, 0:CH], dtu[:, k % 2, :], ALU.mult)\
                            .then_inc(bu_ok, 1)

                    def scan(g):
                        s, d = g % DS, (g // DS) % 2
                        dve.wait_ge(bu_ok, g + 1)
                        dve.wait_ge(a_ok, g + 1)
                        if g >= 3:
                            dve.wait_ge(hc_ok, g - 2)
                        if g >= 2 * DS:
                            dve.wait_ge(st_ok, g - 2 * DS + 1)
                        V.tensor_tensor_scan(rev(hs[:, g % 3, :], d), rev(dA[:, g % 3, :], d), rev(dBu[:, g % 3, :], d),
                                             state[:, d, s:s + 1], ALU.mult, ALU.add).then_inc(h_ok, 1)

                    BEFORE = {7: lambda k: soft_x(k), 8: lambda k: split_bc(k, 0), 9: lambda k: split_bc(k, 2),
                              10: lambda k: soft_rest(k), 11: lambda k: soft_sub(k), 12: lambda k: soft_max(k),
                              13: lambda k: soft_u(k)}
                    AFTER = {8: lambda k: split_bc(k, 1), 9: lambda k: split_bc(k, 3), 10: lambda k: split_bc(k, 4)}
                    BETWEEN = {9: lambda k: soft_y(k)}

                    V.memset(state[:, :, :], 0.0).then_inc(st0, 1)
                    dve.wait_ge(st0, 1)
                    soft_x(0)
                    for i in range(5):
                        split_bc(0, i)
                    soft_y(0)
                    soft_rest(0)
                    soft_sub(0)
                    soft_max(0)
                    soft_u(0)
                    G = STEPS * DS
                    bu(0)
                    for g in range(G):
                        k, s = g // DS, g % DS
                        if g + 1 < G:
                            bu(g + 1)
                        if s == POST_AT + 2 and k:
                            y_plus_ud(k - 1)
                        if k + 1 < STEPS and s in BEFORE:
                            BEFORE[s](k + 1)
                        scan(g)
                        if k + 1 < STEPS and s in AFTER:
                            AFTER[s](k + 1)
                            if s in BETWEEN:
                                BETWEEN[s](k + 1)
                    y_plus_ud(STEPS - 1)

                @block.gpsimd
                def _(pool):
                    P = nc.gpsimd
                    G = STEPS * DS

                    def gate(k):
                        c = chunk_of(k)
                        z = zs[k % 2][:, c * CH:(c + 1) * CH]
                        pool.wait_ge(yz_ok, k + 1)
                        P.tensor_tensor(z, z, sp[:, 0, :], ALU.mult).then_inc(gated, 1)

                    for g in range(G):
                        k, s, d = g // DS, g % DS, (g // DS) % 2
                        pool.wait_ge(h_ok, g + 1)
                        at = 0 if d else CH - 1
                        P.tensor_copy(state[:, d, s:s + 1], hs[:, g % 3, at:at + 1]).then_inc(st_ok, 1)
                        pool.wait_ge(cb_ok, g + 1)
                        if g >= 3:
                            pool.wait_ge(y_acc, g - 2)
                        P.tensor_tensor(hc[:, g % 3, :], hs[:, g % 3, :], cb[:, g % 3, :], ALU.mult).then_inc(hc_ok, 1)
                        if s == POST_AT + 2 and k:
                            gate(k - 1)
                    gate(STEPS - 1)

            with nc.Block() as block:
                @block.tensor
                def _(pe):
                    def outp(c):
                        if c >= 4:
                            pe.wait_ge(o_rd, c - 3)
                        for j in range(KT):
                            t0 = c * CH + j * TT
                            for d in range(2):
                                last = nc.tensor.matmul(ps[4 + c % 4][0:TT, j * C:(j + 1) * C], zs[d][:, t0:t0 + TT],
                                                        wo[d][:, :], start=(d == 0), stop=(d == 1))
                        last.then_inc(o_ps, 1)

                    def tokens_T(c):
                        pe.wait_ge(d_tok, c + 1)
                        if c:
                            pe.wait_ge(dT_sb, c)
                            pe.wait_ge(dp_r, 2 * c - 1)
                        for j in range(KT):
                            last = nc.tensor.transpose(ps[2][:, j * TT:(j + 1) * TT],
                                                       xnt[:, c % 2, j].rearrange("p a b -> p (a b)"),
                                                       ident[0:TT, 0:TT])
                        last.then_inc(dT_ps, 1)

                    def logits(c):
                        pe.wait_ge(dT_sb, c + 1)
                        for j in range(KT):
                            last = nc.tensor.matmul(ps[3][0:TT, (c * KT + j) * EX:(c * KT + j + 1) * EX],
                                                    xn32[:, c % 2, j * TT:(j + 1) * TT], wr[:, :],
                                                    start=True, stop=True)
                        last.then_inc(lg_ps, 1)

                    for c in range(3):
                        outp(c)
                    for c in range(NCH):
                        tokens_T(c)
                        if c + 3 < NCH:
                            outp(c + 3)
                        logits(c)

                @block.scalar
                def _(act):
                    for c in range(NCH):
                        act.wait_ge(dT_ps, c + 1)
                        A = nc.scalar
                        cols = slice(c * CH, (c + 1) * CH)
                        A.activation(tok_parts[:, 0, cols], ps[2][:, 0:CH], ACT.Copy).then_inc(dp_a, 1)
                        A.activation(tok_parts[0:C, 1, cols], ps[2][0:C, 0:CH], ACT.Copy)
                        if c >= 2:
                            act.wait_ge(lg_ps, c - 1)
                        A.activation(xn32[:, c % 2, :], ps[2][0:C, 0:CH], ACT.Copy).then_inc(dT_sb, 1)
                        act.wait_ge(dp_r, 2 * c + 1)
                        A.activation(tok_parts[C:128, 0, cols], hc[C:128, 0, :], ACT.Copy).then_inc(dp_a, 1)
                        act.wait_ge(dp_r, 2 * c + 2)
                        A.activation(tok_parts[C:128, 1, cols], hc[C:128, 1, :], ACT.Copy).then_inc(dp_a, 1)
                    act.wait_ge(e_req, 1)
                    nc.scalar.activation(l1[:, 4, :], l1[:, 3, :], ACT.Exp).then_inc(e_ok, 1)

                @block.gpsimd
                def _(pool):
                    for c in range(NCH):
                        i = c % 2
                        pool.wait_ge(pw_req, 2 * NCH + 2 * c + 1)
                        nc.gpsimd.tensor_tensor(stat[:, i, 2, :], stat[:, i, 1, :], half_pow[0:TT, 0:KT], ALU.pow)\
                            .then_inc(pw_done, 1)
                        pool.wait_ge(pw_req, 2 * NCH + 2 * c + 2)
                        nc.gpsimd.tensor_tensor(stat[:, i, 4, :], stat[:, i, 3, :], half_pow[0:TT, 0:KT], ALU.pow)\
                            .then_inc(pw_done, 1)

                @block.vector
                def _(dve):
                    V = nc.vector
                    link = linker(dve, d_ch)

                    def residual(c):
                        r = res[:, c * KT:(c + 1) * KT, :]
                        dve.wait_ge(o_ps, c + 1)
                        V.tensor_tensor(r, tile4(ps[4 + c % 4], C), r, ALU.add).then_inc(o_rd, 1)
                        dve.wait_ge(o_rd, c + 1)
                        norm_mean(link, r, c % 2)

                    def normalised(c):
                        link(V.tensor_tensor(tmp[:, 1], tmp[:, 0], bc_last(stat[:, c % 2, 2, :], C), ALU.mult))

                    def tokens(c):
                        st = stat[:, c % 2]
                        dve.wait_ge(pw_done, 2 * NCH + 2 * c + 2)
                        if c >= 2:
                            dve.wait_ge(dT_ps, c - 1)
                        V.tensor_tensor(xnt[:, c % 2, :, 0, :], tmp[:, 1], bc_last(st[:, 4, :], C), ALU.mult)
                        V.tensor_tensor(xnt[:, c % 2, :, 1, :], tmp[:, 1], bc_last(st[:, 4, :], C), ALU.mult)\
                            .then_inc(d_tok, 1)
                        link(V.tensor_tensor(sq2[:, c * KT:(c + 1) * KT], st[:, 3, :], st[:, 4, :], ALU.mult))

                    def remainder_hi(c):
                        cols = slice(c * CH, (c + 1) * CH)
                        if c:
                            dve.wait_ge(dp_a, 3 * c)
                        dve.wait_ge(dp_a, 3 * c + 1)
                        V.tensor_tensor(hc[C:128, 0, :], ps[2][C:128, 0:CH], tok_parts[C:128, 0, cols], ALU.subtract)\
                            .then_inc(dp_r, 1)

                    def remainder_mid(c):
                        cols = slice(c * CH, (c + 1) * CH)
                        dve.wait_ge(dp_r, 2 * c + 1)
                        dve.wait_ge(dp_a, 3 * c + 2)
                        V.tensor_tensor(hc[C:128, 1, :], hc[C:128, 0, :], tok_parts[C:128, 0, cols], ALU.subtract)\
                            .then_inc(dp_r, 1)

                    for c in range(NCH + 2):
                        if c < NCH:
                            residual(c)
                        if 0 < c <= NCH:
                            norm_again(dve, link, (c - 1) % 2, 2 * NCH + 2 * (c - 1))
                            normalised(c - 1)
                        if c >= 2:
                            remainder_hi(c - 2)
                        if c < NCH:
                            norm_var(link, res[:, c * KT:(c + 1) * KT, :], tmp[:, 0], c % 2)
                        if c >= 2:
                            remainder_mid(c - 2)
                        if 0 < c <= NCH:
                            tokens(c - 1)
                    dve.wait_ge(lg_ps, NCH)
                    L, eq, cand, s1, s2, t8 = (lg[:, i] for i in range(6))
                    rk = rank8[:, :].unsqueeze(1).to_broadcast([TT, NT, EX])
                    link(V.tensor_tensor(L, ps[3][0:TT, 0:NT * EX].rearrange("p (n e) -> p n e", e=EX),
                                         bc_last(sq2[:, :], EX), ALU.mult))
                    link(V.tensor_tensor(L, L, br[:, :].unsqueeze(1).to_broadcast([TT, NT, EX]), ALU.add))

                    def top(src, sel, m):
                        link(V.reduce_max(m, src, axis=AX.X))
                        link(V.tensor_tensor(eq, src, bc_last(m, EX), ALU.is_equal))
                        link(V.tensor_tensor(cand, eq, rk, ALU.mult))
                        link(V.reduce_max(l1[:, 7, :], cand, axis=AX.X))
                        link(V.tensor_tensor(sel, rk, bc_last(l1[:, 7, :], EX), ALU.is_equal))

                    top(L, s1, l1[:, 0, :])
                    link(V.scalar_tensor_tensor(t8, s1, -FAR, L, ALU.mult, ALU.add))
                    top(t8, s2, l1[:, 1, :])
                    V.tensor_tensor(l1[:, 3, :], l1[:, 1, :], l1[:, 0, :], ALU.subtract).then_inc(e_req, 1)
                    dve.wait_ge(e_ok, 1)
                    link(V.tensor_scalar(l1[:, 5, :], l1[:, 4, :], 1.0, None, ALU.add))
                    link(V.reciprocal(l1[:, 5, :], l1[:, 5, :]))
                    link(V.tensor_tensor(l1[:, 6, :], l1[:, 4, :], l1[:, 5, :], ALU.mult))
                    link(V.tensor_tensor(s1, s1, bc_last(l1[:, 5, :], EX), ALU.mult))
                    link(V.tensor_tensor(s2, s2, bc_last(l1[:, 6, :], EX), ALU.mult))
                    link(V.tensor_tensor(wgt[:, :, :], s1, s2, ALU.add))
                    link(V.tensor_copy(wgt3[:, :, 0, :], wgt[:, :, :]))
                    link(V.tensor_tensor(wgt[:, :, :], wgt[:, :, :], wgt3[:, :, 0, :], ALU.subtract))
                    link(V.tensor_copy(wgt3[:, :, 1, :], wgt[:, :, :]))
                    link(V.tensor_tensor(wgt[:, :, :], wgt[:, :, :], wgt3[:, :, 1, :], ALU.subtract))
                    link(V.tensor_copy(wgt3[:, :, 2, :], wgt[:, :, :]))

            ORDER = [4 * p + 2 * (i % 2) + i // 2 for p in range(EX // 2) for i in range(4)]
            PAIRS = EX // 2
            with nc.Block() as block:
                G = NCH * MT

                @block.tensor
                def _(pe):
                    def up(g):
                        c, m = g // MT, ORDER[g % MT]
                        if g >= 3:
                            pe.wait_ge(g_ok, g - 2)
                        for i in range(3):
                            last = nc.tensor.matmul(ps[g % 3][:, 0:CH], we1s[i][:, m, :],
                                                    tok_parts[:, i // 2, c * CH:(c + 1) * CH],
                                                    start=(i == 0), stop=(i == 2))
                        last.then_inc(up_ps, 1)

                    def down(g):
                        P = g // 4
                        pe.wait_ge(g_ok, g + 2)
                        if g % 4 == 0 and P >= 2:
                            pe.wait_ge(ye_dve, P - 1)
                        for i in range(2):
                            m = ORDER[(g + i) % MT]
                            last = nc.tensor.matmul(ps[3 + P % 2][C * i:C * i + C, 0:CH], we2[:, m, :],
                                                    hg[:, (g + i) % 4, :], start=(g % 4 == 0), stop=(g % 4 == 2))
                        last.then_inc(dn, 1)

                    def weights(c, i):
                        q = c * (PAIRS + 1) + i
                        if q >= 2:
                            pe.wait_ge(wb_sb, q - 1)
                        bank = ps[5 + q % 2]
                        if i == 0:
                            out = bank[0:3 * EX, 0:CH // 2].bitcast(BF16)
                            for j in range(KT):
                                last = nc.tensor.transpose(out[:, j * TT:(j + 1) * TT],
                                                           wgt3[:, c * KT + j].rearrange("p a b -> p (a b)"),
                                                           identb[0:TT, 0:TT])
                        else:
                            pe.wait_ge(wb_sb, c * (PAIRS + 1) + 1)
                            last = nc.tensor.matmul(bank[:, 0:CH],
                                                    pick_w[:, 2 * i - 2:2 * i, :].rearrange("p a b -> p (a b)"),
                                                    wT[:, c % 2, :], start=True, stop=True)
                        last.then_inc(wb_ps, 1)

                    def fold(P):
                        p, c = P % PAIRS, P // PAIRS
                        pe.wait_ge(ye_dve, P + 1)
                        if p == 0 and c:
                            pe.wait_ge(o_sum, c)
                        for j in range(KT):
                            last = nc.tensor.matmul(ps[7][0:TT, j * 128:(j + 1) * 128],
                                                    yw[:, P % 3, j * TT:(j + 1) * TT], ident[:, :], is_transpose=True,
                                                    start=(p == 0 and j == 0), stop=(p == PAIRS - 1 and j == KT - 1),
                                                    skip_group_check=True)
                        last.then_inc(ye_T, 1)

                    up(0)
                    up(1)
                    up(2)
                    for g in range(0, G, 2):
                        c, m = g // MT, g % MT
                        if m == 0:
                            weights(c, 0)
                        if m % 4 == 0:
                            weights(c, m // 4 + 1)
                        down(g)
                        if g + 3 < G:
                            up(g + 3)
                        if m % 4 == 2 and g >= 4:
                            fold(g // 4 - 1)
                        if g + 4 < G:
                            up(g + 4)
                    fold(G // 4 - 1)

                @block.scalar
                def _(act):
                    def copy_w(c, i):
                        q = c * (PAIRS + 1) + i
                        act.wait_ge(wb_ps, q + 1)
                        if i == 0:
                            A.activation(wT[:, c % 2, :], ps[5 + q % 2][0:3 * EX, 0:CH // 2].bitcast(BF16), ACT.Copy)\
                                .then_inc(wb_sb, 1)
                        else:
                            P = c * PAIRS + i - 1
                            if P >= 3:
                                act.wait_ge(ye_dve, P - 2)
                            A.activation(wb[:, P % 3, :], ps[5 + q % 2][:, 0:CH], ACT.Copy).then_inc(wb_sb, 1)

                    A = nc.scalar
                    for g in range(G):
                        c, m = g // MT, ORDER[g % MT]
                        act.wait_ge(up_ps, g + 1)
                        if g >= 4:
                            act.wait_ge(dn, (g - 4) // 2 + 1)
                        A.activation(hg[:, g % 4, :], ps[g % 3][:, 0:CH], ACT.Gelu, bias=be1[:, m:m + 1])\
                            .then_inc(g_ok, 1)
                        if g % MT == 0:
                            copy_w(c, 0)
                        if g % 4 == 1:
                            copy_w(c, g % MT // 4 + 1)

                @block.vector
                def _(dve):
                    V = nc.vector

                    def finish(c):
                        dve.wait_ge(ye_T, PAIRS * (c + 1))
                        if c >= 2:
                            dve.wait_ge(stored[c % 2], 16 * (c // 2))
                        ob, b7 = outb[:, c % 2], tile4(ps[7], 128)
                        V.tensor_tensor(tmp[:, 0], b7[:, :, 0:C], res[:, c * KT:(c + 1) * KT, :], ALU.add)\
                            .then_inc(w_ok, 1)
                        dve.wait_ge(w_ok, c + 1)
                        V.tensor_tensor(ob, b7[:, :, C:128], tmp[:, 0], ALU.add).then_inc(o_sum, 1)

                    for P in range(NCH * PAIRS):
                        c, p = P // PAIRS, P % PAIRS
                        dve.wait_ge(dn, 2 * P + 2)
                        dve.wait_ge(wb_sb, c * (PAIRS + 1) + p + 2)
                        if P >= 3:
                            dve.wait_ge(ye_T, P - 2)
                        V.scalar_tensor_tensor(yw[:, P % 3, :], ps[3 + P % 2][:, 0:CH], be2[:, p:p + 1],
                                               wb[:, P % 3, :], ALU.add, ALU.mult).then_inc(ye_dve, 1)
                        if p == 1 and c:
                            finish(c - 1)
                    finish(NCH - 1)

                @block.sync
                def _(sp_):
                    for c in range(NCH):
                        sp_.wait_ge(o_sum, c + 1)
                        if c >= 2:
                            sp_.wait_ge(stored[c % 2], 16 * (c // 2))
                        sp_.dma_start(o_dram[img][:, c * KT:(c + 1) * KT, :], outb[:, c % 2])\
                            .then_inc(stored[c % 2], 16)
                    for i in range(2):
                        sp_.wait_ge(stored[i], 16 * ((NCH + 1 - i) // 2))

            for s in loop_sems:
                nc.gpsimd.sem_clear(s)
            nc.all_engine_barrier()


def _layouts(np, I):
    a = {k: np.asarray(v) for k, v in I.items()}
    L = {"x": a["x"]}
    cv = lambda n: a["L0_conv_" + n]
    L["ident"] = np.eye(128, dtype=np.float32)
    own = np.repeat(np.eye(8, dtype=np.float32), PD, axis=0)
    L["quad_mask"] = np.tile(own, (3, 1))
    L["four_mask"] = np.tile(own[0:16, 0:4], (6, 1))
    L["rank8"] = np.tile(np.arange(EX, 0, -1, dtype=np.float32), (TT, 1))
    L["pick"] = np.concatenate([np.tile(np.eye(2 * DS, dtype=np.float32), (3, 1)),
                                np.zeros((32, 2 * DS), np.float32)])
    L["w1"] = cv("W1").transpose(1, 0, 2).reshape(C, 128)
    L["w2"] = cv("W2").reshape(QUADS, 8, 3, 3, PD, PD).transpose(3, 1, 4, 2, 0, 5).reshape(96, 3 * QUADS, PD)
    L["w3"] = cv("W3").reshape(128, C)

    def wide(n):
        third = cv(n + "3").reshape(ZP, 2, C).transpose(1, 2, 0).reshape(128, ZP)
        return np.concatenate([cv(n + "1").reshape(128, 1), cv(n + "2").reshape(128, 1), third], axis=1)

    rows = lambda n: np.repeat(cv(n + "3"), PD, axis=0)
    L["bnv"] = np.concatenate([wide("V"), rows("V")], axis=1)
    L["bng"] = np.concatenate([wide("G"), rows("G")], axis=1)
    L["bnm"], L["bnb"], L["bnbe"] = wide("M"), wide("B"), wide("Be")
    L["gb"] = np.stack([a["L1_attn_ln_gamma"], a["L1_attn_ln_beta"]], axis=1)
    for d, p in enumerate("fb"):
        m = lambda n: a[f"L1_attn_{p}_{n}"]
        inp = m("in_proj_w").transpose(1, 0)
        L[f"wx{d}"] = np.tile(inp[:, 0:DI].reshape(1, C, 1, DI), (2, 1, 2, 1)).reshape(128, 2, DI)
        taps = m("conv_w").reshape(DI, TAPS).transpose(1, 0)
        if d:
            taps = taps[::-1]
        taps = taps.reshape(2, 2, DI).transpose(1, 0, 2)
        L[f"tapw{d}"] = np.repeat(taps, C, axis=0)
        L[f"wz{d}"] = inp[:, DI:2 * DI]
        L[f"wdt_a{d}"] = m("x_proj_w")[0:DR]
        L[f"wdt_b{d}"] = m("dt_proj_w").transpose(1, 0)
        L[f"wbc{d}"] = m("x_proj_w")[DR:DR + 2 * DS].transpose(1, 0)
        L[f"wo{d}"] = m("out_proj_w").transpose(1, 0)
        L[f"dvec{d}"] = np.concatenate([m("conv_b").reshape(DI, 1), m("dt_proj_b").reshape(DI, 1),
                                        m("D").reshape(DI, 1), m("A_log")], axis=1)
    f = lambda n: a["L1_ffn_" + n]
    L["we1"] = np.tile(f("W1").transpose(1, 0, 2).reshape(C, MT, 128), (2, 1, 1))
    L["pick_w"] = np.tile(np.eye(EX, dtype=np.float32), (3, 1))
    L["we2"] = f("W2").reshape(MT, 128, C).transpose(1, 0, 2)
    L["be1"] = f("b1").reshape(MT, 128).transpose(1, 0)
    L["be2"] = f("b2").reshape(EX // 2, 128).transpose(1, 0)
    L["lng"], L["lnb"] = (np.tile(f(n).transpose(1, 0), (2, 1)) for n in ("ln_g", "ln_b"))
    L["wr"] = f("Wr")
    L["br"] = np.tile(f("br").reshape(1, EX), (TT, 1))
    return {k: np.ascontiguousarray(v) for k, v in L.items()}


def kernel(**inputs):
    import numpy as _np
    import concourse.bacc as _bacc
    from concourse import mybir as _mybir
    from concourse.bass_utils import run_bass_kernel_spmd as _run

    nc = _bacc.Bacc("TRN2", target_bir_lowering=False, num_devices=1)
    arrays, T = {}, {}
    for name, a in _layouts(_np, inputs).items():
        arrays[f"in_{name}_dram"] = a
        T[name] = nc.dram_tensor(f"in_{name}_dram", a.shape, _mybir.dt.from_np(a.dtype), kind="ExternalInput").ap()
    T["out"] = nc.dram_tensor("out_0_dram", (NB, HH, WW, C), _mybir.dt.float32, kind="ExternalOutput").ap()
    T["h2_scratch"] = nc.dram_tensor("h2_scratch", (2, 3, 16, ZT, CH), BF16, kind="Internal").ap()
    T["w3_scratch"] = nc.dram_tensor("w3_scratch", (128, 3, C), BF16, kind="Internal").ap()
    build(nc, T)
    r = _run(nc, [arrays], core_ids=[0])
    return r.results[0]["out_0_dram"]
```

```python
import concourse.bass as bass
from concourse import mybir
from contextlib import ExitStack

F32 = mybir.dt.float32
BF16 = mybir.dt.bfloat16
ALU = mybir.AluOpType
ACT = mybir.ActivationFunctionType
AX = mybir.AxisListType

NB, HH, WW, C = 8, 56, 56, 64
TOK = HH * WW
ROWS = 8
CH = ROWS * WW
NCH = TOK // CH
TT = 112
KT = CH // TT
NT = TOK // TT
PATHS, PD = 32, 4
PW = WW + 2
ZP = PATHS * C // 128
DI, DS, DR, TAPS = 128, 16, 16, 4
EX, HID = 8, 256
MT = EX * HID // 128
LN_EPS, BN_EPS = 1e-5, 1e-3
DT_CLAMP = 40.0
FAR = 1.0e30
QUADS = 4
H1_SIZE = (HH + 2) * PW + 2
SLAB = (ROWS + 2) * PW
COMBOS = (0, 1, 2, 0, 1, 0)
W_COMBOS = (0, 0, 0, 1, 1, 2)
ZT = 8
ACT_J = (1, 3, 5, 7, 9, 11, 13, 15)
SECOND_AT = (5, 8, 11)
DVE_J = tuple(j for j in range(ZP) if j not in ACT_J)
PRE = 4
STEPS = 2 * NCH


def build(nc, T):
    ctx = ExitStack()
    with ctx:
        def sb(name, shape, dt=F32):
            return ctx.enter_context(nc.sbuf_tensor(name, shape, dt))

        sems = []

        def sem(name):
            s = ctx.enter_context(nc.semaphore(name))
            sems.append(s)
            return s

        ident = sb("ident", [128, 128])
        identb = sb("identb", [128, 128], BF16)
        quad_mask = sb("quad_mask", [96, 8])
        four_mask = sb("four_mask", [96, 4])
        rank8 = sb("rank8", [TT, EX])
        pick_small = sb("pick_small", [128, 2 * DS])
        pick = sb("pick", [128, 2 * DS, 128], BF16)
        half_pow = sb("half_pow", [128, 82])
        w1 = sb("w1", [C, 128])
        w2c = sb("w2c", [96, 3 * QUADS, PD])
        w2 = sb("w2", [96, 3 * QUADS, 8 * PD])
        w3c = sb("w3c", [128, C])
        w3p = sb("w3p", [128, 3, C], BF16)
        w3x = sb("w3x", [96, ZT, C], BF16)
        w3 = sb("w3", [96, ZT, 4, C], BF16)
        bnv = sb("bnv", [128, 82])
        bng = sb("bng", [128, 82])
        bnm = sb("bnm", [128, 18])
        bnb = sb("bnb", [128, 18])
        bnbe = sb("bnbe", [128, 18])
        nb3 = sb("nb3", [128, ZP])
        sum_b3 = sb("sum_b3", [128, 1])
        gb = sb("gb", [C, 2])
        wx = [sb(f"wx{d}", [128, 2, DI]) for d in range(2)]
        tapw = [sb(f"tapw{d}", [128, 2, DI]) for d in range(2)]
        wz = [sb(f"wz{d}", [C, DI]) for d in range(2)]
        wdt_a = [sb(f"wdt_a{d}", [DR, DI]) for d in range(2)]
        wdt_b = [sb(f"wdt_b{d}", [DR, DI]) for d in range(2)]
        wdt = [sb(f"wdt{d}", [DI, DI]) for d in range(2)]
        wbc = [sb(f"wbc{d}", [DI, 2 * DS]) for d in range(2)]
        wo = [sb(f"wo{d}", [DI, C]) for d in range(2)]
        dvec = [sb(f"dvec{d}", [DI, 3 + DS]) for d in range(2)]
        we1s = [sb(f"we1s{i}", [128, MT, 128], BF16) for i in range(3)]
        we2 = sb("we2", [128, MT, C])
        pick_w_small = sb("pick_w_small", [3 * EX, EX])
        pick_w = sb("pick_w", [3 * EX, EX, C], BF16)
        be1 = sb("be1", [128, MT])
        be2 = sb("be2", [128, EX // 2])
        lng = sb("lng", [128, EX])
        lnb = sb("lnb", [128, EX])
        wr = sb("wr", [C, EX])
        br = sb("br", [TT, EX])

        x_tok = sb("x_tok", [TT, NT, C])
        res = sb("res", [TT, NT, C])
        xn = sb("xn", [128, TOK + 6])
        u = [sb(f"u{d}", [DI, TOK]) for d in range(2)]
        zs = [sb(f"zs{d}", [DI, TOK]) for d in range(2)]

        xT = sb("xT", [C, 2, CH])
        h1 = sb("h1", [128, H1_SIZE])
        h1v = h1[:, 0:(HH + 2) * PW].rearrange("p (r w) -> p r w", w=PW)
        h2 = sb("h2", [128, 2, CH])
        rz = sb("rz", [128, 4, CH])
        tmp = sb("tmp", [TT, 3, KT, C])
        xnt = sb("xnt", [TT, 2, KT, 2, C])
        stat = sb("stat", [TT, 2, 8, KT])
        sq2 = sb("sq2", [TT, NT])
        dtv = sb("dtv", [DI, 2, CH])
        dtu = sb("dtu", [DI, 2, CH])
        sp = sb("sp", [DI, 4, CH])
        bct = sb("bct", [TT, KT, 3, 2 * DS], BF16)
        bcr = sb("bcr", [TT, KT, 2 * DS])
        bc3 = sb("bc3", [128, 2, CH], BF16)
        dA = sb("dA", [DI, 3, CH])
        dBu = sb("dBu", [DI, 3, CH])
        acc = dBu
        hs = sb("hs", [DI, 3, CH])
        cb = sb("cb", [DI, 3, CH])
        hc = sb("hc", [DI, 3, CH])
        slab = [zs[i][0:96, 0:QUADS * SLAB].rearrange("p (q n) -> p q n", q=QUADS) for i in range(2)]
        h2p = dA[:, :, :].rearrange("p a b -> p (a b)").bitcast(BF16).rearrange("p (i a n) -> p i a n", i=2, a=3)
        h3 = [u[i][0:96, :].bitcast(BF16)[:, 0:ZT * CH].rearrange("p (t n) -> p t n", t=ZT) for i in range(2)]
        state = sb("state", [DI, 2, DS])
        ytok = sb("ytok", [TT, KT * 128])
        hg = rz
        lg = sp[0:TT, :, :].rearrange("p a b -> p (a b)").rearrange("p (i n e) -> p i n e", n=NT, e=EX)
        l1 = sb("l1", [TT, 8, NT])
        wgt = sb("wgt", [TT, NT, EX])
        wgt3 = sb("wgt3", [TT, NT, 3, EX], BF16)
        wT = sb("wT", [3 * EX, 2, CH], BF16)
        yw = dA
        wb = hs
        xn32 = cb[0:C, :, :]
        tok_parts = u[0][:, :].bitcast(BF16).rearrange("p (i t) -> p i t", i=2)
        we1 = u[1][:, 0:MT * 128].rearrange("p (m h) -> p m h", m=MT)
        we1r = zs[0][:, 0:MT * 128].rearrange("p (m h) -> p m h", m=MT)
        outb = dBu[0:TT, :, :].rearrange("p a b -> p (a b)")[:, 0:2 * KT * C].rearrange("p (i k c) -> p i k c", k=KT, c=C)

        ps = [ctx.enter_context(nc.psum_tensor(f"ps{i}", [128, 512], F32)) for i in range(8)]

        x_dram = T["x"].rearrange("b h w c -> b (h w) c").rearrange("b (n p) c -> b p n c", p=TT)
        o_dram = T["out"].rearrange("b h w c -> b (h w) c").rearrange("b (n p) c -> b p n c", p=TT)

        s_load = sem("s_load")
        s_prep = sem("s_prep")
        s_pool = sem("s_pool")
        s_pe = sem("s_pe")
        s_act = sem("s_act")
        s_w3, s_w3d, s_w3x = sem("s_w3"), sem("s_w3d"), sem("s_w3x")

        LOADS = [(ident, "ident"), (quad_mask, "quad_mask"), (four_mask, "four_mask"), (rank8, "rank8"),
                 (pick_small, "pick"), (w1, "w1"), (w2c, "w2"), (w3c, "w3"), (bnv, "bnv"), (bng, "bng"),
                 (bnm, "bnm"), (bnb, "bnb"), (bnbe, "bnbe"), (gb, "gb"), (we1, "we1"), (we2, "we2"),
                 (be1, "be1"), (be2, "be2"), (lng, "lng"), (lnb, "lnb"), (wr, "wr"), (br, "br"),
                 (pick_w_small, "pick_w")]
        for d in range(2):
            LOADS += [(wx[d], f"wx{d}"), (tapw[d], f"tapw{d}"), (wz[d], f"wz{d}"), (wdt_a[d], f"wdt_a{d}"),
                      (wdt_b[d], f"wdt_b{d}"), (wbc[d], f"wbc{d}"), (wo[d], f"wo{d}"), (dvec[d], f"dvec{d}")]

        with nc.Block() as block:
            @block.sync
            def _(sp_):
                for tile, name in LOADS:
                    src, dst = T[name], tile
                    idx = tuple(slice(None) for _ in tile.shape)
                    sp_.dma_start(dst[idx], src).then_inc(s_load, 16)
                sp_.wait_ge(s_w3, 1)
                sp_.dma_start(T["w3_scratch"], w3p[:, :, :]).then_inc(s_w3d, 16)
                sp_.wait_ge(s_w3d, 16)
                for k in range(6):
                    sp_.dma_start(w3x[16 * k:16 * k + 16, :, :],
                                  T["w3_scratch"][:, W_COMBOS[k], :].rearrange("(t c) n -> c t n", c=16))\
                       .then_inc(s_w3x, 16)

            @block.gpsimd
            def _(pool):
                pool.memset(half_pow[:, :], -0.5).then_inc(s_pool, 1)
                pool.memset(h1[:, :], 0.0).then_inc(s_pool, 1)
                pool.memset(xn[:, :], 0.0).then_inc(s_pool, 1)
                pool.memset(bc3[:, :, :], 0.0).then_inc(s_pool, 1)
                pool.wait_ge(s_pool, 1)
                pool.wait_ge(s_prep, 1)
                nc.gpsimd.tensor_tensor(bnv[:, :], bnv[:, :], half_pow[:, :], ALU.pow).then_inc(s_pool, 1)

            @block.scalar
            def _(act):
                act.wait_ge(s_load, 16 * len(LOADS))
                for d in range(2):
                    nc.scalar.activation(dvec[d][:, 3:3 + DS], dvec[d][:, 3:3 + DS], ACT.Exp).then_inc(s_act, 1)

            @block.vector
            def _(dve):
                step = [0]

                def then(ins):
                    step[0] += 1
                    ins.then_inc(s_prep, 1)
                    dve.wait_ge(s_prep, step[0])

                V = nc.vector
                dve.wait_ge(s_load, 16 * len(LOADS))
                then(V.tensor_scalar(bnv[:, :], bnv[:, :], BN_EPS, None, ALU.add))
                then(V.tensor_copy(identb[:, :], ident[:, :]))
                then(V.tensor_copy(pick[:, :, :], pick_small[:, :].unsqueeze(2).to_broadcast([128, 2 * DS, 128])))
                wide = [96, 3 * QUADS, 8, PD]
                then(V.tensor_tensor(w2[:, :, :].rearrange("p t (a b) -> p t a b", b=PD),
                                     w2c[:, :, :].unsqueeze(2).to_broadcast(wide),
                                     quad_mask[:, :].unsqueeze(1).unsqueeze(3).to_broadcast(wide), ALU.mult))
                dve.wait_ge(s_pool, 5)
                then(V.tensor_tensor(bng[:, :], bng[:, :], bnv[:, :], ALU.mult))
                then(V.tensor_tensor(w3c[:, :], w3c[:, :], bng[:, 18:82], ALU.mult))
                then(V.tensor_copy(w3p[:, 0, :], w3c[:, :]))
                then(V.tensor_tensor(w3c[:, :], w3c[:, :], w3p[:, 0, :], ALU.subtract))
                then(V.tensor_copy(w3p[:, 1, :], w3c[:, :]))
                then(V.tensor_tensor(w3c[:, :], w3c[:, :], w3p[:, 1, :], ALU.subtract))
                V.tensor_copy(w3p[:, 2, :], w3c[:, :]).then_inc(s_w3, 1)
                then(V.tensor_tensor(bnb[:, :], bnb[:, :], bnm[:, :], ALU.subtract))
                then(V.tensor_tensor(bnb[:, :], bnb[:, :], bng[:, 0:18], ALU.mult))
                then(V.tensor_tensor(bnb[:, :], bnb[:, :], bnbe[:, :], ALU.add))
                then(V.tensor_scalar(nb3[:, :], bnb[:, 2:18], -1.0, None, ALU.mult))
                then(V.reduce_sum(sum_b3[:, :], bnb[:, 2:18], axis=AX.X))
                for j in ACT_J:
                    then(V.tensor_tensor(sum_b3[:, :], sum_b3[:, :], bnb[:, 2 + j:3 + j], ALU.subtract))
                for d in range(2):
                    then(V.tensor_tensor(wx[d][:, :, :], wx[d][:, :, :], tapw[d][:, :, :], ALU.mult))
                dve.wait_ge(s_w3x, 16 * 6)
                wide = [96, ZT, 4, C]
                then(V.tensor_tensor(w3[:, :, :, :], w3x[:, :, :].unsqueeze(2).to_broadcast(wide),
                                     four_mask[:, :].unsqueeze(1).unsqueeze(3).to_broadcast(wide), ALU.mult))
                dve.wait_ge(s_act, 2)
                for d in range(2):
                    then(V.tensor_scalar(dvec[d][:, 3:3 + DS], dvec[d][:, 3:3 + DS], -1.0, None, ALU.mult))
                dve.wait_ge(s_pe, 1)
                for d in range(2):
                    then(V.tensor_copy(wdt[d][:, :], ps[d][:, 0:DI]))
                then(V.tensor_tensor(be1[:, :], be1[:, :], ps[2][:, 0:MT], ALU.add))
                for e in range(EX):
                    then(V.tensor_scalar(we1[:, 2 * e:2 * e + 2, :], we1[:, 2 * e:2 * e + 2, :],
                                         lng[:, e:e + 1], None, ALU.mult))
                then(V.tensor_copy(we1s[0][:, :, :], we1))
                then(V.tensor_tensor(we1r, we1, we1s[0][:, :, :], ALU.subtract))
                then(V.tensor_copy(we1s[1][:, :, :], we1r))
                then(V.tensor_tensor(we1r, we1r, we1s[1][:, :, :], ALU.subtract))
                then(V.tensor_copy(we1s[2][0:C, :, :], we1r[0:C]))
                then(V.tensor_copy(we1s[2][C:128, :, :], we1s[0][C:128, :, :]))
                then(V.tensor_copy(pick_w[:, :, :], pick_w_small[:, :].unsqueeze(2).to_broadcast([3 * EX, EX, C])))

            @block.tensor
            def _(pe):
                pe.wait_ge(s_load, 16 * len(LOADS))
                for d in range(2):
                    nc.tensor.matmul(ps[d][:, 0:DI], wdt_a[d][:, :], wdt_b[d][:, :], start=True, stop=True)
                for m in range(MT):
                    last = nc.tensor.matmul(ps[2][:, m:m + 1], we1[0:C, m, :], lnb[0:C, m // 2:m // 2 + 1],
                                            start=True, stop=True)
                last.then_inc(s_pe, 1)

        for s in sems:
            nc.gpsimd.sem_clear(s)
        nc.all_engine_barrier()

        x_in = sem("x_in")
        xT_ps, xT_sb = sem("xT_ps"), sem("xT_sb")
        h1_ps, h1_sb = sem("h1_ps"), sem("h1_sb")
        h1_kept, h1_pre = sem("h1_kept"), sem("h1_pre")
        h2_ps, h2_p, h2_r = sem("h2_ps"), sem("h2_p"), sem("h2_r")
        slabbed = [sem("slabbed0"), sem("slabbed1")]
        slab_pre = [sem("slab_pre0"), sem("slab_pre1")]
        bounced = [sem("bounced0"), sem("bounced1")]
        arranged = [sem("arranged0"), sem("arranged1")]
        z_ps, z_dve, z_act, z_T = sem("z_ps"), sem("z_dve"), sem("z_act"), sem("z_T")
        x1_ps, x1_out = sem("x1_ps"), sem("x1_out")
        a_ch, pw_req, pw_done = sem("a_ch"), sem("pw_req"), sem("pw_done")
        xn_tok, xn_ps, xn_sb = sem("xn_tok"), sem("xn_ps"), sem("xn_sb")
        b_ps, b_sb = sem("b_ps"), sem("b_sb")
        dt_ps, bc_ps, bc_tok, bcT_ps, bcT_sb = (sem(n) for n in ("dt_ps", "bc_ps", "bc_tok", "bcT_ps", "bcT_sb"))
        dt_x, dt_e, dt_y, dt_r, dt_l, dt_s, dt_ok, dtu_ok = (sem(n) for n in
            ("dt_x", "dt_e", "dt_y", "dt_r", "dt_l", "dt_s", "dt_ok", "dtu_ok"))
        bc_part, gated = sem("bc_part"), sem("gated")
        bb_ps, cb_ps, a_ok, cb_ok = sem("bb_ps"), sem("cb_ps"), sem("a_ok"), sem("cb_ok")
        bu_ok, h_ok, hc_ok, st_ok, y_acc = (sem(n) for n in ("bu_ok", "h_ok", "hc_ok", "st_ok", "y_acc"))
        y_tok, yT_ps, yz_ok, st0 = sem("y_tok"), sem("yT_ps"), sem("yz_ok"), sem("st0")
        o_ps, d_ch, d_tok, dT_ps, dT_sb, lg_ps, lg_ok = (sem(n) for n in
            ("o_ps", "d_ch", "d_tok", "dT_ps", "dT_sb", "lg_ps", "lg_ok"))
        dp_a, dp_r, o_rd = sem("dp_a"), sem("dp_r"), sem("o_rd")
        r_ch, e_req, e_ok, routed, w_ok = sem("r_ch"), sem("e_req"), sem("e_ok"), sem("routed"), sem("w_ok")
        wb_ps, wb_sb, up_ps, g_ok, dn, ye_dve, ye_sum, ye_T, o_sum = (sem(n) for n in
            ("wb_ps", "wb_sb", "up_ps", "g_ok", "dn", "ye_dve", "ye_sum", "ye_T", "o_sum"))
        stored = [sem("stored0"), sem("stored1")]
        loop_sems = sems[8:]
        last_sems = [x_in, h1_pre, r_ch, e_req, e_ok, routed, w_ok, wb_ps, wb_sb, up_ps, g_ok, dn, ye_dve, ye_sum, ye_T, o_sum] + slab_pre + stored
        done_sems = [s for s in loop_sems if s not in last_sems]

        def tile4(bank, n):
            return bank[0:TT, 0:KT * n].rearrange("p (k n) -> p k n", n=n)

        def bc_last(ap, n):
            return ap.unsqueeze(2).to_broadcast([ap.shape[0], ap.shape[1], n])

        def norm_sums(link, src, xc, i):
            norm_mean(link, src, i)
            norm_var(link, src, xc, i)

        def norm_mean(link, src, i):
            V, st = nc.vector, stat[:, i]
            link(V.reduce_sum(st[:, 0, :], src, axis=AX.X))
            link(V.tensor_scalar(st[:, 0, :], st[:, 0, :], 1.0 / C, None, ALU.mult))

        def norm_var(link, src, xc, i):
            V, st = nc.vector, stat[:, i]
            link(V.tensor_tensor(xc, src, bc_last(st[:, 0, :], C), ALU.subtract))
            link(V.tensor_tensor(tmp[:, 2], xc, xc, ALU.mult))
            link(V.reduce_sum(st[:, 5, :], tmp[:, 2], axis=AX.X))
            link(V.tensor_scalar(st[:, 5, :], st[:, 5, :], 1.0 / C, None, ALU.mult))
            V.tensor_scalar(st[:, 1, :], st[:, 5, :], LN_EPS, None, ALU.add).then_inc(pw_req, 1)

        def norm_again(dve, link, i, pw_n):
            V, st = nc.vector, stat[:, i]
            dve.wait_ge(pw_done, pw_n + 1)
            link(V.tensor_tensor(st[:, 3, :], st[:, 5, :], st[:, 2, :], ALU.mult))
            link(V.tensor_tensor(st[:, 3, :], st[:, 3, :], st[:, 2, :], ALU.mult))
            V.tensor_scalar(st[:, 3, :], st[:, 3, :], LN_EPS, None, ALU.add).then_inc(pw_req, 1)

        def linker(dve, s):
            count = [0]

            def link(ins):
                count[0] += 1
                ins.then_inc(s, 1)
                dve.wait_ge(s, count[0])
            return link

        def rev(ap, d):
            return ap[:, ::-1] if d else ap

        def chunk_of(k):
            return k // 2 if k % 2 == 0 else NCH - 1 - k // 2

        def x_T(c, bank):
            for k in range(KT):
                last = nc.tensor.transpose(bank[0:C, k * TT:(k + 1) * TT], x_tok[:, c * KT + k, :],
                                           ident[0:TT, 0:TT])
            return last

        def paths_in(c, bank):
            return nc.tensor.matmul(bank[:, 0:CH], w1[:, :], xT[:, c % 2, :], start=True, stop=True)

        def keep_xT(c, bank):
            return nc.scalar.activation(xT[:, c % 2, :], bank[0:C, 0:CH], ACT.Copy)

        def keep_h1(c, bank):
            return nc.scalar.activation(h1v[:, 1 + c * ROWS:1 + (c + 1) * ROWS, 1:1 + WW],
                                        bank[:, 0:CH].rearrange("p (r w) -> p r w", w=WW), ACT.Relu,
                                        bias=bnb[:, 0:1], scale=bng[:, 0:1])

        def keep_rows(sp_, c, kept):
            a = 0 if c == 0 else (1 + c * ROWS) * PW
            b = H1_SIZE if c == NCH - 1 else (1 + (c + 1) * ROWS) * PW
            sp_.dma_start(T["h1_scratch"][:, a:b], h1[:, a:b]).then_inc(kept, 16)

        def cut_slab(sp_, c, cut):
            for dx in range(3):
                at = c * ROWS * PW + dx
                sp_.dma_start(slab[c % 2][32 * dx:32 * dx + 32, :, :],
                              T["h1_scratch"][:, at:at + SLAB].rearrange("(q p) n -> p q n", p=32))\
                   .then_inc(cut[c % 2], 16)

        with nc.Block() as block:
            @block.sync
            def _(sp_):
                sp_.dma_start(x_tok[:, :, :], x_dram[0]).then_inc(x_in, 16)
                for c in range(PRE):
                    sp_.wait_ge(h1_sb, c + 1)
                    keep_rows(sp_, c, h1_pre)
                    sp_.wait_ge(h1_pre, 16 * (c + 1))
                    if 1 <= c <= 2:
                        cut_slab(sp_, c - 1, slab_pre)
                for c in range(2):
                    sp_.wait_ge(slab_pre[c], 16 * 3)

            @block.tensor
            def _(pe):
                pe.wait_ge(x_in, 16)
                for c in range(PRE):
                    if c:
                        pe.wait_ge(xT_sb, c)
                    x_T(c, ps[0]).then_inc(xT_ps, 1)
                    pe.wait_ge(xT_sb, c + 1)
                    if c:
                        pe.wait_ge(h1_sb, c)
                    paths_in(c, ps[1]).then_inc(h1_ps, 1)

            @block.scalar
            def _(act):
                for c in range(PRE):
                    act.wait_ge(xT_ps, c + 1)
                    keep_xT(c, ps[0]).then_inc(xT_sb, 1)
                    act.wait_ge(h1_ps, c + 1)
                    keep_h1(c, ps[1]).then_inc(h1_sb, 1)

        for s in loop_sems:
            nc.gpsimd.sem_clear(s)
        nc.all_engine_barrier()

        with nc.Fori(0, NB) as img:
            with nc.Block() as block:
                @block.sync
                def _(sp_):
                    def shift(c):
                        sp_.wait_ge(h1_kept, 16 * (min(c + 2, NCH) - PRE))
                        sp_.wait_ge(h2_ps, c - 1)
                        cut_slab(sp_, c, slabbed)

                    def put(c):
                        if c >= 2:
                            sp_.wait_ge(arranged[c % 2], 48 * (c // 2))
                        for a in range(3):
                            sp_.wait_ge(h2_p, 3 * c + a + 1)
                            sp_.dma_start(T["h2_scratch"][c % 2, a].rearrange("c t n -> t c n"), h2p[:, c % 2, a, :])\
                               .then_inc(bounced[c % 2], 16)

                    def arrange(c):
                        sp_.wait_ge(bounced[c % 2], 48 * (c // 2 + 1))
                        if c >= 2:
                            sp_.wait_ge(z_ps, ZP * (c - 1))
                        src = T["h2_scratch"][c % 2].rearrange("a c t n -> (a c) t n")
                        row = 0
                        for parts in (3, 2, 1):
                            sp_.dma_start(h3[c % 2][row:row + 16 * parts, :, :], src[0:16 * parts])\
                               .then_inc(arranged[c % 2], 16)
                            row += 16 * parts

                    put(0)
                    arrange(0)
                    sp_.wait_ge(h2_ps, 1)
                    cut_slab(sp_, 2, slabbed)
                    for c in range(NCH):
                        if c + PRE < NCH:
                            sp_.wait_ge(h1_sb, c + 1)
                            keep_rows(sp_, c + PRE, h1_kept)
                        if c + 1 < NCH:
                            put(c + 1)
                            arrange(c + 1)
                        if c + 3 < NCH:
                            shift(c + 3)

                @block.gpsimd
                def _(pool):
                    def remainder(c, i):
                        pool.wait_ge(h2_p, 3 * c + i)
                        if i == 1 and c:
                            pool.wait_ge(h2_p, 3 * c)
                        src = h2[:, c % 2, :] if i == 1 else sp[:, 1, :]
                        nc.gpsimd.tensor_tensor(sp[:, i, :], src, h2p[:, c % 2, i - 1, :], ALU.subtract).then_inc(h2_r, 1)

                    remainder(0, 1)
                    remainder(0, 2)
                    remainder(1, 1)
                    remainder(1, 2)
                    for c in range(NCH):
                        i = c % 2
                        if c + 2 < NCH:
                            remainder(c + 2, 1)
                            remainder(c + 2, 2)
                        pool.wait_ge(pw_req, 2 * c + 1)
                        nc.gpsimd.tensor_tensor(stat[:, i, 2, :], stat[:, i, 1, :], half_pow[0:TT, 0:KT], ALU.pow)\
                            .then_inc(pw_done, 1)
                        pool.wait_ge(pw_req, 2 * c + 2)
                        nc.gpsimd.tensor_tensor(stat[:, i, 4, :], stat[:, i, 3, :], half_pow[0:TT, 0:KT], ALU.pow)\
                            .then_inc(pw_done, 1)

                @block.tensor
                def _(pe):
                    def first(c):
                        if c > PRE:
                            pe.wait_ge(xT_sb, c - PRE)
                        x_T(c, ps[0]).then_inc(xT_ps, 1)

                    def first_paths(c):
                        pe.wait_ge(xT_sb, c - PRE + 1)
                        if c > PRE:
                            pe.wait_ge(h1_sb, c - PRE)
                        paths_in(c, ps[1]).then_inc(h1_ps, 1)

                    def second(c, dy):
                        if dy == 0:
                            if c >= 2:
                                pe.wait_ge(slabbed[c % 2], 16 * 3 * (c // 2))
                            if c:
                                pe.wait_ge(h2_p, 3 * c - 2)
                        for q in range(QUADS):
                            rows = slab[c % 2][:, q, dy * PW:(dy + ROWS) * PW]
                            last = nc.tensor.matmul(ps[2][32 * q:32 * q + 32, 0:CH], w2[:, dy * QUADS + q, :],
                                                    rows.rearrange("p (r w) -> p r w", w=PW)[:, :, 0:WW],
                                                    start=(dy == 0), stop=(dy == 2))
                        if dy == 2:
                            last.then_inc(h2_ps, 1)

                    def fold(c, m):
                        n = len(ACT_J)
                        if m < n:
                            src = rz[:, (c * n + m) % 4, :]
                            pe.wait_ge(z_act, c * n + m + 1)
                        else:
                            src = acc[:, c % 2, :]
                            pe.wait_ge(z_dve, (c + 1) * len(DVE_J))
                        if m == 0 and c:
                            pe.wait_ge(x1_out, c)
                        for k in range(KT):
                            last = nc.tensor.matmul(ps[3][0:TT, k * 128:(k + 1) * 128], src[:, k * TT:(k + 1) * TT],
                                                    ident[:, :], is_transpose=True, start=(m == 0 and k == 0),
                                                    stop=(m == n and k == KT - 1), skip_group_check=True)
                        last.then_inc(z_T, 1)

                    def third(c):
                        pe.wait_ge(arranged[c % 2], 48 * (c // 2 + 1))
                        m = 0
                        for j in range(ZP):
                            g = c * ZP + j - 4
                            if g >= 0:
                                cc, jj = g // ZP, g % ZP
                                if jj in ACT_J:
                                    pe.wait_ge(z_act, cc * len(ACT_J) + ACT_J.index(jj) + 1)
                                else:
                                    pe.wait_ge(z_dve, cc * len(DVE_J) + DVE_J.index(jj) + 1)
                            nc.tensor.matmul(ps[4 + j % 4][:, 0:CH],
                                             w3[:, j // 2, 2 * (j % 2):2 * (j % 2) + 2, :].rearrange("p a b -> p (a b)"),
                                             h3[c % 2][:, j // 2, :], start=True, stop=True).then_inc(z_ps, 1)
                            if j < 3 and c:
                                fold(c - 1, len(ACT_J) - 2 + j)
                            if j == 3 and c + PRE < NCH:
                                first_paths(c + PRE)
                            if j == 4 and c >= 2:
                                norm_T(c - 2)
                            if j in SECOND_AT and c + 2 < NCH:
                                second(c + 2, SECOND_AT.index(j))
                            if m < len(ACT_J) - 2 and j >= ACT_J[m] + 4:
                                fold(c, m)
                                m += 1

                    def norm_T(c):
                        pe.wait_ge(xn_tok, c + 1)
                        pe.wait_ge(xT_sb, NCH - PRE)
                        if c:
                            pe.wait_ge(xn_sb, c)
                        for k in range(KT):
                            last = nc.tensor.transpose(ps[0][0:C, k * TT:(k + 1) * TT], xnt[:, c % 2, k, 0, :],
                                                       ident[0:TT, 0:TT])
                        last.then_inc(xn_ps, 1)

                    for c in range(2):
                        for dy in range(3):
                            second(c, dy)
                    for c in range(NCH):
                        if c + PRE < NCH:
                            first(c + PRE)
                        third(c)
                    for m in range(len(ACT_J) - 2, len(ACT_J) + 1):
                        fold(NCH - 1, m)
                    norm_T(NCH - 2)
                    norm_T(NCH - 1)

                @block.scalar
                def _(act):
                    A = nc.scalar

                    def evac_x(c):
                        act.wait_ge(xT_ps, c - PRE + 1)
                        if c >= PRE + 2:
                            act.wait_ge(h1_ps, c - PRE - 1)
                        keep_xT(c, ps[0]).then_inc(xT_sb, 1)

                    def evac_h1(c):
                        act.wait_ge(h1_ps, c - PRE + 1)
                        keep_h1(c, ps[1]).then_inc(h1_sb, 1)

                    def evac_h2(c):
                        act.wait_ge(h2_ps, c + 1)
                        if c >= 2:
                            act.wait_ge(bounced[c % 2], 48 * (c // 2))
                        A.activation(h2[:, c % 2, :], ps[2][:, 0:CH], ACT.Relu,
                                     bias=bnb[:, 1:2], scale=bng[:, 1:2])
                        A.activation(h2p[:, c % 2, 0, :], ps[2][:, 0:CH], ACT.Relu,
                                     bias=bnb[:, 1:2], scale=bng[:, 1:2]).then_inc(h2_p, 1)

                    def part(c, i):
                        act.wait_ge(h2_r, 2 * c + i)
                        A.activation(h2p[:, c % 2, i, :], sp[:, i, :], ACT.Copy).then_inc(h2_p, 1)

                    def evac_xn(c):
                        act.wait_ge(xn_ps, c + 1)
                        t0 = c * CH
                        A.activation(xn[0:C, 3 + t0:3 + t0 + CH], ps[0][0:C, 0:CH], ACT.Identity,
                                     bias=gb[:, 1:2], scale=gb[:, 0:1])
                        A.activation(xn[C:128, 2 + t0:2 + t0 + CH], ps[0][0:C, 0:CH], ACT.Identity,
                                     bias=gb[:, 1:2], scale=gb[:, 0:1]).then_inc(xn_sb, 1)

                    def rectify(c, m):
                        n, j = len(ACT_J), ACT_J[m]
                        act.wait_ge(z_ps, c * ZP + j + 1)
                        gg = c * n + m - 4
                        if gg >= 0:
                            act.wait_ge(z_T, (gg // n) * (n + 1) + gg % n + 1)
                        A.activation(rz[:, (c * n + m) % 4, :], ps[4 + j % 4][:, 0:CH], ACT.Relu,
                                     bias=bnb[:, 2 + j:3 + j]).then_inc(z_act, 1)

                    evac_h2(0)
                    part(0, 1)
                    part(0, 2)
                    evac_h2(1)
                    for c in range(NCH):
                        more = c + 1 < NCH
                        if c + 4 < NCH:
                            evac_x(c + 4)
                        rectify(c, 0)
                        if more:
                            part(c + 1, 1)
                        if c + 4 < NCH:
                            evac_h1(c + 4)
                        rectify(c, 1)
                        rectify(c, 2)
                        if more:
                            part(c + 1, 2)
                        rectify(c, 3)
                        if c >= 2:
                            evac_xn(c - 2)
                        rectify(c, 4)
                        rectify(c, 5)
                        rectify(c, 6)
                        if c + 2 < NCH:
                            evac_h2(c + 2)
                        rectify(c, 7)
                    evac_xn(NCH - 2)
                    evac_xn(NCH - 1)

                @block.vector
                def _(dve):
                    V = nc.vector
                    link = linker(dve, a_ch)

                    def rectify(c, m):
                        j, a = DVE_J[m], acc[:, c % 2, :]
                        z = ps[4 + j % 4][:, 0:CH]
                        if m == 0 and c >= 2:
                            dve.wait_ge(z_T, (len(ACT_J) + 1) * (c - 1))
                        dve.wait_ge(z_ps, c * ZP + j + 1)
                        if m:
                            dve.wait_ge(z_dve, c * len(DVE_J) + m)
                            V.scalar_tensor_tensor(a, z, nb3[:, j:j + 1], a, ALU.max, ALU.add).then_inc(z_dve, 1)
                        else:
                            V.tensor_scalar(a, z, nb3[:, j:j + 1], sum_b3[:, 0:1], ALU.max, ALU.add)\
                                .then_inc(z_dve, 1)

                    def paths_out(c):
                        n0 = c * KT
                        b3 = tile4(ps[3], 128)
                        dve.wait_ge(z_T, (len(ACT_J) + 1) * (c + 1))
                        link(V.tensor_tensor(tmp[:, 0], b3[:, :, 0:C], x_tok[:, n0:n0 + KT, :], ALU.add))
                        V.tensor_tensor(tmp[:, 1], b3[:, :, C:128], tmp[:, 0], ALU.add).then_inc(x1_out, 1)
                        dve.wait_ge(x1_out, c + 1)
                        link(V.tensor_scalar(res[:, n0:n0 + KT, :], tmp[:, 1], 0.0, None, ALU.max))

                    def tokens_out(c):
                        r, st = res[:, c * KT:(c + 1) * KT, :], stat[:, c % 2]
                        link(V.tensor_tensor(tmp[:, 1], tmp[:, 0], bc_last(st[:, 2, :], C), ALU.mult))
                        V.tensor_tensor(r, r, tmp[:, 1], ALU.add)
                        dve.wait_ge(pw_done, 2 * c + 2)
                        if c >= 2:
                            dve.wait_ge(xn_ps, c - 1)
                        V.tensor_tensor(xnt[:, c % 2, :, 0, :], tmp[:, 1], bc_last(st[:, 4, :], C), ALU.mult)\
                            .then_inc(xn_tok, 1)

                    for c in range(NCH + 1):
                        here, behind = c < NCH, c > 0
                        if here:
                            rectify(c, 0)
                            rectify(c, 1)
                            rectify(c, 2)
                        if behind:
                            paths_out(c - 1)
                        if here:
                            rectify(c, 3)
                        if behind:
                            norm_sums(link, res[:, (c - 1) * KT:c * KT, :], tmp[:, 0], (c - 1) % 2)
                        if here:
                            rectify(c, 4)
                            rectify(c, 5)
                        if behind:
                            norm_again(dve, link, (c - 1) % 2, 2 * (c - 1))
                        if here:
                            rectify(c, 6)
                        if behind:
                            tokens_out(c - 1)
                        if here:
                            rectify(c, 7)

            with nc.Block() as block:
                @block.tensor
                def _(pe):
                    for i in range(2 * STEPS):
                        c, d, z = i // 4, (i // 2) % 2, i % 2
                        t0 = c * CH
                        if i >= 8:
                            pe.wait_ge(b_sb, i - 7)
                        bank = ps[i % 8][:, 0:CH]
                        if z:
                            nc.tensor.matmul(bank, wz[d][:, :], xn[0:C, t0 + 3:t0 + 3 + CH], start=True, stop=True)\
                                .then_inc(b_ps, 1)
                        else:
                            at = t0 + 3 * d
                            nc.tensor.matmul(bank, wx[d][:, 0, :], xn[:, at:at + CH], start=True, stop=False)
                            nc.tensor.matmul(bank, wx[d][:, 1, :], xn[:, at + 2:at + 2 + CH], start=False, stop=True)\
                                .then_inc(b_ps, 1)

                @block.scalar
                def _(act):
                    for i in range(2 * STEPS):
                        c, d, z = i // 4, (i // 2) % 2, i % 2
                        act.wait_ge(b_ps, i + 1)
                        if z:
                            nc.scalar.activation(zs[d][:, c * CH:(c + 1) * CH], ps[i % 8][:, 0:CH], ACT.Silu)\
                                .then_inc(b_sb, 1)
                        else:
                            nc.scalar.activation(u[d][:, c * CH:(c + 1) * CH], ps[i % 8][:, 0:CH], ACT.Silu,
                                                 bias=dvec[d][:, 0:1]).then_inc(b_sb, 1)

            def ucols(k):
                c = chunk_of(k)
                return u[k % 2][:, c * CH:(c + 1) * CH]

            POST_AT = 3

            with nc.Block() as block:
                @block.tensor
                def _(pe):
                    def prep_dt(k):
                        d = k % 2
                        if k >= 2:
                            pe.wait_ge(yz_ok, k - 1)
                        nc.tensor.matmul(ps[0][:, 0:CH], wdt[d][:, :], ucols(k), start=True, stop=True)\
                            .then_inc(dt_ps, 1)

                    def prep_bc(k):
                        d, c = k % 2, chunk_of(k)
                        if k:
                            pe.wait_ge(bcT_sb, k)
                        for j in range(KT):
                            last = nc.tensor.matmul(ps[1][0:TT, 32 * j:32 * j + 32],
                                                    u[d][:, c * CH + j * TT:c * CH + (j + 1) * TT], wbc[d][:, :],
                                                    start=True, stop=True)
                        last.then_inc(bc_ps, 1)

                    def prep_T(k):
                        pe.wait_ge(bc_tok, k + 1)
                        out = ps[1][0:96, 0:CH // 2].bitcast(BF16)
                        for j in range(KT):
                            last = nc.tensor.transpose(out[:, j * TT:(j + 1) * TT],
                                                       bct[:, j].rearrange("p a b -> p (a b)"), identb[0:TT, 0:TT])
                        last.then_inc(bcT_ps, 1)

                    def fold(g):
                        k, s = g // DS, g % DS
                        pe.wait_ge(hc_ok, g + 1)
                        if s == 0 and k >= 2:
                            pe.wait_ge(y_tok, k - 1)
                        bank = ps[2 if k % 2 == 0 else 7]
                        for j in range(KT):
                            last = nc.tensor.matmul(bank[0:TT, j * 128:(j + 1) * 128],
                                                    hc[:, g % 3, j * TT:(j + 1) * TT], ident[:, :], is_transpose=True,
                                                    start=(s == 0 and j == 0), stop=(s == DS - 1 and j == KT - 1),
                                                    skip_group_check=True)
                        last.then_inc(y_acc, 1)

                    def post(k):
                        pe.wait_ge(y_tok, k + 1)
                        if k + 1 < STEPS:
                            pe.wait_ge(dt_ok, k + 2)
                        for j in range(KT):
                            last = nc.tensor.transpose(ps[0][:, j * TT:(j + 1) * TT], ytok[:, j * 128:(j + 1) * 128],
                                                       ident[0:TT, 0:TT])
                        last.then_inc(yT_ps, 1)

                    prep_dt(0)
                    prep_bc(0)
                    prep_T(0)
                    G = STEPS * DS
                    for g in range(G):
                        k, s = g // DS, g % DS
                        if s == 0:
                            pe.wait_ge(bcT_sb, k + 1)
                        if g >= 2:
                            pe.wait_ge(bu_ok, g - 1)
                            pe.wait_ge(cb_ok, g - 1)
                        nc.tensor.matmul(ps[3 + g % 2][:, 0:CH], pick[:, s, :], bc3[:, k % 2, :], start=True, stop=True)\
                            .then_inc(bb_ps, 1)
                        nc.tensor.matmul(ps[5 + g % 2][:, 0:CH], pick[:, DS + s, :], bc3[:, k % 2, :],
                                         start=True, stop=True).then_inc(cb_ps, 1)
                        if g >= 3:
                            fold(g - 3)
                        if s == POST_AT + 1 and k:
                            post(k - 1)
                        if s == 7 and k + 1 < STEPS:
                            prep_bc(k + 1)
                        if s == 8 and k + 1 < STEPS:
                            prep_dt(k + 1)
                        if s == 12 and k + 1 < STEPS:
                            prep_T(k + 1)
                    for g in range(G - 3, G):
                        fold(g)
                    post(STEPS - 1)

                @block.scalar
                def _(act):
                    A = nc.scalar
                    A.preload_act_table_set("natural_log_exp_and_others")

                    def soft_exp(k):
                        act.wait_ge(dt_x, k + 1)
                        A.activation(sp[:, 1, :], sp[:, 0, :], ACT.Exp).then_inc(dt_e, 1)

                    def soft_y(k):
                        act.wait_ge(dt_e, k + 1)
                        A.activation(sp[:, 2, :], sp[:, 1, :], ACT.Copy, bias=1.0).then_inc(dt_y, 1)

                    def soft_ln(k):
                        act.wait_ge(dt_y, k + 1)
                        A.activation(sp[:, 3, :], sp[:, 2, :], ACT.Ln).then_inc(dt_l, 1)

                    def copy_bc(k):
                        act.wait_ge(bcT_ps, k + 1)
                        A.activation(bc3[0:96, k % 2, :], ps[1][0:96, 0:CH // 2].bitcast(BF16), ACT.Copy)\
                            .then_inc(bcT_sb, 1)

                    soft_exp(0)
                    soft_y(0)
                    soft_ln(0)
                    copy_bc(0)
                    G = STEPS * DS
                    for g in range(G):
                        k, s = g // DS, g % DS
                        if s == 0:
                            act.wait_ge(dt_ok, k + 1)
                        if g >= 3:
                            act.wait_ge(h_ok, g - 2)
                        A.activation(dA[:, g % 3, :], dtv[:, k % 2, :], ACT.Exp, scale=dvec[k % 2][:, 3 + s:4 + s])\
                            .then_inc(a_ok, 1)
                        act.wait_ge(cb_ps, g + 1)
                        if g >= 3:
                            act.wait_ge(hc_ok, g - 2)
                        A.activation(cb[:, g % 3, :], ps[5 + g % 2][:, 0:CH], ACT.Copy).then_inc(cb_ok, 1)
                        if s == POST_AT and k:
                            act.wait_ge(y_acc, DS * k)
                            A.activation(ytok[:, :], ps[2 if (k - 1) % 2 == 0 else 7][0:TT, :], ACT.Copy)\
                                .then_inc(y_tok, 1)
                        if k + 1 < STEPS:
                            if s == 10:
                                soft_exp(k + 1)
                            if s == 11:
                                soft_y(k + 1)
                            if s == 12:
                                soft_ln(k + 1)
                            if s == 13:
                                copy_bc(k + 1)
                    act.wait_ge(y_acc, G)
                    A.activation(ytok[:, :], ps[2 if (STEPS - 1) % 2 == 0 else 7][0:TT, :], ACT.Copy)\
                        .then_inc(y_tok, 1)

                @block.vector
                def _(dve):
                    V = nc.vector

                    def soft_x(k):
                        dve.wait_ge(dt_ps, k + 1)
                        if k >= 2:
                            dve.wait_ge(gated, k - 1)
                        V.tensor_scalar(sp[:, 0, :], ps[0][:, 0:CH], dvec[k % 2][:, 1:2], DT_CLAMP, ALU.add, ALU.min)\
                            .then_inc(dt_x, 1)

                    def soft_rest(k):
                        dve.wait_ge(dt_y, k + 1)
                        V.scalar_tensor_tensor(sp[:, 1, :], sp[:, 2, :], -1.0, sp[:, 1, :], ALU.add, ALU.subtract)\
                            .then_inc(dt_r, 1)

                    def soft_max(k):
                        dve.wait_ge(dt_s, k + 1)
                        V.scalar_tensor_tensor(dtv[:, k % 2, :], ps[0][:, 0:CH], dvec[k % 2][:, 1:2], sp[:, 3, :],
                                               ALU.add, ALU.max).then_inc(dt_ok, 1)

                    def soft_sub(k):
                        dve.wait_ge(dt_l, k + 1)
                        dve.wait_ge(dt_r, k + 1)
                        V.tensor_tensor(sp[:, 3, :], sp[:, 3, :], sp[:, 1, :], ALU.subtract).then_inc(dt_s, 1)

                    def soft_u(k):
                        dve.wait_ge(dt_ok, k + 1)
                        V.tensor_tensor(dtu[:, k % 2, :], dtv[:, k % 2, :], ucols(k), ALU.mult).then_inc(dtu_ok, 1)

                    def split_bc(k, i):
                        if i == 0:
                            dve.wait_ge(bc_ps, k + 1)
                            if k:
                                dve.wait_ge(bcT_ps, k)
                        else:
                            dve.wait_ge(bc_part, 4 * k + i)
                        src = tile4(ps[1], 2 * DS)
                        if i == 0:
                            V.tensor_copy(bct[:, :, 0, :], src).then_inc(bc_part, 1)
                        elif i == 1:
                            V.tensor_tensor(bcr[:, :, :], src, bct[:, :, 0, :], ALU.subtract).then_inc(bc_part, 1)
                        elif i == 2:
                            V.tensor_copy(bct[:, :, 1, :], bcr[:, :, :]).then_inc(bc_part, 1)
                        elif i == 3:
                            V.tensor_tensor(bcr[:, :, :], bcr[:, :, :], bct[:, :, 1, :], ALU.subtract)\
                                .then_inc(bc_part, 1)
                        else:
                            V.tensor_copy(bct[:, :, 2, :], bcr[:, :, :]).then_inc(bc_tok, 1)

                    def y_plus_ud(k):
                        dve.wait_ge(yT_ps, k + 1)
                        V.scalar_tensor_tensor(sp[:, 0, :], ucols(k), dvec[k % 2][:, 2:3], ps[0][:, 0:CH],
                                               ALU.mult, ALU.add).then_inc(yz_ok, 1)

                    def bu(g):
                        k = g // DS
                        dve.wait_ge(bb_ps, g + 1)
                        if g % DS == 0:
                            dve.wait_ge(dtu_ok, k + 1)
                        if g >= 3:
                            dve.wait_ge(h_ok, g - 2)
                        V.tensor_tensor(dBu[:, g % 3, :], ps[3 + g % 2][:, 0:CH], dtu[:, k % 2, :], ALU.mult)\
                            .then_inc(bu_ok, 1)

                    def scan(g):
                        s, d = g % DS, (g // DS) % 2
                        dve.wait_ge(bu_ok, g + 1)
                        dve.wait_ge(a_ok, g + 1)
                        if g >= 3:
                            dve.wait_ge(hc_ok, g - 2)
                        if g >= 2 * DS:
                            dve.wait_ge(st_ok, g - 2 * DS + 1)
                        V.tensor_tensor_scan(rev(hs[:, g % 3, :], d), rev(dA[:, g % 3, :], d), rev(dBu[:, g % 3, :], d),
                                             state[:, d, s:s + 1], ALU.mult, ALU.add).then_inc(h_ok, 1)

                    def prepare_before(k, s):
                        if s == 7:
                            split_bc(k, 0)
                        if s == 8:
                            soft_x(k)
                        if s == 9:
                            split_bc(k, 3)
                        if s == 11:
                            soft_rest(k)
                        if s == 12:
                            soft_sub(k)
                        if s == 13:
                            soft_max(k)
                        if s == 14:
                            soft_u(k)

                    def prepare_after(k, s):
                        if s == 7:
                            split_bc(k, 1)
                        if s == 8:
                            split_bc(k, 2)
                        if s == 9:
                            split_bc(k, 4)

                    V.memset(state[:, :, :], 0.0).then_inc(st0, 1)
                    dve.wait_ge(st0, 1)
                    soft_x(0)
                    for i in range(5):
                        split_bc(0, i)
                    soft_rest(0)
                    soft_sub(0)
                    soft_max(0)
                    soft_u(0)
                    G = STEPS * DS
                    bu(0)
                    for g in range(G):
                        k, s = g // DS, g % DS
                        if g + 1 < G:
                            bu(g + 1)
                        if s == POST_AT + 3 and k:
                            y_plus_ud(k - 1)
                        if k + 1 < STEPS:
                            prepare_before(k + 1, s)
                        scan(g)
                        if k + 1 < STEPS:
                            prepare_after(k + 1, s)
                    y_plus_ud(STEPS - 1)

                @block.gpsimd
                def _(pool):
                    P = nc.gpsimd
                    G = STEPS * DS

                    def gate(k):
                        c = chunk_of(k)
                        z = zs[k % 2][:, c * CH:(c + 1) * CH]
                        pool.wait_ge(yz_ok, k + 1)
                        P.tensor_tensor(z, z, sp[:, 0, :], ALU.mult).then_inc(gated, 1)

                    for g in range(G):
                        k, s, d = g // DS, g % DS, (g // DS) % 2
                        pool.wait_ge(h_ok, g + 1)
                        at = 0 if d else CH - 1
                        P.tensor_copy(state[:, d, s:s + 1], hs[:, g % 3, at:at + 1]).then_inc(st_ok, 1)
                        pool.wait_ge(cb_ok, g + 1)
                        if g >= 3:
                            pool.wait_ge(y_acc, g - 2)
                        P.tensor_tensor(hc[:, g % 3, :], hs[:, g % 3, :], cb[:, g % 3, :], ALU.mult).then_inc(hc_ok, 1)
                        if s == POST_AT + 3 and k:
                            gate(k - 1)
                    gate(STEPS - 1)

            with nc.Block() as block:
                @block.tensor
                def _(pe):
                    def outp(c):
                        if c >= 4:
                            pe.wait_ge(o_rd, c - 3)
                        for j in range(KT):
                            t0 = c * CH + j * TT
                            for d in range(2):
                                last = nc.tensor.matmul(ps[3 + c % 4][0:TT, j * C:(j + 1) * C], zs[d][:, t0:t0 + TT],
                                                        wo[d][:, :], start=(d == 0), stop=(d == 1))
                        last.then_inc(o_ps, 1)

                    def tokens_T(c):
                        pe.wait_ge(d_tok, c + 1)
                        if c:
                            pe.wait_ge(dT_sb, c)
                            pe.wait_ge(dp_r, 2 * c - 1)
                        for j in range(KT):
                            last = nc.tensor.transpose(ps[2][:, j * TT:(j + 1) * TT],
                                                       xnt[:, c % 2, j].rearrange("p a b -> p (a b)"),
                                                       ident[0:TT, 0:TT])
                        last.then_inc(dT_ps, 1)

                    def logits(c):
                        pe.wait_ge(dT_sb, c + 1)
                        for j in range(KT):
                            last = nc.tensor.matmul(ps[7][0:TT, (c * KT + j) * EX:(c * KT + j + 1) * EX],
                                                    xn32[:, c % 2, j * TT:(j + 1) * TT], wr[:, :],
                                                    start=True, stop=True)
                        last.then_inc(lg_ps, 1)

                    for c in range(3):
                        outp(c)
                    for c in range(NCH):
                        tokens_T(c)
                        if c + 3 < NCH:
                            outp(c + 3)
                        logits(c)

                @block.scalar
                def _(act):
                    for c in range(NCH):
                        act.wait_ge(dT_ps, c + 1)
                        A = nc.scalar
                        cols = slice(c * CH, (c + 1) * CH)
                        A.activation(tok_parts[:, 0, cols], ps[2][:, 0:CH], ACT.Copy).then_inc(dp_a, 1)
                        A.activation(tok_parts[0:C, 1, cols], ps[2][0:C, 0:CH], ACT.Copy)
                        if c >= 2:
                            act.wait_ge(lg_ps, c - 1)
                        A.activation(xn32[:, c % 2, :], ps[2][0:C, 0:CH], ACT.Copy).then_inc(dT_sb, 1)
                        act.wait_ge(dp_r, 2 * c + 1)
                        A.activation(tok_parts[C:128, 0, cols], hc[C:128, 0, :], ACT.Copy).then_inc(dp_a, 1)
                        act.wait_ge(dp_r, 2 * c + 2)
                        A.activation(tok_parts[C:128, 1, cols], hc[C:128, 1, :], ACT.Copy).then_inc(dp_a, 1)

                @block.gpsimd
                def _(pool):
                    for c in range(NCH):
                        i = c % 2
                        pool.wait_ge(pw_req, 2 * NCH + 2 * c + 1)
                        nc.gpsimd.tensor_tensor(stat[:, i, 2, :], stat[:, i, 1, :], half_pow[0:TT, 0:KT], ALU.pow)\
                            .then_inc(pw_done, 1)
                        pool.wait_ge(pw_req, 2 * NCH + 2 * c + 2)
                        nc.gpsimd.tensor_tensor(stat[:, i, 4, :], stat[:, i, 3, :], half_pow[0:TT, 0:KT], ALU.pow)\
                            .then_inc(pw_done, 1)

                @block.vector
                def _(dve):
                    V = nc.vector
                    link = linker(dve, d_ch)

                    def residual(c):
                        r = res[:, c * KT:(c + 1) * KT, :]
                        dve.wait_ge(o_ps, c + 1)
                        V.tensor_tensor(r, tile4(ps[3 + c % 4], C), r, ALU.add).then_inc(o_rd, 1)
                        dve.wait_ge(o_rd, c + 1)
                        norm_mean(link, r, c % 2)

                    def normalised(c):
                        link(V.tensor_tensor(tmp[:, 1], tmp[:, 0], bc_last(stat[:, c % 2, 2, :], C), ALU.mult))

                    def tokens(c):
                        st = stat[:, c % 2]
                        dve.wait_ge(pw_done, 2 * NCH + 2 * c + 2)
                        if c >= 2:
                            dve.wait_ge(dT_ps, c - 1)
                        V.tensor_tensor(xnt[:, c % 2, :, 0, :], tmp[:, 1], bc_last(st[:, 4, :], C), ALU.mult)
                        V.tensor_tensor(xnt[:, c % 2, :, 1, :], tmp[:, 1], bc_last(st[:, 4, :], C), ALU.mult)\
                            .then_inc(d_tok, 1)
                        link(V.tensor_tensor(sq2[:, c * KT:(c + 1) * KT], st[:, 3, :], st[:, 4, :], ALU.mult))

                    def remainder_hi(c):
                        cols = slice(c * CH, (c + 1) * CH)
                        if c:
                            dve.wait_ge(dp_a, 3 * c)
                        dve.wait_ge(dp_a, 3 * c + 1)
                        V.tensor_tensor(hc[C:128, 0, :], ps[2][C:128, 0:CH], tok_parts[C:128, 0, cols], ALU.subtract)\
                            .then_inc(dp_r, 1)

                    def remainder_mid(c):
                        cols = slice(c * CH, (c + 1) * CH)
                        dve.wait_ge(dp_r, 2 * c + 1)
                        dve.wait_ge(dp_a, 3 * c + 2)
                        V.tensor_tensor(hc[C:128, 1, :], hc[C:128, 0, :], tok_parts[C:128, 0, cols], ALU.subtract)\
                            .then_inc(dp_r, 1)

                    for c in range(NCH + 2):
                        if c < NCH:
                            residual(c)
                        if 0 < c <= NCH:
                            norm_again(dve, link, (c - 1) % 2, 2 * NCH + 2 * (c - 1))
                            normalised(c - 1)
                        if c >= 2:
                            remainder_hi(c - 2)
                        if c < NCH:
                            norm_var(link, res[:, c * KT:(c + 1) * KT, :], tmp[:, 0], c % 2)
                        if c >= 2:
                            remainder_mid(c - 2)
                        if 0 < c <= NCH:
                            tokens(c - 1)

            ORDER = [4 * p + 2 * (i % 2) + i // 2 for p in range(EX // 2) for i in range(4)]
            PAIRS = EX // 2
            UP = (0, 1, 2, 5)
            first_layer = [(what, c) for c in range(PRE) for what in ("x_T", "paths_in")]
            BANK6 = [(6, "parts", 0), (6, "pair", 0), (8, "pair", 1), (10, "pair", 2), (12, "parts", 1), (12, "pair", 3)]
            for g in range(MT - 2, NCH * MT, 2):
                c, m = g // MT, g % MT
                if m in (0, 4, 8) and first_layer:
                    BANK6.append((g,) + first_layer.pop(0))
                if m == MT - 4 and c + 1 < NCH:
                    BANK6.append((g, "parts", c + 1))
                if m % 4 == 2 and g + 2 < NCH * MT:
                    BANK6.append((g, "pair", (g + 2) // 4))

            def read_out(what, of):
                return [b[1:] for b in BANK6].index((what, of)) + 1

            with nc.Block() as block:
                G = NCH * MT

                @block.tensor
                def _(pe):
                    def up(g):
                        c, m = g // MT, ORDER[g % MT]
                        if g >= 4:
                            pe.wait_ge(g_ok, g - 3)
                        for i in range(3):
                            last = nc.tensor.matmul(ps[UP[g % 4]][:, 0:CH], we1s[i][:, m, :],
                                                    tok_parts[:, i // 2, c * CH:(c + 1) * CH],
                                                    start=(i == 0), stop=(i == 2))
                        last.then_inc(up_ps, 1)

                    def down(g):
                        P = g // 4
                        pe.wait_ge(g_ok, g + 2)
                        if g % 4 == 0 and P >= 2:
                            pe.wait_ge(ye_dve, P - 1)
                        for i in range(2):
                            m = ORDER[(g + i) % MT]
                            last = nc.tensor.matmul(ps[3 + P % 2][C * i:C * i + C, 0:CH], we2[:, m, :],
                                                    hg[:, (g + i) % 4, :], start=(g % 4 == 0), stop=(g % 4 == 2))
                        last.then_inc(dn, 1)

                    def through_bank6(q):
                        what, of = BANK6[q][1:]
                        if q:
                            pe.wait_ge(wb_sb, q)
                        if what == "parts":
                            if of == 0:
                                pe.wait_ge(routed, 1)
                            out = ps[6][0:3 * EX, 0:CH // 2].bitcast(BF16)
                            for j in range(KT):
                                last = nc.tensor.transpose(out[:, j * TT:(j + 1) * TT],
                                                           wgt3[:, of * KT + j].rearrange("p a b -> p (a b)"),
                                                           identb[0:TT, 0:TT])
                        elif what == "pair":
                            i = of % PAIRS
                            last = nc.tensor.matmul(ps[6][:, 0:CH],
                                                    pick_w[:, 2 * i:2 * i + 2, :].rearrange("p a b -> p (a b)"),
                                                    wT[:, of // PAIRS % 2, :], start=True, stop=True)
                        elif what == "x_T":
                            pe.wait_ge(x_in, 16)
                            last = x_T(of, ps[6])
                        else:
                            last = paths_in(of, ps[6])
                        last.then_inc(wb_ps, 1)

                    def fold(c):
                        pe.wait_ge(ye_sum, (PAIRS - 1) * (c + 1))
                        if c:
                            pe.wait_ge(o_sum, c)
                        for j in range(KT):
                            last = nc.tensor.transpose(ps[7][0:TT, j * 128:(j + 1) * 128],
                                                       yw[:, c % 2, j * TT:(j + 1) * TT], ident[:, :])
                        last.then_inc(ye_T, 1)

                    for g in range(4):
                        up(g)
                    for g in range(0, G, 2):
                        c, m = g // MT, g % MT
                        down(g)
                        if g + 4 < G:
                            up(g + 4)
                        if m == 2 and c:
                            fold(c - 1)
                        if g + 5 < G:
                            up(g + 5)
                        for q in range(len(BANK6)):
                            if BANK6[q][0] == g:
                                through_bank6(q)
                    fold(NCH - 1)

                @block.scalar
                def _(act):
                    A = nc.scalar

                    def read_bank6(q):
                        what, of = BANK6[q][1:]
                        act.wait_ge(wb_ps, q + 1)
                        if what == "parts":
                            out = A.activation(wT[:, of % 2, :], ps[6][0:3 * EX, 0:CH // 2].bitcast(BF16), ACT.Copy)
                        elif what == "pair":
                            if of >= 3:
                                act.wait_ge(ye_dve, of - 2)
                            out = A.activation(wb[:, of % 3, :], ps[6][:, 0:CH], ACT.Copy)
                        elif what == "x_T":
                            out = keep_xT(of, ps[6])
                        else:
                            out = keep_h1(of, ps[6])
                        out.then_inc(wb_sb, 1)

                    for g in range(G):
                        m = ORDER[g % MT]
                        act.wait_ge(up_ps, g + 1)
                        if g >= 4:
                            act.wait_ge(dn, (g - 4) // 2 + 1)
                        A.activation(hg[:, g % 4, :], ps[UP[g % 4]][:, 0:CH], ACT.Gelu, bias=be1[:, m:m + 1])\
                            .then_inc(g_ok, 1)
                        if g == 3:
                            act.wait_ge(e_req, 1)
                            A.activation(l1[:, 4, :], l1[:, 3, :], ACT.Exp).then_inc(e_ok, 1)
                        for q in range(len(BANK6)):
                            made, what = BANK6[q][0:2]
                            if g == made + (4 if what == "pair" else 3):
                                read_bank6(q)

                @block.vector
                def _(dve):
                    V = nc.vector
                    link = linker(dve, r_ch)

                    def finish(c):
                        dve.wait_ge(ye_T, c + 1)
                        if c >= 2:
                            dve.wait_ge(stored[c % 2], 16 * (c // 2))
                        ob, b7 = outb[:, c % 2], tile4(ps[7], 128)
                        V.tensor_tensor(tmp[:, 0], b7[:, :, 0:C], res[:, c * KT:(c + 1) * KT, :], ALU.add)\
                            .then_inc(w_ok, 1)
                        dve.wait_ge(w_ok, c + 1)
                        V.tensor_tensor(ob, b7[:, :, C:128], tmp[:, 0], ALU.add).then_inc(o_sum, 1)

                    L, eq, cand, s1, s2, t8 = (lg[:, i] for i in range(6))
                    rk = rank8[:, :].unsqueeze(1).to_broadcast([TT, NT, EX])
                    link(V.tensor_tensor(L, ps[7][0:TT, 0:NT * EX].rearrange("p (n e) -> p n e", e=EX),
                                         bc_last(sq2[:, :], EX), ALU.mult))
                    link(V.tensor_tensor(L, L, br[:, :].unsqueeze(1).to_broadcast([TT, NT, EX]), ALU.add))

                    def top(src, sel, m):
                        link(V.reduce_max(m, src, axis=AX.X))
                        link(V.tensor_tensor(eq, src, bc_last(m, EX), ALU.is_equal))
                        link(V.tensor_tensor(cand, eq, rk, ALU.mult))
                        link(V.reduce_max(l1[:, 7, :], cand, axis=AX.X))
                        link(V.tensor_tensor(sel, rk, bc_last(l1[:, 7, :], EX), ALU.is_equal))

                    top(L, s1, l1[:, 0, :])
                    link(V.scalar_tensor_tensor(t8, s1, -FAR, L, ALU.mult, ALU.add))
                    top(t8, s2, l1[:, 1, :])
                    V.tensor_tensor(l1[:, 3, :], l1[:, 1, :], l1[:, 0, :], ALU.subtract).then_inc(e_req, 1)
                    dve.wait_ge(e_ok, 1)
                    link(V.tensor_scalar(l1[:, 5, :], l1[:, 4, :], 1.0, None, ALU.add))
                    link(V.reciprocal(l1[:, 5, :], l1[:, 5, :]))
                    link(V.tensor_tensor(l1[:, 6, :], l1[:, 4, :], l1[:, 5, :], ALU.mult))
                    link(V.tensor_tensor(s1, s1, bc_last(l1[:, 5, :], EX), ALU.mult))
                    link(V.tensor_tensor(s2, s2, bc_last(l1[:, 6, :], EX), ALU.mult))
                    link(V.tensor_tensor(wgt[:, :, :], s1, s2, ALU.add))
                    link(V.tensor_copy(wgt3[:, :, 0, :], wgt[:, :, :]))
                    link(V.tensor_tensor(wgt[:, :, :], wgt[:, :, :], wgt3[:, :, 0, :], ALU.subtract))
                    link(V.tensor_copy(wgt3[:, :, 1, :], wgt[:, :, :]))
                    link(V.tensor_tensor(wgt[:, :, :], wgt[:, :, :], wgt3[:, :, 1, :], ALU.subtract))
                    V.tensor_copy(wgt3[:, :, 2, :], wgt[:, :, :]).then_inc(routed, 1)

                    for P in range(NCH * PAIRS):
                        c, p = P // PAIRS, P % PAIRS
                        dve.wait_ge(dn, 2 * P + 2)
                        dve.wait_ge(wb_sb, read_out("pair", P))
                        total, y = yw[:, c % 2, :], yw[:, 2, :]
                        if p == 0 and c >= 2:
                            dve.wait_ge(ye_T, c - 1)
                        if p and P > 1:
                            dve.wait_ge(ye_sum, (PAIRS - 1) * c + p - 1)
                        V.scalar_tensor_tensor(y if p else total, ps[3 + P % 2][:, 0:CH], be2[:, p:p + 1],
                                               wb[:, P % 3, :], ALU.add, ALU.mult).then_inc(ye_dve, 1)
                        if p:
                            dve.wait_ge(ye_dve, P + 1)
                            V.tensor_tensor(total, total, y, ALU.add).then_inc(ye_sum, 1)
                        if p == 0 and c:
                            finish(c - 1)
                    finish(NCH - 1)

                @block.gpsimd
                def _(pool):
                    for s in done_sems:
                        nc.gpsimd.sem_clear(s)

                @block.sync
                def _(sp_):
                    sp_.dma_start(x_tok[:, :, :], x_dram[img + 1]).then_inc(x_in, 16)
                    for c in range(NCH):
                        if c >= NCH - PRE:
                            cc = c - NCH + PRE
                            sp_.wait_ge(wb_sb, read_out("paths_in", cc))
                            keep_rows(sp_, cc, h1_pre)
                            sp_.wait_ge(h1_pre, 16 * (cc + 1))
                            if 1 <= cc <= 2:
                                cut_slab(sp_, cc - 1, slab_pre)
                        sp_.wait_ge(o_sum, c + 1)
                        if c >= 2:
                            sp_.wait_ge(stored[c % 2], 16 * (c // 2))
                        sp_.dma_start(o_dram[img][:, c * KT:(c + 1) * KT, :], outb[:, c % 2])\
                            .then_inc(stored[c % 2], 16)
                    for i in range(2):
                        sp_.wait_ge(stored[i], 16 * ((NCH + 1 - i) // 2))
                        sp_.wait_ge(slab_pre[i], 16 * 3)

            for s in last_sems:
                nc.gpsimd.sem_clear(s)
            nc.all_engine_barrier()


def _layouts(np, I):
    a = {k: np.asarray(v) for k, v in I.items()}
    L = {"x": np.concatenate([a["x"], np.zeros((1,) + a["x"].shape[1:], a["x"].dtype)])}
    cv = lambda n: a["L0_conv_" + n]
    L["ident"] = np.eye(128, dtype=np.float32)
    own = np.repeat(np.eye(8, dtype=np.float32), PD, axis=0)
    L["quad_mask"] = np.tile(own, (3, 1))
    L["four_mask"] = np.tile(own[0:16, 0:4], (6, 1))
    L["rank8"] = np.tile(np.arange(EX, 0, -1, dtype=np.float32), (TT, 1))
    L["pick"] = np.concatenate([np.tile(np.eye(2 * DS, dtype=np.float32), (3, 1)),
                                np.zeros((32, 2 * DS), np.float32)])
    L["w1"] = cv("W1").transpose(1, 0, 2).reshape(C, 128)
    L["w2"] = cv("W2").reshape(QUADS, 8, 3, 3, PD, PD).transpose(3, 1, 4, 2, 0, 5).reshape(96, 3 * QUADS, PD)
    L["w3"] = cv("W3").reshape(128, C)

    def wide(n):
        third = cv(n + "3").reshape(ZP, 2, C).transpose(1, 2, 0).reshape(128, ZP)
        return np.concatenate([cv(n + "1").reshape(128, 1), cv(n + "2").reshape(128, 1), third], axis=1)

    rows = lambda n: np.repeat(cv(n + "3"), PD, axis=0)
    L["bnv"] = np.concatenate([wide("V"), rows("V")], axis=1)
    L["bng"] = np.concatenate([wide("G"), rows("G")], axis=1)
    L["bnm"], L["bnb"], L["bnbe"] = wide("M"), wide("B"), wide("Be")
    L["gb"] = np.stack([a["L1_attn_ln_gamma"], a["L1_attn_ln_beta"]], axis=1)
    for d, p in enumerate("fb"):
        m = lambda n: a[f"L1_attn_{p}_{n}"]
        inp = m("in_proj_w").transpose(1, 0)
        L[f"wx{d}"] = np.tile(inp[:, 0:DI].reshape(1, C, 1, DI), (2, 1, 2, 1)).reshape(128, 2, DI)
        taps = m("conv_w").reshape(DI, TAPS).transpose(1, 0)
        if d:
            taps = taps[::-1]
        taps = taps.reshape(2, 2, DI).transpose(1, 0, 2)
        L[f"tapw{d}"] = np.repeat(taps, C, axis=0)
        L[f"wz{d}"] = inp[:, DI:2 * DI]
        L[f"wdt_a{d}"] = m("x_proj_w")[0:DR]
        L[f"wdt_b{d}"] = m("dt_proj_w").transpose(1, 0)
        L[f"wbc{d}"] = m("x_proj_w")[DR:DR + 2 * DS].transpose(1, 0)
        L[f"wo{d}"] = m("out_proj_w").transpose(1, 0)
        L[f"dvec{d}"] = np.concatenate([m("conv_b").reshape(DI, 1), m("dt_proj_b").reshape(DI, 1),
                                        m("D").reshape(DI, 1), m("A_log")], axis=1)
    f = lambda n: a["L1_ffn_" + n]
    L["we1"] = np.tile(f("W1").transpose(1, 0, 2).reshape(C, MT, 128), (2, 1, 1))
    L["pick_w"] = np.tile(np.eye(EX, dtype=np.float32), (3, 1))
    L["we2"] = f("W2").reshape(MT, 128, C).transpose(1, 0, 2)
    L["be1"] = f("b1").reshape(MT, 128).transpose(1, 0)
    L["be2"] = f("b2").reshape(EX // 2, 128).transpose(1, 0)
    L["lng"], L["lnb"] = (np.tile(f(n).transpose(1, 0), (2, 1)) for n in ("ln_g", "ln_b"))
    L["wr"] = f("Wr")
    L["br"] = np.tile(f("br").reshape(1, EX), (TT, 1))
    return {k: np.ascontiguousarray(v) for k, v in L.items()}


def kernel(**inputs):
    import numpy as _np
    import concourse.bacc as _bacc
    from concourse import mybir as _mybir
    from concourse.bass_utils import run_bass_kernel_spmd as _run

    nc = _bacc.Bacc("TRN2", target_bir_lowering=False, num_devices=1)
    arrays, T = {}, {}
    for name, a in _layouts(_np, inputs).items():
        arrays[f"in_{name}_dram"] = a
        T[name] = nc.dram_tensor(f"in_{name}_dram", a.shape, _mybir.dt.from_np(a.dtype), kind="ExternalInput").ap()
    T["out"] = nc.dram_tensor("out_0_dram", (NB, HH, WW, C), _mybir.dt.float32, kind="ExternalOutput").ap()
    T["h2_scratch"] = nc.dram_tensor("h2_scratch", (2, 3, 16, ZT, CH), BF16, kind="Internal").ap()
    T["h1_scratch"] = nc.dram_tensor("h1_scratch", (128, H1_SIZE), F32, kind="Internal").ap()
    T["w3_scratch"] = nc.dram_tensor("w3_scratch", (128, 3, C), BF16, kind="Internal").ap()
    build(nc, T)
    r = _run(nc, [arrays], core_ids=[0])
    return r.results[0]["out_0_dram"]
```
